# Optimizing a Trainium2 kernel written in Bass

```python
import numpy as np
import jax
import jax.numpy as jnp

def _softmax(x, axis=-1):
    return jax.nn.softmax(x, axis=axis)

def _gelu(x):
    return jax.nn.gelu(x, approximate=True)

def _silu(x):
    return jax.nn.silu(x)

def _sigmoid(x):
    return jax.nn.sigmoid(x)

def _layernorm(x, axis=-1, eps=1e-05):
    m = jnp.mean(x, axis=axis, keepdims=True)
    v = jnp.var(x, axis=axis, keepdims=True)
    return (x - m) / jnp.sqrt(v + eps)

def _scatter_add(tgt, idx, src, axis=0):
    return tgt.at[idx].add(src)

def _segment_sum(src, seg, n):
    return jax.ops.segment_sum(src, seg, n)
kernel_name = 'mk_adj_preln_d4_adj_r2_1f9b5d'

def setup_inputs(seed: int=0):
    np.random.seed(seed)
    _w = jnp.asarray

    def _rec_inputs():
        import jax
        import jax.numpy as jnp
        _gk = jax.random.key(seed)
        x = 7.22e-05 + 1 * jax.random.normal(jax.random.fold_in(_gk, 1), (16, 512, 256), jnp.float32)
        _w = (1.0 + jnp.arange(512, dtype=jnp.float32)) ** (-0.5)
        _w = _w / _w.mean()
        _pij = jnp.clip(0.0078125 * _w[:, None] * _w[None, :], 0.0, 1.0)
        _a = jax.random.uniform(jax.random.fold_in(_gk, 2), (16, 512, 512)) < _pij
        _a = jnp.logical_or(_a, jnp.swapaxes(_a, -1, -2))
        _a = jnp.logical_or(_a, jnp.eye(512, dtype=bool))
        _af = _a.astype(jnp.float32)
        _af = _af * jax.random.uniform(jax.random.fold_in(_gk, 3), (16, 512, 512), jnp.float32, 0.05, 1)
        adj = _af
        _nm = jnp.ones((16, 512), dtype=bool)
        nodemask = _nm
        return (x, adj, nodemask)
    x, adj, nodemask = _rec_inputs()

    def _L0_gnn_setup():
        import jax, jax.numpy as jnp
        import numpy as np
        EPS_LN = 1e-05

        def hypergraph_conv(x, adj, W, b):
            N, C, _ = adj.shape
            H = (adj != 0).astype(x.dtype)
            w = adj.reshape(N, -1)[:, :C]
            xw = jnp.einsum('ncd,hd->nch', x, W)
            Dn = jnp.einsum('nce,ne->nc', H, w)
            Dn = jnp.where(Dn > 0, 1.0 / Dn, 0.0)
            Be = H.sum(axis=1)
            Be = jnp.where(Be > 0, 1.0 / Be, 0.0)
            m = Be[:, :, None] * jnp.einsum('nce,nch->neh', H, xw)
            out = Dn[:, :, None] * jnp.einsum('nce,neh->nch', H, m)
            return out + b

        def layer_norm(x, g, b):
            mu = jnp.mean(x, axis=-1, keepdims=True)
            var = jnp.var(x, axis=-1, keepdims=True)
            return (x - mu) * jax.lax.rsqrt(var + EPS_LN) * g + b
        key = jax.random.key(seed)
        ks = jax.random.split(key, 4)
        N, C, Din, Dh, Dout = (16, 512, 256, 512, 256)
        x = jax.random.normal(ks[0], (N, C, Din), dtype=jnp.float32)
        adj = jax.random.uniform(ks[1], (N, C, C), dtype=jnp.float32, minval=0.1, maxval=1.0)
        W1 = jax.random.normal(ks[2], (Dh, Din), dtype=jnp.float32) * (1.0 / np.sqrt(Din))
        b1 = jnp.zeros((Dh,), dtype=jnp.float32)
        gamma = jnp.ones((Dh,), dtype=jnp.float32)
        beta = jnp.zeros((Dh,), dtype=jnp.float32)
        W2 = jax.random.normal(ks[3], (Dout, Dh), dtype=jnp.float32) * (1.0 / np.sqrt(Dh))
        b2 = jnp.zeros((Dout,), dtype=jnp.float32)
        return {'x': x, 'adj': adj, 'W1': W1, 'b1': b1, 'gamma': gamma, 'beta': beta, 'W2': W2, 'b2': b2}
    _L0_gnn_all = _L0_gnn_setup()
    _L0_gnn_in = {k: v for k, v in _L0_gnn_all.items() if k in ('W1', 'b1', 'gamma', 'beta', 'W2', 'b2')}
    del _L0_gnn_all

    def _L1_gnn_setup():
        import jax, jax.numpy as jnp
        import numpy as np
        HEADS = 8
        DIM_HEAD = 64
        LA = 0.33
        LD = 0.33
        LG = 0.33
        key = jax.random.key(seed)
        ks = jax.random.split(key, 6)
        B, N, D = (4, 512, 256)
        inner = HEADS * DIM_HEAD
        x = jax.random.normal(ks[0], (B, N, D), jnp.float32)
        mask = jax.random.uniform(ks[1], (B, N)) < 0.9
        adjacency_mat = (jax.random.uniform(ks[2], (B, N, N)) < 0.05).astype(jnp.float32)
        distance_mat = jax.random.uniform(ks[3], (B, N, N), jnp.float32) * 5.0
        W_qkv = jax.random.normal(ks[4], (D, inner * 3), jnp.float32) * 0.02
        W_out = jax.random.normal(ks[5], (inner, D), jnp.float32) * 0.02
        b_out = jnp.zeros((D,), jnp.float32)
        return {'x': x, 'mask': mask, 'adjacency_mat': adjacency_mat, 'distance_mat': distance_mat, 'W_qkv': W_qkv, 'W_out': W_out, 'b_out': b_out}
    _L1_gnn_all = _L1_gnn_setup()
    _L1_gnn_in = {k: v for k, v in _L1_gnn_all.items() if k in ('W_qkv', 'W_out', 'b_out')}
    del _L1_gnn_all

    def _L2_gnn_setup():
        import jax, jax.numpy as jnp
        import numpy as np
        B, N, D_IN, D_OUT = (4, 2048, 256, 256)
        key = jax.random.key(seed)
        k1, k2, k3, k4 = jax.random.split(key, 4)
        x = jax.random.normal(k1, (B, N, D_IN), dtype=jnp.float32)
        A_shape = jax.random.uniform(k2, (B, N, N), dtype=jnp.float32)
        w = jax.random.normal(k3, (D_IN, D_OUT), dtype=jnp.float32)
        a = jax.random.normal(k4, (D_OUT,), dtype=jnp.float32)
        return {'x': x, 'A_shape': A_shape, 'w': w, 'a': a}
    _L2_gnn_all = _L2_gnn_setup()
    _L2_gnn_in = {k: v for k, v in _L2_gnn_all.items() if k in ('w', 'a')}
    del _L2_gnn_all

    def _L3_gnn_setup():
        import jax, jax.numpy as jnp
        import numpy as np
        EPS = 1e-06
        key = jax.random.key(seed)
        k1, k2, k3 = jax.random.split(key, 3)
        B, N, F, O = (8, 2048, 256, 256)
        x = jax.random.normal(k1, (B, N, F), dtype=jnp.float32)
        adj = jax.random.uniform(k2, (B, N, N), dtype=jnp.float32)
        W = jax.random.normal(k3, (O, 2 * F), dtype=jnp.float32) * (1.0 / np.sqrt(2 * F))
        return {'x': x, 'adj': adj, 'W': W}
    _L3_gnn_all = _L3_gnn_setup()
    _L3_gnn_in = {k: v for k, v in _L3_gnn_all.items() if k in ('W',)}
    del _L3_gnn_all
    return {'x': x, 'adj': adj, 'nodemask': nodemask, 'L0_gnn_W1': _L0_gnn_in['W1'], 'L0_gnn_b1': _L0_gnn_in['b1'], 'L0_gnn_gamma': _L0_gnn_in['gamma'], 'L0_gnn_beta': _L0_gnn_in['beta'], 'L0_gnn_W2': _L0_gnn_in['W2'], 'L0_gnn_b2': _L0_gnn_in['b2'], 'L1_gnn_W_qkv': _L1_gnn_in['W_qkv'], 'L1_gnn_W_out': _L1_gnn_in['W_out'], 'L1_gnn_b_out': _L1_gnn_in['b_out'], 'L2_gnn_w': _L2_gnn_in['w'], 'L2_gnn_a': _L2_gnn_in['a'], 'L3_gnn_W': _L3_gnn_in['W']}

def reference(x, adj, nodemask, L0_gnn_W1, L0_gnn_b1, L0_gnn_gamma, L0_gnn_beta, L0_gnn_W2, L0_gnn_b2, L1_gnn_W_qkv, L1_gnn_W_out, L1_gnn_b_out, L2_gnn_w, L2_gnn_a, L3_gnn_W):
    import jax
    import jax.numpy as jnp

    def _L0_gnn_ref(x, adj, W1, b1, gamma, beta, W2, b2):
        import jax, jax.numpy as jnp
        import numpy as np
        EPS_LN = 1e-05

        def hypergraph_conv(x, adj, W, b):
            N, C, _ = adj.shape
            H = (adj != 0).astype(x.dtype)
            w = adj.reshape(N, -1)[:, :C]
            xw = jnp.einsum('ncd,hd->nch', x, W)
            Dn = jnp.einsum('nce,ne->nc', H, w)
            Dn = jnp.where(Dn > 0, 1.0 / Dn, 0.0)
            Be = H.sum(axis=1)
            Be = jnp.where(Be > 0, 1.0 / Be, 0.0)
            m = Be[:, :, None] * jnp.einsum('nce,nch->neh', H, xw)
            out = Dn[:, :, None] * jnp.einsum('nce,neh->nch', H, m)
            return out + b

        def layer_norm(x, g, b):
            mu = jnp.mean(x, axis=-1, keepdims=True)
            var = jnp.var(x, axis=-1, keepdims=True)
            return (x - mu) * jax.lax.rsqrt(var + EPS_LN) * g + b
        h = jax.nn.relu(hypergraph_conv(x, adj, W1, b1))
        h = layer_norm(h, gamma, beta)
        y = hypergraph_conv(h, adj, W2, b2)
        return y + x

    def _L1_gnn_ref(x, mask, adjacency_mat, distance_mat, W_qkv, W_out, b_out):
        import jax, jax.numpy as jnp
        import numpy as np
        HEADS = 8
        DIM_HEAD = 64
        LA = 0.33
        LD = 0.33
        LG = 0.33
        B, N, _ = x.shape
        scale = DIM_HEAD ** (-0.5)
        qkv = (x @ W_qkv).reshape(B, N, HEADS, 3, DIM_HEAD)
        q, k, v = (jnp.transpose(qkv[..., i, :], (0, 2, 1, 3)) for i in range(3))
        dots = jnp.einsum('bhid,bhjd->bhij', q, k) * scale
        big = jnp.finfo(dots.dtype).max
        m2 = mask[:, None, :, None] & mask[:, None, None, :]
        dots = jnp.where(m2, dots, -big)
        attn = jax.nn.softmax(dots, axis=-1) * LA
        adj = jnp.where(m2, adjacency_mat[:, None], 0.0)
        dist = jnp.where(m2, distance_mat[:, None], big)
        attn = attn + LG * adj + LD * jnp.exp(-dist)
        out = jnp.einsum('bhij,bhjd->bhid', attn, v)
        out = jnp.transpose(out, (0, 2, 1, 3)).reshape(B, N, HEADS * DIM_HEAD)
        return out @ W_out + b_out

    def _L2_gnn_ref(x, A_shape, w, a):
        import jax, jax.numpy as jnp
        import numpy as np
        B, N, D_IN, D_OUT = (4, 2048, 256, 256)
        y = x @ w
        s = y @ a
        A = s[..., :, None] + s[..., None, :]
        A = jnp.tanh(A / 8.0) * 8.0
        A = jnp.where(A >= 0, A, 0.1 * A)
        A = jnp.exp(A) * A_shape
        A = A / jnp.sum(A, axis=-1, keepdims=True)
        A = A * jnp.sum(A_shape, axis=-1, keepdims=True)
        out = A @ x @ w
        return out

    def _L3_gnn_ref(x, adj, W):
        import jax, jax.numpy as jnp
        import numpy as np
        EPS = 1e-06
        deg = jnp.sum(adj, axis=-1, keepdims=True)
        agg = jnp.einsum('bij,bjf->bif', adj, x) / jnp.maximum(deg, EPS)
        cat = jnp.concatenate([x, agg], axis=2)
        out = jnp.einsum('bnf,of->bno', cat, W)
        return jax.nn.relu(out)
    h = jnp.maximum(_layernorm(x, axis=-1), 0.0)
    x = x + _L0_gnn_ref(h, adj, L0_gnn_W1, L0_gnn_b1, L0_gnn_gamma, L0_gnn_beta, L0_gnn_W2, L0_gnn_b2)
    h = jnp.maximum(_layernorm(x, axis=-1), 0.0)
    x = x + _L1_gnn_ref(h, nodemask, adj, adj, L1_gnn_W_qkv, L1_gnn_W_out, L1_gnn_b_out)
    h = jnp.maximum(_layernorm(x, axis=-1), 0.0)
    x = x + _L2_gnn_ref(h, adj, L2_gnn_w, L2_gnn_a)
    h = jnp.maximum(_layernorm(x, axis=-1), 0.0)
    x = x + _L3_gnn_ref(h, adj, L3_gnn_W)
    return x

_drawn_inputs = setup_inputs


def setup_inputs(seed=0):
    import zlib

    import numpy as np

    out = dict(_drawn_inputs(seed))
    spreads = {'L0_gnn_b1': (0.0, 0.1),
     'L0_gnn_gamma': (1.0, 0.2),
     'L0_gnn_beta': (0.0, 0.1),
     'L0_gnn_b2': (0.0, 0.49),
     'L1_gnn_b_out': (0.0, 0.8)}
    factors = {'L3_gnn_W': 8.0}
    for name, (base, spread) in spreads.items():
        noise = np.random.default_rng([zlib.crc32(name.encode()), seed]).standard_normal(out[name].shape)
        drawn = base * np.exp(spread * noise) if base else spread * noise
        out[name] = jnp.asarray(drawn.astype(out[name].dtype))
    for name, factor in factors.items():
        out[name] = (out[name] * factor).astype(out[name].dtype)
    return out
```

```python
from contextlib import ExitStack

import concourse.bass as bass
from concourse import mybir

F32 = mybir.dt.float32
F16 = mybir.dt.float16
U8 = mybir.dt.uint8
ALU = mybir.AluOpType
ACT = mybir.ActivationFunctionType
AX_X = mybir.AxisListType.X

P = 128
BATCHES = 16
NODES = 512
NT = NODES // P
D = 256
FD = D // P
DH = 512
HD = DH // P
HEADS = 8
DIM_HEAD = 64
PAIRS = HEADS // 2
EPS_LN = 1e-5
EPS_DEG = 1e-6
MIX = 0.33
TANH_RANGE = 8.0
LEAK = 0.1
MASKED = 1e30
TINY = 1.2e-38
BANKS = 3



def front_tasks():
    t4 = range(NT)
    tasks = [("load_adj",), ("mask",), ("hmat",), ("ln0",)]
    tasks += [("ht", t) for t in t4]
    tasks += [("dn",), ("h0",)]
    tasks += [("gexp", t) for t in t4]
    tasks += [("m", t) for t in t4]
    tasks += [("u", f) for f in range(FD)]
    tasks += [("w1", t) for t in t4]
    tasks += [("ln1",), ("pad",), ("ln1_apply",)]
    tasks += [("gt", h) for h in range(HD)]
    tasks += [("z", t) for t in t4]
    tasks += [("m2", t) for t in t4]
    tasks += [("x1", t) for t in t4]
    tasks += [("ln2",), ("pad",), ("h1",)]
    tasks += [("h1t", f) for f in range(FD)]
    for p in range(PAIRS):
        tasks += [("qk", p, 0), ("qk", p, 1), ("stack", p)]
    return [("F",) + t for t in tasks]


def back_tasks():
    t4 = range(NT)
    tasks = [("deg",)]
    tasks += [("at", t) for t in t4]
    tasks += [("lnb2",), ("pad",), ("h2",), ("sb",)]
    tasks += [("h2t", f) for f in range(FD)]
    tasks += [("y", t) for t in t4]
    tasks += [("pair_exp", t) for t in t4]
    tasks += [("pad",), ("pad",)]
    tasks += [("o2", t) for t in t4]
    tasks += [("lnb3",), ("pad",), ("h3",)]
    tasks += [("h3t", f) for f in range(FD)]
    tasks += [("zp", t) for t in t4]
    tasks += [("agg", t) for t in t4]
    tasks += [("store",)]
    return [("B",) + t for t in tasks]


def attention_ticks():
    tiles = HEADS * NT
    ticks = []
    for g in range(tiles + 3):
        tick = []
        if g < tiles:
            tick.append(("A", "score", g))
        if 1 <= g <= tiles:
            tick.append(("A", "norm", g - 1))
        if 2 <= g <= tiles + 1:
            tick.append(("A", "turn", g - 2))
        if g >= 3 and (g - 3) % NT == NT - 1:
            tick.append(("A", "pv", (g - 3) // NT))
        ticks.append(tick)
    return ticks


def spread(a, b):
    out, i, j = [], 0, 0
    while i < len(a) or j < len(b):
        if j >= len(b) or (i < len(a) and i * len(b) <= j * len(a)):
            out.append(a[i])
            i += 1
        else:
            out.append(b[j])
            j += 1
    return out


def body_order(with_front, with_back):
    head = [("A", "v", t) for t in range(NT)]
    if with_back:
        head += [("B", "load_adj")] + [("B", "wo", t) for t in range(NT)]
    if with_front:
        head += [("F", "load_x")]
    rest = spread(front_tasks() if with_front else [], back_tasks() if with_back else [])
    ticks = attention_ticks()
    order, done = list(head), 0
    for n, tick in enumerate(ticks):
        order += tick
        upto = len(rest) * (n + 1) // len(ticks)
        order += rest[done:upto]
        done = upto
    return order


BANK_USES = {"ht", "dn", "m", "u", "w1", "gt", "z", "m2", "x1", "h1t", "qk", "v",
             "wo", "at", "sb", "h2t", "y", "o2", "h3t", "zp", "agg"}


class Batch:

    def __init__(self, turn, offset):
        self.turn, self.offset = turn, offset

    def exists(self):
        return not isinstance(self.turn, int) or 2 * self.turn + self.offset >= 0

    def before(self, n=1):
        return Batch(self.turn, self.offset - n)

    @property
    def index(self):
        return self.turn * 2 + self.offset

    @property
    def slot(self):
        return self.offset % 2

    def nth(self, per, k):
        return self.turn * (2 * per) + (self.offset * per + k)


def parts(fori):
    yield {"F": Batch(0, 0)}, [("F", "load_x")] + front_tasks()
    yield {"F": Batch(0, 1), "A": Batch(0, 0)}, body_order(True, False)
    with fori(0, (BATCHES - 2) // 2) as turn:
        for k in (1, 2):
            yield ({"F": Batch(turn, k + 1), "A": Batch(turn, k), "B": Batch(turn, k - 1)},
                   body_order(True, True))
    yield {"A": Batch(0, BATCHES - 1), "B": Batch(0, BATCHES - 2)}, body_order(False, True)
    yield {"B": Batch(0, BATCHES - 1)}, ([("B", "load_adj")] + [("B", "wo", t) for t in range(NT)]
                                         + back_tasks())


def walk(fori, handlers, start_part=None):
    for batches, order in parts(fori):
        if start_part:
            start_part(batches, order)
        for n, (stage, name, *where) in enumerate(order):
            if name != "pad" and (stage, name) in handlers:
                handlers[stage, name](batches[stage], *where)


def gnn_kernel(nc, x, adj, nodemask, W1, b1, gamma, beta, W2, b2, Wqkv, Wout, bout, w, a, W3, out):
    with ExitStack() as ctx:
        def sb(name, shape, dt=F32):
            return ctx.enter_context(nc.sbuf_tensor(name, shape, dt))

        def sem(name):
            return ctx.enter_context(nc.semaphore(name))

        ident = sb("ident", [P, P])
        ident16 = sb("ident16", [P, P], F16)
        ones = sb("ones", [P, P])
        half_power = sb("half_power", [P, NT])
        eps_tile = sb("eps_tile", [P, NT])
        minus_one = sb("minus_one", [P, NT])
        w1t = sb("w1t", [P, FD, DH])
        w2t = sb("w2t", [P, HD, D])
        wqk = sb("wqk", [P, 2, FD, DH])
        wv = sb("wv", [P, FD, DH])
        wo = sb("wo", [P, PAIRS, D])
        wl2 = sb("wl2", [P, FD, D])
        w3t = sb("w3t", [P, FD, 2 * D])
        b1row = sb("b1row", [P, DH])
        b2row = sb("b2row", [P, D])
        boutrow = sb("boutrow", [P, D])
        warow = sb("warow", [P, D])
        gcol = sb("gcol", [P, HD])
        bcol = sb("bcol", [P, HD])
        wacol = sb("wacol", [P, FD])

        adjf = sb("adjf", [P, 2, NT, NODES])
        hmat = sb("hmat", [P, NT, NODES], F16)
        htm = sb("htm", [P, NT, NODES], F16)
        SPLIT = 2 * D + 2
        hz = sb("hz", [P, NT, SPLIT], F16)
        mm = sb("mm", [P, NT, 2, D], F16)
        colf = sb("colf", [P, FD, NODES])
        rbuf = sb("rbuf", [P, NT, DH])
        xs = sb("xs", [P, 2, NT, D])
        hrow = sb("hrow", [P, NT, D])
        nat = sb("nat", [P, 2, 4, NODES], F16)
        mrow8 = sb("mrow8", [P, NODES], U8)
        mcol8 = sb("mcol8", [P, NT], U8)
        mrow = sb("mrow", [P, NODES])
        mcol = sb("mcol", [P, NT])
        wcol = sb("wcol", [P, NT])
        wcol2 = sb("wcol2", [P, NT, 2], F16)
        dsum = sb("dsum", [P, NT])
        dpos = sb("dpos", [P, NT])
        dinv = sb("dinv", [P, NT])
        binv = sb("binv", [P, NT])
        qs = sb("qs", [P, HEADS, NODES], F16)
        ks = sb("ks", [P, HEADS, 2, NODES], F16)
        vs = sb("vs", [P, NT, HEADS, 2, DIM_HEAD], F16)
        mbias = sb("mbias", [P, 2, NODES])
        escale = sb("escale", [P, 2, NT])
        sm = sb("sm", [P, NT, NODES])
        smax = sb("smax", [P, NT])
        nbias = sb("nbias", [P, NT])
        esum = sb("esum", [P, NT])
        einv = sb("einv", [P, NT])
        pt = sb("pt", [P, 2, 2, NT, NODES], F16)
        otmp = sb("otmp", [DIM_HEAD, NODES])
        ot = sb("ot", [P, PAIRS, NODES])
        adjb = sb("adjb", [P, NT, NODES])
        th = sb("th", [P, NT, NODES])
        xb = sb("xb", [P, NT, D])
        hb = sb("hb", [P, NT, D])
        hbt = sb("hbt", [P, FD, NODES])
        yz = sb("yz", [P, NT, D + 1])
        deg = sb("deg", [P, NT])
        rdeg = sb("rdeg", [P, NT])
        sj = sb("sj", [P, NT])
        sj8 = sb("sj8", [P, NT])
        rden = sb("rden", [P, NT])
        stats = sb("stats", [P, 2, NT, 6])
        moments = sb("moments", [P, 2, NT, 2])
        vpe = sb("vpe", [P, 2, NT])
        rstd = sb("rstd", [P, 2, NT])
        nmr = sb("nmr", [P, 2, NT])

        bank = [ctx.enter_context(nc.psum_tensor(f"bank{i}", [P, 512], F32)) for i in range(BANKS)]
        psS = [ctx.enter_context(nc.psum_tensor(f"psS{i}", [P, 512], F32)) for i in range(2)]
        psT = [ctx.enter_context(nc.psum_tensor(f"psT{i}", [P, 512], F32)) for i in range(2)]
        psO = ctx.enter_context(nc.psum_tensor("psO", [P, 512], F32))

        s_const = sem("s_const")
        s_wload = sem("s_wload")
        s_ones = sem("s_ones")
        s_wready = sem("s_wready")
        s_wturn = sem("s_wturn")
        s_wcopy = sem("s_wcopy")
        s_wa = sem("s_wa")
        adj_in = sem("adj_in")
        x_in = sem("x_in")
        mask_in = sem("mask_in")
        adjb_in = sem("adjb_in")
        stack_in = [sem(f"stack_in{p}") for p in range(PAIRS)]
        out_stored = sem("out_stored")
        ready = {n: sem(f"{n}_ready") for n in sorted(BANK_USES | {"score", "turn", "pv"})}
        by_act = {n: sem(f"{n}_act") for n in ("ht", "m", "u", "gt", "z", "m2", "h1t", "qk", "v",
                                              "turn", "pv", "at", "sb", "h2t", "y", "h3t", "zp")}
        by_dve = {n: sem(f"{n}_dve") for n in ("dn", "m", "w1", "z", "m2", "x1", "qk", "v", "score",
                                              "turn", "pv", "wo", "o2", "agg")}
        mask_done = sem("mask_done")
        hmat_done = sem("hmat_done")
        wcol_done = sem("wcol_done")
        binv_done = sem("binv_done")
        dn_step = sem("dn_step")
        relu_done = sem("relu_done")
        h0_done = sem("h0_done")
        h0_high = sem("h0_high")
        h0_low = sem("h0_low")
        xh_done = sem("xh_done")
        g1_done = sem("g1_done")
        h1_done = sem("h1_done")
        xbias_done = sem("xbias_done")
        LNS = ("ln0", "ln1", "ln2", "lnb2", "lnb3")
        ln_stats = {n: sem(f"{n}_stats") for n in LNS}
        ln_moments = {n: sem(f"{n}_moments") for n in LNS}
        ln_scale = {n: sem(f"{n}_scale") for n in LNS}
        gexp_done = sem("gexp_done")
        gadd_done = sem("gadd_done")
        shared_done = sem("shared_done")
        nbias_done = sem("nbias_done")
        exp_done = sem("exp_done")
        einv_done = sem("einv_done")
        attn_done = sem("attn_done")
        deg_step = sem("deg_step")
        h2_done = sem("h2_done")
        sj_done = sem("sj_done")
        diag_done = sem("diag_done")
        leaky_done = sem("leaky_done")
        pexp_done = sem("pexp_done")
        pair_done = sem("pair_done")
        rden_done = sem("rden_done")
        h3_done = sem("h3_done")
        sum_done = sem("sum_done")

        freed = {"ht": (by_act, 4), "dn": (by_dve, 1), "m": (by_dve, 4), "u": (by_act, 2),
                 "w1": (by_dve, 4), "gt": (by_act, 4), "z": (by_dve, 4), "m2": (by_dve, 4),
                 "x1": (by_dve, 4), "h1t": (by_act, 2), "qk": (by_dve, 8), "v": (by_dve, 4),
                 "wo": (by_dve, 4), "at": (by_act, 4), "sb": (by_act, 4), "h2t": (by_act, 2),
                 "y": (by_act, 4), "o2": (by_dve, 4), "h3t": (by_act, 2), "zp": (by_act, 4),
                 "agg": (by_dve, 4)}

        def use_number(name, where):
            if name == "qk":
                return 2 * where[0] + where[1] + 1
            if name == "sb":
                return 4
            return (where[0] if where else 0) + 1

        sp_went = sem("sp_went")
        dve_went = sem("dve_went")

        current = {}

        def bank_uses(order):
            return [task for task in order if task[1] in BANK_USES]

        def note_part(batches, order):
            current["uses"] = bank_uses(order)

        def bank_of(b, name, *where):
            n = next(i for i, task in enumerate(current["uses"]) if task[1:] == (name,) + where)
            return bank[n % BANKS][:]

        block = ctx.enter_context(nc.Block())

        @block.sync
        def _(sp):
            sp.dma_start(rbuf[:, 0:HD, 0:D], W1.rearrange("(t p) d -> p t d", p=P)).then_inc(s_wload, 16)
            sp.dma_start(th[:, 0:FD, :], W2.rearrange("(t p) h -> p t h", p=P)).then_inc(s_wload, 16)
            sp.dma_start(th[:, FD:2 * FD, :], W3.rearrange("(t p) f -> p t f", p=P)).then_inc(s_wload, 16)
            sp.dma_start(wl2[:], w.rearrange("(t p) d -> p t d", p=P)).then_inc(s_wload, 16)
            sp.dma_start(warow[:], a.partition_broadcast(P)).then_inc(s_wload, 16)
            sp.dma_start(gcol[:], gamma.rearrange("(t p) -> p t", p=P), allow_slow_non_contiguous=True).then_inc(s_wload, 16)
            sp.dma_start(bcol[:], beta.rearrange("(t p) -> p t", p=P), allow_slow_non_contiguous=True).then_inc(s_wload, 16)
            sp.dma_start(b1row[:], b1.partition_broadcast(P)).then_inc(s_wload, 16)
            sp.dma_start(b2row[:], b2.partition_broadcast(P)).then_inc(s_wload, 16)
            sp.dma_start(boutrow[:], bout.partition_broadcast(P)).then_inc(s_wload, 16)
            qkv = Wqkv.rearrange("(t p) (h c d) -> p c t h d", p=P, h=HEADS, c=3)
            for t in range(FD):
                for c in range(2):
                    sp.dma_start(wqk[:, c, t, :].rearrange("p (h d) -> p h d", h=HEADS),
                                 qkv[:, c, t]).then_inc(s_wload, 16)
                sp.dma_start(wv[:, t, :].rearrange("p (h d) -> p h d", h=HEADS),
                             qkv[:, 2, t]).then_inc(s_wload, 16)
            sp.dma_start(wo[:], Wout.rearrange("(t p) d -> p t d", p=P)).then_inc(s_wload, 16)

            def load_adj(b):
                if b.before(2).exists():
                    sp.wait_ge(attn_done, b.before(2).nth(32, 32))
                    sp.sem_inc(sp_went, 1)
                    sp.wait_ge(wcol_done, b.before(1).nth(2, 2))
                    sp.sem_inc(sp_went, 1)
                    sp.wait_ge(shared_done, b.before(1).nth(4, 4))
                    sp.sem_inc(sp_went, 1)
                elif b.before(1).exists():
                    sp.wait_ge(wcol_done, b.before(1).nth(2, 2))
                    sp.sem_inc(sp_went, 1)
                    sp.wait_ge(shared_done, b.before(1).nth(4, 4))
                    sp.sem_inc(sp_went, 1)
                sp.dma_start(adjf[:, b.slot], adj[b.index].rearrange("(t p) c -> p t c", p=P)).then_inc(adj_in, 16)
                sp.dma_start(wcol[:], adj[b.index, 0, :].rearrange("(t p) -> p t", p=P),
                             allow_slow_non_contiguous=True).then_inc(adj_in, 16)
                sp.dma_start(mcol8[:], nodemask[b.index].rearrange("(t p) -> p t", p=P),
                             allow_slow_non_contiguous=True).then_inc(mask_in, 16)
                sp.dma_start(mrow8[:], nodemask[b.index].partition_broadcast(P)).then_inc(mask_in, 16)

            def load_x(b):
                if b.before(2).exists():
                    sp.wait_ge(by_dve["wo"], b.before(2).nth(4, 4))
                    sp.sem_inc(sp_went, 1)
                sp.dma_start(xs[:, b.slot], x[b.index].rearrange("(t p) d -> p t d", p=P)).then_inc(x_in, 16)

            def stack(b, p):
                sp.wait_ge(by_act["qk"], b.nth(8, 2 * p + 2))
                sp.sem_inc(sp_went, 1)
                sp.wait_ge(by_dve["qk"], b.nth(8, 2 * p + 2))
                sp.sem_inc(sp_went, 1)
                if b.before().exists():
                    sp.wait_ge(ready["score"], b.before().nth(32, 8 * p + 8))
                    sp.sem_inc(sp_went, 1)
                for e in range(2):
                    rows = slice(e * DIM_HEAD, (e + 1) * DIM_HEAD)
                    h = 2 * p + e
                    for part in range(2):
                        to = slice(part * DIM_HEAD, (part + 1) * DIM_HEAD)
                        sp.dma_start(qs[to, h, :], nat[rows, p % 2, part, :]).then_inc(stack_in[p], 16)
                        sp.dma_start(ks[to, h, :, :], nat[rows, p % 2, 2:4, :]).then_inc(stack_in[p], 16)

            def load_adjb(b):
                if b.before().exists():
                    sp.wait_ge(ready["agg"], b.before().nth(4, 4))
                    sp.sem_inc(sp_went, 1)
                sp.dma_start(adjb[:], adj[b.index].rearrange("(t p) c -> p t c", p=P)).then_inc(adjb_in, 16)

            def store(b):
                sp.wait_ge(by_dve["agg"], b.nth(4, 4))
                sp.sem_inc(sp_went, 1)
                sp.wait_ge(sum_done, b.nth(4, 4))
                sp.sem_inc(sp_went, 1)
                sp.dma_start(out[b.index].rearrange("(t p) d -> p t d", p=P), hb[:]).then_inc(out_stored, 16)

            walk(sp.Fori, {("F", "load_adj"): load_adj, ("F", "load_x"): load_x, ("F", "stack"): stack,
                           ("B", "load_adj"): load_adjb, ("B", "store"): store})
            sp.wait_ge(out_stored, 16 * BATCHES)

        @block.gpsimd
        def _(pool):
            pool.memset(ones[:], 1.0).then_inc(s_ones, 1)
            pool.memset(half_power[:], -0.5).then_inc(s_const, 1)
            pool.memset(eps_tile[:], EPS_LN).then_inc(s_const, 1)
            pool.memset(minus_one[:], -1.0).then_inc(s_const, 1)
            pool.memset(hz[:, :, D:D + 2], 1.0).then_inc(s_const, 1)
            pool.memset(yz[:, :, D:D + 1], 1.0).then_inc(s_const, 1)
            pool.wait_ge(s_ones, 1)
            pool.affine_select(out=ident[:], in_=ones[:], compare_op=ALU.is_equal, fill=0.0, base=0,
                               pattern=[[-1, P]], channel_multiplier=1).then_inc(s_const, 1)
            pool.wait_ge(s_const, 6)
            pool.tensor_copy(ident16[:], ident[:]).then_inc(s_const, 1)

            def ln_scales(name, chain):
                def scales(b):
                    pool.wait_ge(ln_moments[name], b.nth(4, 4))
                    pool.tensor_tensor(vpe[:, chain], moments[:, chain, :, 1], eps_tile[:],
                                       ALU.add).then_inc(ln_scale[name], 1)
                    pool.wait_ge(ln_scale[name], b.nth(4, 1))
                    pool.tensor_tensor(rstd[:, chain], vpe[:, chain], half_power[:],
                                       ALU.pow).then_inc(ln_scale[name], 1)
                    pool.wait_ge(ln_scale[name], b.nth(4, 2))
                    pool.tensor_tensor(vpe[:, chain], moments[:, chain, :, 0], rstd[:, chain],
                                       ALU.mult).then_inc(ln_scale[name], 1)
                    pool.wait_ge(ln_scale[name], b.nth(4, 3))
                    pool.tensor_tensor(nmr[:, chain], vpe[:, chain], minus_one[:],
                                       ALU.mult).then_inc(ln_scale[name], 1)
                return scales

            def h0(b):
                pool.wait_ge(h0_done, b.nth(4, 4))
                pool.tensor_tensor(xs[:, b.slot], xs[:, b.slot], hrow[:], ALU.add).then_inc(xh_done, 1)
                pool.wait_ge(h0_high, b.nth(1, 1))
                pool.tensor_tensor(hz[:, :, D + 2:], hrow[:], hz[:, :, 0:D], ALU.subtract).then_inc(h0_low, 1)
                pool.wait_ge(xh_done, b.nth(2, 1))
                pool.tensor_tensor(xs[:, b.slot], xs[:, b.slot],
                                   b2row[:].unsqueeze(1).to_broadcast([P, NT, D]), ALU.add).then_inc(xh_done, 1)

            def gexp(b, t):
                tile = adjf[:, b.slot, t, :]
                pool.wait_ge(gexp_done, b.nth(4, t + 1))
                pool.wait_ge(hmat_done, b.nth(1, 1))
                pool.tensor_tensor(tile, tile, colf[:, t % 2, :], ALU.add).then_inc(gadd_done, 1)
                pool.wait_ge(gadd_done, b.nth(8, 2 * t + 1))
                pool.wait_ge(mask_done, b.nth(4, 4))
                pool.tensor_tensor(tile, tile, mrow[:], ALU.mult).then_inc(gadd_done, 1)
                pool.wait_ge(gadd_done, b.nth(8, 2 * t + 2))
                pool.tensor_tensor(tile, tile, mcol[:, t:t + 1].to_broadcast([P, NODES]),
                                   ALU.mult).then_inc(shared_done, 1)

            def h1(b):
                pool.wait_ge(h1_done, b.nth(4, 4))
                pool.tensor_tensor(xs[:, b.slot], xs[:, b.slot],
                                   boutrow[:].unsqueeze(1).to_broadcast([P, NT, D]), ALU.add).then_inc(xbias_done, 1)

            def pair_exp(b, t):
                pool.wait_ge(pexp_done, b.nth(4, t + 1))
                pool.wait_ge(by_act["at"], b.nth(4, t + 1))
                pool.tensor_tensor(th[:, t, :], th[:, t, :], adjb[:, t, :], ALU.mult).then_inc(pair_done, 1)

            walk(pool.Fori, {("F", "ln0"): ln_scales("ln0", 0), ("F", "h0"): h0, ("F", "gexp"): gexp,
                             ("F", "ln1"): ln_scales("ln1", 0), ("F", "ln2"): ln_scales("ln2", 0),
                             ("F", "h1"): h1, ("B", "lnb2"): ln_scales("lnb2", 1),
                             ("B", "pair_exp"): pair_exp, ("B", "lnb3"): ln_scales("lnb3", 1)})

        @block.scalar
        def _(act):
            weight_tiles = ([w1t[:, f, :] for f in range(FD)]
                            + [w2t[:, h, :] for h in range(HD)]
                            + [w3t[:, f, half * D:(half + 1) * D] for f in range(FD) for half in range(2)])
            for n, tile in enumerate(weight_tiles):
                act.wait_ge(s_wturn, n + 1)
                width = tile.shape[-1]
                act.activation(tile, bank[n % 2][:, 0:width], ACT.Copy).then_inc(s_wcopy, 1)

            def ht(b, t):
                act.wait_ge(ready["ht"], b.nth(4, t + 1))
                act.activation(htm[:, t, :], bank_of(b, "ht", t).bitcast(F16)[:, 0:NODES], ACT.Copy)\
                    .then_inc(by_act["ht"], 1)

            def h0(b):
                act.wait_ge(ln_scale["ln0"], b.nth(4, 4))
                act.wait_ge(x_in, b.nth(16, 16))
                for t in range(NT):
                    act.activation(hrow[:, t, :], xs[:, b.slot, t, :], ACT.Relu, bias=nmr[:, 0, t:t + 1],
                                   scale=rstd[:, 0, t:t + 1]).then_inc(h0_done, 1)

            def gexp(b, t):
                act.wait_ge(adj_in, b.nth(32, 32))
                if t == 0 and b.before().exists():
                    act.wait_ge(ready["v"], b.before().nth(4, 4))
                if t >= 2:
                    act.wait_ge(gadd_done, b.nth(8, 2 * (t - 2) + 1))
                act.activation(colf[:, t % 2, :], adjf[:, b.slot, t, :], ACT.Exp, scale=-1.0).then_inc(gexp_done, 1)

            def m(b, t):
                act.wait_ge(binv_done, b.nth(8, 2 * t + 2))
                act.activation(mm[:, t, 0, :], bank_of(b, "m", t)[:, 0:D], ACT.Copy,
                               scale=binv[:, t:t + 1]).then_inc(by_act["m"], 1)

            def u(b, f):
                act.wait_ge(ready["u"], b.nth(2, f + 1))
                act.wait_ge(gadd_done, b.nth(8, 7))
                act.activation(colf[:, f, :], bank_of(b, "u", f), ACT.Copy).then_inc(by_act["u"], 1)

            def w1(b, t):
                act.wait_ge(by_dve["w1"], b.nth(4, t + 1))
                act.activation(rbuf[:, t, :], rbuf[:, t, :], ACT.Relu).then_inc(relu_done, 1)

            def ln1_apply(b):
                act.wait_ge(ln_scale["ln1"], b.nth(4, 4))
                for t in range(NT):
                    act.activation(rbuf[:, t, :], rbuf[:, t, :], ACT.Identity, bias=nmr[:, 0, t:t + 1],
                                   scale=rstd[:, 0, t:t + 1]).then_inc(g1_done, 1)

            def gt(b, h):
                act.wait_ge(ready["gt"], b.nth(4, h + 1))
                act.activation(rbuf[:, :, h * P:(h + 1) * P],
                               bank_of(b, "gt", h).rearrange("p (t n) -> p t n", t=NT), ACT.Identity,
                               bias=bcol[:, h:h + 1], scale=gcol[:, h:h + 1]).then_inc(by_act["gt"], 1)

            def z(b, t):
                act.wait_ge(ready["z"], b.nth(4, t + 1))
                act.activation(hz[:, t, 0:D], bank_of(b, "z", t)[:, 0:D], ACT.Copy).then_inc(by_act["z"], 1)

            def m2(b, t):
                act.wait_ge(ready["m2"], b.nth(4, t + 1))
                act.activation(mm[:, t, 0, :], bank_of(b, "m2", t)[:, 0:D], ACT.Copy,
                               scale=binv[:, t:t + 1]).then_inc(by_act["m2"], 1)

            def h1(b):
                act.wait_ge(ln_scale["ln2"], b.nth(4, 4))
                for t in range(NT):
                    act.activation(hrow[:, t, :], xs[:, b.slot, t, :], ACT.Relu, bias=nmr[:, 0, t:t + 1],
                                   scale=rstd[:, 0, t:t + 1]).then_inc(h1_done, 1)

            def h1t(b, f):
                act.wait_ge(ready["h1t"], b.nth(2, f + 1))
                act.activation(colf[:, f, :], bank_of(b, "h1t", f), ACT.Copy).then_inc(by_act["h1t"], 1)

            def qk(b, p, c):
                act.wait_ge(ready["qk"], b.nth(8, 2 * p + c + 1))
                if p >= 2:
                    act.wait_ge(stack_in[p - 2], b.nth(128, 128))
                elif b.before().exists():
                    act.wait_ge(stack_in[p + 2], b.before().nth(128, 128))
                act.activation(nat[:, p % 2, 2 * c, :], bank_of(b, "qk", p, c), ACT.Copy).then_inc(by_act["qk"], 1)

            def v(b, t):
                act.wait_ge(ready["v"], b.nth(4, t + 1))
                act.activation(vs[:, t, :, 0, :], bank_of(b, "v", t).rearrange("p (h d) -> p h d", h=HEADS),
                               ACT.Copy).then_inc(by_act["v"], 1)

            def score(b, g):
                act.wait_ge(nbias_done, b.nth(32, g + 1))
                if g >= NT:
                    act.wait_ge(attn_done, b.nth(32, g - NT + 1))
                elif b.before().exists():
                    act.wait_ge(attn_done, b.before().nth(32, 32 - NT + g + 1))
                act.activation(sm[:, g % NT, :], sm[:, g % NT, :], ACT.Exp, bias=nbias[:, g % NT:g % NT + 1],
                               scale=escale[:, b.slot, g % NT:g % NT + 1],
                               accum_out=esum[:, g % NT:g % NT + 1]).then_inc(exp_done, 1)

            def turn(b, g):
                act.wait_ge(ready["turn"], b.nth(32, g + 1))
                h, t = g // NT, g % NT
                if h >= 2:
                    act.wait_ge(ready["pv"], b.nth(8, h - 1))
                act.activation(pt[:, h % 2, 0, :, t * P:(t + 1) * P],
                               psT[g % 2][:].rearrange("p (j n) -> p j n", j=NT), ACT.Copy).then_inc(by_act["turn"], 1)

            def pv(b, h):
                act.wait_ge(ready["pv"], b.nth(8, h + 1))
                if h >= 1:
                    act.wait_ge(by_dve["pv"], b.nth(8, h))
                elif b.before().exists():
                    act.wait_ge(by_dve["pv"], b.before().nth(8, 8))
                act.activation(otmp[:], psO[DIM_HEAD:P, :], ACT.Copy).then_inc(by_act["pv"], 1)

            def at(b, t):
                act.wait_ge(ready["at"], b.nth(4, t + 1))
                act.wait_ge(deg_step, b.nth(3, 1))
                act.activation(adjb[:, t, :], bank_of(b, "at", t), ACT.Copy).then_inc(by_act["at"], 1)

            def h2(b):
                act.wait_ge(ln_scale["lnb2"], b.nth(4, 4))
                if b.before().exists():
                    act.wait_ge(out_stored, b.before().nth(16, 16))
                for t in range(NT):
                    act.activation(hb[:, t, :], xb[:, t, :], ACT.Relu, bias=nmr[:, 1, t:t + 1],
                                   scale=rstd[:, 1, t:t + 1]).then_inc(h2_done, 1)

            def sb_(b):
                act.wait_ge(ready["sb"], b.nth(1, 1))
                for j in range(NT):
                    act.activation(th[:, :, j * P:(j + 1) * P],
                                   bank_of(b, "sb").rearrange("p (t n) -> p t n", t=NT), ACT.Tanh,
                                   bias=sj8[:, j:j + 1], scale=1.0 / TANH_RANGE).then_inc(by_act["sb"], 1)

            def h2t(b, f):
                act.wait_ge(ready["h2t"], b.nth(2, f + 1))
                act.activation(hbt[:, f, :], bank_of(b, "h2t", f), ACT.Copy).then_inc(by_act["h2t"], 1)

            def y(b, t):
                act.wait_ge(ready["y"], b.nth(4, t + 1))
                if b.before().exists():
                    act.wait_ge(by_dve["agg"], b.before().nth(4, 4))
                act.activation(yz[:, t, 0:D], bank_of(b, "y", t)[:, 0:D], ACT.Copy).then_inc(by_act["y"], 1)

            def pair_exp(b, t):
                act.wait_ge(leaky_done, b.nth(4, t + 1))
                act.activation(th[:, t, :], th[:, t, :], ACT.Exp, scale=TANH_RANGE).then_inc(pexp_done, 1)

            def h3(b):
                act.wait_ge(ln_scale["lnb3"], b.nth(4, 4))
                act.wait_ge(sj_done, b.nth(5, 4))
                for t in range(NT):
                    act.activation(hb[:, t, :], xb[:, t, :], ACT.Relu, bias=nmr[:, 1, t:t + 1],
                                   scale=rstd[:, 1, t:t + 1]).then_inc(h3_done, 1)

            def h3t(b, f):
                act.wait_ge(ready["h3t"], b.nth(2, f + 1))
                act.activation(hbt[:, f, :], bank_of(b, "h3t", f), ACT.Copy).then_inc(by_act["h3t"], 1)

            def zp(b, t):
                act.wait_ge(ready["zp"], b.nth(4, t + 1))
                act.activation(yz[:, t, 0:D], bank_of(b, "zp", t)[:, 0:D], ACT.Copy).then_inc(by_act["zp"], 1)
                act.activation(hb[:, t, :], bank_of(b, "zp", t)[:, D:], ACT.Copy).then_inc(by_act["zp"], 1)

            walk(act.Fori, {
                ("F", "ht"): ht, ("F", "h0"): h0, ("F", "gexp"): gexp, ("F", "m"): m, ("F", "u"): u,
                ("F", "w1"): w1, ("F", "ln1_apply"): ln1_apply, ("F", "gt"): gt, ("F", "z"): z, ("F", "m2"): m2,
                ("F", "h1"): h1, ("F", "h1t"): h1t, ("F", "qk"): qk, ("A", "v"): v, ("A", "score"): score,
                ("A", "turn"): turn, ("A", "pv"): pv, ("B", "at"): at, ("B", "h2"): h2, ("B", "sb"): sb_,
                ("B", "h2t"): h2t, ("B", "y"): y, ("B", "pair_exp"): pair_exp, ("B", "h3"): h3,
                ("B", "h3t"): h3t, ("B", "zp"): zp}, note_part)

        @block.vector
        def _(dve):
            dve.wait_ge(s_wload, 16 * 17)
            for f in range(FD):
                dve.tensor_tensor_reduce(hb[:, f, :], wl2[:, f, :], warow[:], 1.0, 0.0, ALU.mult, ALU.add,
                                         wacol[:, f:f + 1]).then_inc(s_wa, 1)
            dve.wait_ge(s_wa, FD)
            dve.wait_ge(s_const, 7)
            for f in range(FD):
                dve.tensor_scalar(hb[:, f, 0:P], ident[:], wacol[:, f:f + 1], None, ALU.mult).then_inc(s_wa, 1)
            dve.wait_ge(s_wturn, FD + HD + 2 * FD + 1)
            dve.tensor_copy(warow[:], bank[2][:, 0:D]).then_inc(s_wready, 1)

            def mask(b):
                dve.wait_ge(mask_in, b.nth(32, 32))
                if b.before(2).exists():
                    dve.wait_ge(exp_done, b.before(2).nth(32, 32))
                dve.tensor_copy(mrow[:], mrow8[:]).then_inc(mask_done, 1)
                dve.tensor_copy(mcol[:], mcol8[:]).then_inc(mask_done, 1)
                dve.wait_ge(mask_done, b.nth(4, 2))
                dve.tensor_scalar(mbias[:, b.slot], mrow[:], 1.0, MASKED, ALU.subtract, ALU.mult).then_inc(mask_done, 1)
                dve.tensor_scalar(escale[:, b.slot], mcol[:], DIM_HEAD ** -0.5, None, ALU.mult).then_inc(mask_done, 1)

            def hmat_(b):
                dve.wait_ge(adj_in, b.nth(32, 32))
                dve.tensor_scalar(hmat[:], adjf[:, b.slot], 0.0, None, ALU.not_equal).then_inc(hmat_done, 1)
                dve.tensor_copy(wcol2[:, :, 0], wcol[:]).then_inc(wcol_done, 1)
                dve.wait_ge(wcol_done, b.nth(2, 1))
                dve.tensor_tensor(wcol2[:, :, 1], wcol[:], wcol2[:, :, 0], ALU.subtract).then_inc(wcol_done, 1)

            def norm(name, chain, source, arrived):
                def moments_of(b):
                    arrived(b)
                    for t in range(NT):
                        dve.bn_stats(stats[:, chain, t, :], source(b)[:, t, :]).then_inc(ln_stats[name], 1)
                    for t in range(NT):
                        dve.wait_ge(ln_stats[name], b.nth(4, t + 1))
                        dve.sem_inc(dve_went, 1)
                        dve.bn_aggr(moments[:, chain, t, :], stats[:, chain, t, :]).then_inc(ln_moments[name], 1)
                return moments_of

            def dn(b):
                dve.wait_ge(ready["dn"], b.nth(1, 1))
                dve.reduce_sum(dsum[:], bank_of(b, "dn")[:, 0:2 * NT].rearrange("p (t c) -> p t c", c=2), AX_X)\
                    .then_inc(by_dve["dn"], 1)
                dve.wait_ge(by_dve["dn"], b.nth(1, 1))
                dve.tensor_scalar(dpos[:], dsum[:], 0.0, None, ALU.is_gt).then_inc(dn_step, 1)
                dve.tensor_scalar(dinv[:], dsum[:], TINY, None, ALU.max).then_inc(dn_step, 1)
                dve.wait_ge(dn_step, b.nth(4, 2))
                dve.reciprocal(dinv[:], dinv[:]).then_inc(dn_step, 1)
                dve.wait_ge(dn_step, b.nth(4, 3))
                dve.tensor_tensor(dinv[:], dinv[:], dpos[:], ALU.mult).then_inc(dn_step, 1)

            def h0(b):
                dve.wait_ge(h0_done, b.nth(4, 4))
                dve.tensor_copy(hz[:, :, 0:D], hrow[:]).then_inc(h0_high, 1)

            def m(b, t):
                dve.wait_ge(ready["m"], b.nth(4, t + 1))
                dve.tensor_scalar(binv[:, t:t + 1], bank_of(b, "m", t)[:, D:D + 1], 1.0, None, ALU.max)\
                    .then_inc(binv_done, 1)
                dve.wait_ge(binv_done, b.nth(8, 2 * t + 1))
                dve.reciprocal(binv[:, t:t + 1], binv[:, t:t + 1]).then_inc(binv_done, 1)
                dve.wait_ge(by_act["m"], b.nth(4, t + 1))
                dve.scalar_tensor_tensor(mm[:, t, 1, :], bank_of(b, "m", t)[:, 0:D], binv[:, t:t + 1],
                                         mm[:, t, 0, :], ALU.mult, ALU.subtract).then_inc(by_dve["m"], 1)

            def w1(b, t):
                dve.wait_ge(ready["w1"], b.nth(4, t + 1))
                dve.wait_ge(dn_step, b.nth(4, 4))
                dve.scalar_tensor_tensor(rbuf[:, t, :], bank_of(b, "w1", t), dinv[:, t:t + 1], b1row[:],
                                         ALU.mult, ALU.add).then_inc(by_dve["w1"], 1)

            def z(b, t):
                dve.wait_ge(by_act["z"], b.nth(4, t + 1))
                dve.tensor_tensor(hz[:, t, D + 2:], bank_of(b, "z", t)[:, 0:D], hz[:, t, 0:D], ALU.subtract)\
                    .then_inc(by_dve["z"], 1)

            def m2(b, t):
                dve.wait_ge(by_act["m2"], b.nth(4, t + 1))
                dve.scalar_tensor_tensor(mm[:, t, 1, :], bank_of(b, "m2", t)[:, 0:D], binv[:, t:t + 1],
                                         mm[:, t, 0, :], ALU.mult, ALU.subtract).then_inc(by_dve["m2"], 1)

            def x1(b, t):
                dve.wait_ge(ready["x1"], b.nth(4, t + 1))
                dve.wait_ge(xh_done, b.nth(2, 2))
                dve.scalar_tensor_tensor(xs[:, b.slot, t, :], bank_of(b, "x1", t)[:, 0:D], dinv[:, t:t + 1],
                                         xs[:, b.slot, t, :], ALU.mult, ALU.add).then_inc(by_dve["x1"], 1)

            def qk(b, p, c):
                dve.wait_ge(by_act["qk"], b.nth(8, 2 * p + c + 1))
                dve.tensor_tensor(nat[:, p % 2, 2 * c + 1, :], bank_of(b, "qk", p, c), nat[:, p % 2, 2 * c, :],
                                  ALU.subtract).then_inc(by_dve["qk"], 1)

            def v(b, t):
                dve.wait_ge(by_act["v"], b.nth(4, t + 1))
                dve.tensor_tensor(vs[:, t, :, 1, :], bank_of(b, "v", t).rearrange("p (h d) -> p h d", h=HEADS),
                                  vs[:, t, :, 0, :], ALU.subtract).then_inc(by_dve["v"], 1)

            def score(b, g):
                s = slice(g % NT, g % NT + 1)
                dve.wait_ge(ready["score"], b.nth(32, g + 1))
                if g >= NT:
                    dve.wait_ge(ready["turn"], b.nth(32, g - NT + 1))
                elif b.before().exists():
                    dve.wait_ge(ready["turn"], b.before().nth(32, 32 - NT + g + 1))
                dve.sem_inc(dve_went, 1)
                dve.tensor_tensor_reduce(sm[:, g % NT, :], psS[g % 2][:], mbias[:, b.slot], 1.0, -3.4e38,
                                         ALU.add, ALU.max, smax[:, s]).then_inc(by_dve["score"], 1)
                dve.wait_ge(by_dve["score"], b.nth(32, g + 1))
                dve.scalar_tensor_tensor(nbias[:, s], smax[:, s], -1.0, escale[:, b.slot, s], ALU.mult,
                                         ALU.mult).then_inc(nbias_done, 1)

            def norm_(b, g):
                s = slice(g % NT, g % NT + 1)
                dve.wait_ge(exp_done, b.nth(32, g + 1))
                dve.reciprocal(einv[:, s], esum[:, s]).then_inc(einv_done, 1)
                dve.wait_ge(einv_done, b.nth(32, g + 1))
                if g < NT:
                    dve.wait_ge(shared_done, b.nth(4, g + 1))
                dve.scalar_tensor_tensor(sm[:, g % NT, :], sm[:, g % NT, :], einv[:, s],
                                         adjf[:, b.slot, g % NT, :], ALU.mult, ALU.add).then_inc(attn_done, 1)

            def turn(b, g):
                h, t = g // NT, g % NT
                dve.wait_ge(by_act["turn"], b.nth(32, g + 1))
                cols = slice(t * P, (t + 1) * P)
                dve.tensor_tensor(pt[:, h % 2, 1, :, cols], psT[g % 2][:].rearrange("p (j n) -> p j n", j=NT),
                                  pt[:, h % 2, 0, :, cols], ALU.subtract).then_inc(by_dve["turn"], 1)

            def pv(b, h):
                dve.wait_ge(by_act["pv"], b.nth(8, h + 1))
                if h == 0 and b.before().exists():
                    dve.wait_ge(ready["wo"], b.before().nth(4, 4))
                rows = slice((h % 2) * DIM_HEAD, (h % 2 + 1) * DIM_HEAD)
                dve.tensor_tensor(ot[rows, h // 2, :], psO[0:DIM_HEAD, :], otmp[:], ALU.add).then_inc(by_dve["pv"], 1)

            def wo_(b, t):
                dve.wait_ge(ready["wo"], b.nth(4, t + 1))
                dve.wait_ge(xbias_done, b.nth(1, 1))
                dve.scalar_tensor_tensor(xb[:, t, :], bank_of(b, "wo", t)[:, 0:D], MIX, xs[:, b.slot, t, :],
                                         ALU.mult, ALU.add).then_inc(by_dve["wo"], 1)

            def deg_(b):
                dve.wait_ge(adjb_in, b.nth(16, 16))
                dve.reduce_sum(deg[:], adjb[:], AX_X).then_inc(deg_step, 1)
                dve.wait_ge(deg_step, b.nth(3, 1))
                dve.tensor_scalar(rdeg[:], deg[:], EPS_DEG, None, ALU.max).then_inc(deg_step, 1)
                dve.wait_ge(deg_step, b.nth(3, 2))
                dve.reciprocal(rdeg[:], rdeg[:]).then_inc(deg_step, 1)

            def h2(b):
                for t in range(NT):
                    dve.wait_ge(h2_done, b.nth(4, t + 1))
                    if t == 0 and b.before().exists():
                        dve.wait_ge(ready["o2"], b.before().nth(4, 4))
                    dve.tensor_tensor_reduce(th[:, 1 + t // 2, t % 2 * D:(t % 2 + 1) * D], hb[:, t, :], warow[:], 1.0, 0.0, ALU.mult, ALU.add,
                                             sj[:, t:t + 1]).then_inc(sj_done, 1)
                dve.wait_ge(sj_done, b.nth(5, 4))
                dve.tensor_scalar(sj8[:], sj[:], 1.0 / TANH_RANGE, None, ALU.mult).then_inc(sj_done, 1)
                for t in range(NT):
                    dve.tensor_scalar(th[:, 0, t * P:(t + 1) * P], ident[:], sj[:, t:t + 1], None, ALU.mult)\
                        .then_inc(diag_done, 1)

            def pair_exp(b, t):
                dve.wait_ge(by_act["sb"], b.nth(4, 4))
                dve.scalar_tensor_tensor(th[:, t, :], th[:, t, :], LEAK, th[:, t, :], ALU.mult, ALU.max)\
                    .then_inc(leaky_done, 1)

            def o2(b, t):
                s = slice(t, t + 1)
                dve.wait_ge(ready["o2"], b.nth(4, t + 1))
                dve.reciprocal(rden[:, s], bank_of(b, "o2", t)[:, D:D + 1]).then_inc(rden_done, 1)
                dve.wait_ge(rden_done, b.nth(8, 2 * t + 1))
                dve.tensor_tensor(rden[:, s], rden[:, s], deg[:, s], ALU.mult).then_inc(rden_done, 1)
                dve.wait_ge(rden_done, b.nth(8, 2 * t + 2))
                dve.scalar_tensor_tensor(xb[:, t, :], bank_of(b, "o2", t)[:, 0:D], rden[:, s], xb[:, t, :],
                                         ALU.mult, ALU.add).then_inc(by_dve["o2"], 1)

            def agg(b, t):
                dve.wait_ge(ready["agg"], b.nth(4, t + 1))
                dve.scalar_tensor_tensor(hb[:, t, :], bank_of(b, "agg", t)[:, 0:D], rdeg[:, t:t + 1],
                                         hb[:, t, :], ALU.mult, ALU.add).then_inc(by_dve["agg"], 1)
                dve.wait_ge(by_dve["agg"], b.nth(4, t + 1))
                dve.scalar_tensor_tensor(hb[:, t, :], hb[:, t, :], 0.0, xb[:, t, :], ALU.max, ALU.add)\
                    .then_inc(sum_done, 1)

            def x_here(b):
                dve.wait_ge(x_in, b.nth(16, 16))

            def relu_here(b):
                dve.wait_ge(relu_done, b.nth(4, 4))

            def x1_here(b):
                dve.wait_ge(by_dve["x1"], b.nth(4, 4))

            def x2_here(b):
                dve.wait_ge(by_dve["wo"], b.nth(4, 4))

            def x3_here(b):
                dve.wait_ge(by_dve["o2"], b.nth(4, 4))

            walk(dve.Fori, {
                ("F", "mask"): mask, ("F", "hmat"): hmat_, ("F", "dn"): dn, ("F", "h0"): h0, ("F", "m"): m,
                ("F", "ln0"): norm("ln0", 0, lambda b: xs[:, b.slot], x_here),
                ("F", "ln1"): norm("ln1", 0, lambda b: rbuf[:], relu_here),
                ("F", "ln2"): norm("ln2", 0, lambda b: xs[:, b.slot], x1_here),
                ("F", "w1"): w1, ("F", "z"): z, ("F", "m2"): m2, ("F", "x1"): x1, ("F", "qk"): qk,
                ("A", "v"): v, ("A", "score"): score, ("A", "norm"): norm_, ("A", "turn"): turn, ("A", "pv"): pv,
                ("B", "wo"): wo_, ("B", "deg"): deg_, ("B", "h2"): h2, ("B", "pair_exp"): pair_exp,
                ("B", "lnb2"): norm("lnb2", 1, lambda b: xb[:], x2_here),
                ("B", "lnb3"): norm("lnb3", 1, lambda b: xb[:], x3_here),
                ("B", "o2"): o2, ("B", "agg"): agg}, note_part)

        @block.tensor
        def _(pe):
            pe.wait_ge(s_wload, 16 * 17)
            pe.wait_ge(s_const, 7)
            sources = ([[rbuf[:, h, f * P:(f + 1) * P] for h in range(HD)] for f in range(FD)]
                       + [[th[:, o, h * P:(h + 1) * P] for o in range(FD)] for h in range(HD)]
                       + [[th[:, FD + o, (1 - half) * D + f * P:(1 - half) * D + (f + 1) * P] for o in range(FD)]
                          for f in range(FD) for half in range(2)])
            for n, blocks in enumerate(sources):
                if n >= 2:
                    pe.wait_ge(s_wcopy, n - 1)
                for i, src in enumerate(blocks):
                    last = pe.transpose(bank[n % 2][:, i * P:(i + 1) * P], src, ident[:])
                last.then_inc(s_wturn, 1)
            pe.wait_ge(s_wa, 2 * FD)
            for f in range(FD):
                last = pe.matmul(bank[2][:, f * P:(f + 1) * P], ones[:], hb[:, f, 0:P], start=True, stop=True)
            last.then_inc(s_wturn, 1)
            pe.wait_ge(s_wready, 1)
            pe.wait_ge(s_wcopy, len(sources))

            state = {}

            def start_part(batches, order):
                note_part(batches, order)
                state["batches"], state["uses"] = batches, bank_uses(order)
                if "A" in batches:
                    pe.wait_ge(by_dve["qk"], batches["A"].nth(8, 8))
                if "B" in batches and batches["B"].before().exists():
                    pe.wait_ge(by_dve["agg"], batches["B"].before().nth(4, 4))
                if "B" in batches and "A" not in batches:
                    pe.wait_ge(by_dve["v"], batches["B"].nth(4, 4))

            def claim(b, stage, name, *where):
                n = state["uses"].index((stage, name) + where)
                if n >= BANKS:
                    s, before, *at_ = state["uses"][n - BANKS]
                    sems, per = freed[before]
                    if before == "zp":
                        per, k = 8, 2 * at_[0] + 2
                    else:
                        k = use_number(before, at_)
                    pe.wait_ge(sems[before], state["batches"][s].nth(per, k))
                return bank[n % BANKS][:]

            def ht(b, t):
                pe.wait_ge(hmat_done, b.nth(1, 1))
                out_ = claim(b, "F", "ht", t).bitcast(F16)
                for i in range(NT):
                    last = pe.transpose(out_[:, i * P:(i + 1) * P], hmat[:, i, t * P:(t + 1) * P], ident16[:])
                last.then_inc(ready["ht"], 1)

            def dn(b):
                pe.wait_ge(by_act["ht"], b.nth(4, 4))
                pe.wait_ge(wcol_done, b.nth(2, 2))
                out_ = claim(b, "F", "dn")
                for i in range(NT):
                    for e in range(NT):
                        last = pe.matmul(out_[:, 2 * i:2 * i + 2], htm[:, e, i * P:(i + 1) * P], wcol2[:, e, :],
                                         start=(e == 0), stop=(e == NT - 1))
                last.then_inc(ready["dn"], 1)

            def m(b, t):
                pe.wait_ge(h0_low, b.nth(1, 1))
                out_ = claim(b, "F", "m", t)
                for i in range(NT):
                    lhs = hmat[:, i, t * P:(t + 1) * P]
                    pe.matmul(out_[:, 0:D + 2], lhs, hz[:, i, 0:D + 2], start=(i == 0), stop=False)
                    last = pe.matmul(out_[:, 0:D], lhs, hz[:, i, D + 2:], start=False, stop=(i == NT - 1))
                last.then_inc(ready["m"], 1)

            def u(b, f):
                pe.wait_ge(by_dve["m"], b.nth(4, 4))
                out_ = claim(b, "F", "u", f)
                for e in range(NT):
                    for part in range(2):
                        last = pe.matmul(out_, mm[:, e, part, f * P:(f + 1) * P], htm[:, e, :],
                                         start=(e == 0 and part == 0), stop=(e == NT - 1 and part == 1))
                last.then_inc(ready["u"], 1)

            def w1(b, t):
                pe.wait_ge(by_act["u"], b.nth(2, 2))
                out_ = claim(b, "F", "w1", t)
                for f in range(FD):
                    last = pe.matmul(out_, colf[:, f, t * P:(t + 1) * P], w1t[:, f, :],
                                     start=(f == 0), stop=(f == FD - 1))
                last.then_inc(ready["w1"], 1)

            def gt(b, h):
                pe.wait_ge(g1_done, b.nth(4, 4))
                out_ = claim(b, "F", "gt", h)
                for t in range(NT):
                    last = pe.transpose(out_[:, t * P:(t + 1) * P], rbuf[:, t, h * P:(h + 1) * P], ident[:])
                last.then_inc(ready["gt"], 1)

            def z(b, t):
                pe.wait_ge(by_act["gt"], b.nth(4, 4))
                out_ = claim(b, "F", "z", t)
                for h in range(HD):
                    last = pe.matmul(out_[:, 0:D], rbuf[:, t, h * P:(h + 1) * P], w2t[:, h, :],
                                     start=(h == 0), stop=(h == HD - 1))
                last.then_inc(ready["z"], 1)

            def m2(b, t):
                pe.wait_ge(by_dve["z"], b.nth(4, 4))
                out_ = claim(b, "F", "m2", t)
                for i in range(NT):
                    lhs = hmat[:, i, t * P:(t + 1) * P]
                    pe.matmul(out_[:, 0:D], lhs, hz[:, i, 0:D], start=(i == 0), stop=False)
                    last = pe.matmul(out_[:, 0:D], lhs, hz[:, i, D + 2:], start=False, stop=(i == NT - 1))
                last.then_inc(ready["m2"], 1)

            def x1(b, t):
                pe.wait_ge(by_dve["m2"], b.nth(4, 4))
                out_ = claim(b, "F", "x1", t)
                for e in range(NT):
                    for part in range(2):
                        last = pe.matmul(out_[:, 0:D], htm[:, e, t * P:(t + 1) * P], mm[:, e, part, :],
                                         start=(e == 0 and part == 0), stop=(e == NT - 1 and part == 1))
                last.then_inc(ready["x1"], 1)

            def turned_rows(name, stage, done, source):
                def rows(b, f):
                    pe.wait_ge(done, b.nth(4, 4))
                    out_ = claim(b, stage, name, f)
                    for t in range(NT):
                        last = pe.transpose(out_[:, t * P:(t + 1) * P], source[:, t, f * P:(f + 1) * P], ident[:])
                    last.then_inc(ready[name], 1)
                return rows

            def qk(b, p, c):
                pe.wait_ge(by_act["h1t"], b.nth(2, 2))
                out_ = claim(b, "F", "qk", p, c)
                for f in range(FD):
                    last = pe.matmul(out_, wqk[:, c, f, p * P:(p + 1) * P], colf[:, f, :],
                                     start=(f == 0), stop=(f == FD - 1))
                last.then_inc(ready["qk"], 1)

            def v(b, t):
                pe.wait_ge(by_act["h1t"], b.nth(2, 2))
                out_ = claim(b, "A", "v", t)
                for f in range(FD):
                    last = pe.matmul(out_, colf[:, f, t * P:(t + 1) * P], wv[:, f, :],
                                     start=(f == 0), stop=(f == FD - 1))
                last.then_inc(ready["v"], 1)

            def score(b, g):
                h, t = g // NT, g % NT
                pe.wait_ge(stack_in[h // 2], b.nth(128, 128))
                if g >= 2:
                    pe.wait_ge(by_dve["score"], b.nth(32, g - 1))
                elif b.before().exists():
                    pe.wait_ge(by_dve["score"], b.before().nth(32, 31 + g))
                for part in range(2):
                    last = pe.matmul(psS[g % 2][:], qs[:, h, t * P:(t + 1) * P], ks[:, h, part, :],
                                     start=(part == 0), stop=(part == 1))
                last.then_inc(ready["score"], 1)

            def turn(b, g):
                pe.wait_ge(attn_done, b.nth(32, g + 1))
                if g >= 2:
                    pe.wait_ge(by_dve["turn"], b.nth(32, g - 1))
                elif b.before().exists():
                    pe.wait_ge(by_dve["turn"], b.before().nth(32, 31 + g))
                for j in range(NT):
                    last = pe.transpose(psT[g % 2][:, j * P:(j + 1) * P], sm[:, g % NT, j * P:(j + 1) * P], ident[:])
                last.then_inc(ready["turn"], 1)

            def pv(b, h):
                pe.wait_ge(by_dve["turn"], b.nth(32, NT * (h + 1)))
                if h == 0:
                    pe.wait_ge(by_dve["v"], b.nth(4, 4))
                if h >= 1:
                    pe.wait_ge(by_dve["pv"], b.nth(8, h))
                elif b.before().exists():
                    pe.wait_ge(by_dve["pv"], b.before().nth(8, 8))
                for j in range(NT):
                    for part in range(2):
                        last = pe.matmul(psO[:], vs[:, j, h].rearrange("p c d -> p (c d)"), pt[:, h % 2, part, j, :],
                                         start=(j == 0 and part == 0), stop=(j == NT - 1 and part == 1))
                last.then_inc(ready["pv"], 1)

            def wo_(b, t):
                pe.wait_ge(by_dve["pv"], b.nth(8, 8))
                out_ = claim(b, "B", "wo", t)
                for p in range(PAIRS):
                    last = pe.matmul(out_[:, 0:D], ot[:, p, t * P:(t + 1) * P], wo[:, p, :],
                                     start=(p == 0), stop=(p == PAIRS - 1))
                last.then_inc(ready["wo"], 1)

            def at(b, t):
                pe.wait_ge(adjb_in, b.nth(16, 16))
                out_ = claim(b, "B", "at", t)
                for j in range(NT):
                    last = pe.transpose(out_[:, j * P:(j + 1) * P], adjb[:, t, j * P:(j + 1) * P], ident[:])
                last.then_inc(ready["at"], 1)

            def sb_(b):
                pe.wait_ge(diag_done, b.nth(4, 4))
                out_ = claim(b, "B", "sb")
                pe.matmul(out_, ones[:], th[:, 0, :], start=True, stop=True).then_inc(ready["sb"], 1)

            def y(b, t):
                pe.wait_ge(by_act["h2t"], b.nth(2, 2))
                out_ = claim(b, "B", "y", t)
                for f in range(FD):
                    last = pe.matmul(out_[:, 0:D], hbt[:, f, t * P:(t + 1) * P], wl2[:, f, :],
                                     start=(f == 0), stop=(f == FD - 1))
                last.then_inc(ready["y"], 1)

            def o2(b, t):
                pe.wait_ge(pair_done, b.nth(4, t + 1))
                pe.wait_ge(by_act["y"], b.nth(4, 4))
                out_ = claim(b, "B", "o2", t)
                for j in range(NT):
                    last = pe.matmul(out_[:, 0:D + 1], th[:, t, j * P:(j + 1) * P], yz[:, j, 0:D + 1],
                                     start=(j == 0), stop=(j == NT - 1))
                last.then_inc(ready["o2"], 1)

            def zp(b, t):
                pe.wait_ge(by_act["h3t"], b.nth(2, 2))
                out_ = claim(b, "B", "zp", t)
                for f in range(FD):
                    last = pe.matmul(out_, hbt[:, f, t * P:(t + 1) * P], w3t[:, f, :],
                                     start=(f == 0), stop=(f == FD - 1))
                last.then_inc(ready["zp"], 1)

            def agg(b, t):
                pe.wait_ge(by_act["zp"], b.nth(8, 8))
                out_ = claim(b, "B", "agg", t)
                for j in range(NT):
                    last = pe.matmul(out_[:, 0:D], adjb[:, t, j * P:(j + 1) * P], yz[:, j, 0:D],
                                     start=(j == 0), stop=(j == NT - 1))
                last.then_inc(ready["agg"], 1)

            walk(pe.Fori, {
                ("F", "ht"): ht, ("F", "dn"): dn, ("F", "m"): m, ("F", "u"): u, ("F", "w1"): w1, ("F", "gt"): gt,
                ("F", "z"): z, ("F", "m2"): m2, ("F", "x1"): x1, ("F", "h1t"): turned_rows("h1t", "F", h1_done, hrow),
                ("F", "qk"): qk, ("A", "v"): v, ("A", "score"): score, ("A", "turn"): turn, ("A", "pv"): pv,
                ("B", "wo"): wo_, ("B", "at"): at, ("B", "sb"): sb_,
                ("B", "h2t"): turned_rows("h2t", "B", h2_done, hb), ("B", "y"): y, ("B", "o2"): o2,
                ("B", "h3t"): turned_rows("h3t", "B", h3_done, hb), ("B", "zp"): zp, ("B", "agg"): agg}, start_part)


_INS = ["x", "adj", "nodemask", "L0_gnn_W1", "L0_gnn_b1", "L0_gnn_gamma", "L0_gnn_beta", "L0_gnn_W2",
        "L0_gnn_b2", "L1_gnn_W_qkv", "L1_gnn_W_out", "L1_gnn_b_out", "L2_gnn_w", "L2_gnn_a", "L3_gnn_W"]
_OUTS = [((BATCHES, NODES, D), "float32")]


def kernel(**inputs):
    import numpy as _np
    import concourse.bacc as _bacc
    from concourse import mybir as _mybir
    from concourse.bass_utils import run_bass_kernel_spmd as _run

    nc = _bacc.Bacc("TRN2", target_bir_lowering=False, num_devices=1)
    arrays, args = {}, []
    for name in _INS:
        a = _np.ascontiguousarray(inputs[name])
        if a.dtype == _np.bool_:
            a = a.view(_np.uint8)
        arrays[f"in_{name}_dram"] = a
        args.append(nc.dram_tensor(f"in_{name}_dram", a.shape, _mybir.dt.from_np(a.dtype), kind="ExternalInput").ap())
    for i, (shape, dtype) in enumerate(_OUTS):
        dt = _mybir.dt.from_np(_np.dtype(dtype))
        args.append(nc.dram_tensor(f"out_{i}_dram", shape, dt, kind="ExternalOutput").ap())
    gnn_kernel(nc, *args)
    r = _run(nc, [arrays], core_ids=[0])
    got = tuple(r.results[0][f"out_{i}_dram"] for i in range(len(_OUTS)))
    return got[0]
```

```python
from contextlib import ExitStack

import concourse.bass as bass
from concourse import mybir

F32 = mybir.dt.float32
F16 = mybir.dt.float16
U8 = mybir.dt.uint8
ALU = mybir.AluOpType
ACT = mybir.ActivationFunctionType
AX_X = mybir.AxisListType.X

P = 128
BATCHES = 16
NODES = 512
NT = NODES // P
D = 256
FD = D // P
DH = 512
HD = DH // P
HEADS = 8
DIM_HEAD = 64
PAIRS = HEADS // 2
EPS_LN = 1e-5
EPS_DEG = 1e-6
MIX = 0.33
TANH_RANGE = 8.0
LEAK = 0.1
MASKED = 1e30
TINY = 1.2e-38
BANKS = 3




def tiles(name, count, behind=None):
    tasks = []
    for t in range(count):
        tasks.append((name, t))
        if behind and t:
            tasks.append((behind, t - 1))
    return tasks + ([(behind, count - 1)] if behind else [])


STREAMS = {
    "L": ("F", [("load_adj",), ("load_x",)]),
    "G": ("F", [("mask",)] + tiles("gexp", NT)),
    "F": ("F", [("hmat",), ("ln0",)] + tiles("ht", NT) + [("h0",), ("dn",), ("h0_high",)]
          + tiles("m", NT, "m_low") + tiles("u", FD) + tiles("w1", NT, "ln1_stats") + [("ln1",), ("ln1_apply",)]
          + tiles("gt", HD) + tiles("z", NT) + tiles("m2", NT) + tiles("x1", NT, "ln2_stats")
          + [("ln2",), ("h1",)] + tiles("h1t", FD)
          + [task for p in range(PAIRS) for task in (("qk", p, 0), ("qk", p, 1), ("stack", p))]),
    "V": ("A", tiles("v", NT)),
    "S": ("A", tiles("score", HEADS * NT)),
    "N": ("A", tiles("norm", HEADS * NT)),
    "T": ("A", tiles("turn", HEADS * NT)),
    "O": ("A", tiles("pv", HEADS)),
    "J": ("B", [("load_adj",)] + tiles("at", NT)),
    "B": ("B", tiles("wo", NT, "lnb2_stats") + [("deg",), ("lnb2",), ("h2",), ("sj",), ("sb",)]
          + tiles("leaky", NT) + tiles("h2t", FD) + tiles("y", NT) + tiles("pair_exp", NT)
          + tiles("o2", NT, "lnb3_stats") + [("lnb3",), ("h3",)] + tiles("h3t", FD) + tiles("zp", NT)
          + tiles("agg", NT) + [("store",)]),
}

ORDER = {
    "pe": ("SSBBBBVFFTTSSFFJJFJJVVVSBFTFSTFSFSBBOFFSBTTSTBFFFFTSTSBTBOSSBSFFFSFTTBFFFFTTSSFFFFSTSFFFFT"
           "SOBSBFFTTOFFFTTSSFSTTSFSSOTFSFFTTBSBSTOBSBTTBBTTOTTBBOBB"),
    "dve": ("SSBNNBBBBFBGBVBTBBFTFBSFSVVSNVFNFSFFFTFFTFSSBBBBONNNTTSSTNFNFFNFFFFTFFTTSSSSBNNSSTBTBFNNFO"
           "FNNFTTSFFSFFSTFFFFFFFFFTSONBBNBBBBSTTSONNFNFNTTSSFSSTFTNFSTOFNNNFSSTTFTSONNNNSTSTNNTTOTTBB"
           "OBB"),
    "sp": ("LJLFFFFB"),
    "act": ("SSVFFTTFFJJJJBFVSVSGGVSBFFTTFGSFBBSGSOBTTFFTSSBFFFTFTBTBBBFSSFFFFTSSTSFSBFOBFFTTFFSFFSTSTO"
           "SFFFTTSOBFSFFTTSTTSFSSFOTSFFFTTSSBTBOSBBTTSBSBTTOTTO"),
    "pool": ("BFFGGGGFBBBBFFB"),
}

BANK_USES = {"ht", "dn", "m", "u", "w1", "gt", "z", "m2", "x1", "h1t", "qk", "v",
             "wo", "at", "sb", "h2t", "y", "o2", "h3t", "zp", "agg"}
PRODUCTS = BANK_USES | {"score", "turn", "pv"}


class Batch:

    def __init__(self, turn, offset):
        self.turn, self.offset = turn, offset

    def exists(self):
        return not isinstance(self.turn, int) or 2 * self.turn + self.offset >= 0

    def before(self, n=1):
        return Batch(self.turn, self.offset - n)

    @property
    def index(self):
        return self.turn * 2 + self.offset

    @property
    def slot(self):
        return self.offset % 2

    def nth(self, per, k):
        return self.turn * (2 * per) + (self.offset * per + k)


def parts(fori):
    yield {"F": Batch(0, 0)}
    yield {"F": Batch(0, 1), "A": Batch(0, 0)}
    with fori(0, (BATCHES - 2) // 2) as turn:
        for k in (1, 2):
            yield {"F": Batch(turn, k + 1), "A": Batch(turn, k), "B": Batch(turn, k - 1)}
    yield {"A": Batch(0, BATCHES - 1), "B": Batch(0, BATCHES - 2)}
    yield {"B": Batch(0, BATCHES - 1)}


def tasks_of(engine, names, batches):
    left = {letter: [(stage,) + task for task in tasks if (stage, task[0]) in names]
            for letter, (stage, tasks) in STREAMS.items()}
    tasks = [left[letter].pop(0) for letter in ORDER[engine]]
    return [task for task in tasks if task[0] in batches]


def walk(engine, fori, handlers, start_part=None):
    for batches in parts(fori):
        if start_part:
            start_part(batches)
        for stage, name, *where in tasks_of(engine, handlers, batches):
            handlers[stage, name](batches[stage], *where)


def gnn_kernel(nc, x, adj, nodemask, W1, b1, gamma, beta, W2, b2, Wqkv, Wout, bout, w, a, W3, out):
    with ExitStack() as ctx:
        def sb(name, shape, dt=F32):
            return ctx.enter_context(nc.sbuf_tensor(name, shape, dt))

        def sem(name):
            return ctx.enter_context(nc.semaphore(name))

        ident = sb("ident", [P, P])
        ident16 = sb("ident16", [P, P], F16)
        ones = sb("ones", [P, P])
        half_power = sb("half_power", [P, NT])
        eps_tile = sb("eps_tile", [P, NT])
        minus_one = sb("minus_one", [P, NT])
        w1t = sb("w1t", [P, FD, DH])
        w2t = sb("w2t", [P, HD, D])
        wqk = sb("wqk", [P, 2, FD, DH])
        wv = sb("wv", [P, FD, DH])
        wo = sb("wo", [P, PAIRS, D])
        wl2 = sb("wl2", [P, FD, D])
        w3t = sb("w3t", [P, FD, 2 * D])
        b1row = sb("b1row", [P, DH])
        b2row = sb("b2row", [P, D])
        boutrow = sb("boutrow", [P, D])
        warow = sb("warow", [P, D])
        gcol = sb("gcol", [P, HD])
        bcol = sb("bcol", [P, HD])
        wacol = sb("wacol", [P, FD])

        adjf = sb("adjf", [P, 2, NT, NODES])
        hmat = sb("hmat", [P, NT, NODES], F16)
        htm = sb("htm", [P, NT, NODES], F16)
        SPLIT = 2 * D + 2
        hz = sb("hz", [P, NT, SPLIT], F16)
        mm = sb("mm", [P, NT, 2, D], F16)
        colf = sb("colf", [P, FD, NODES])
        rbuf = sb("rbuf", [P, NT, DH])
        xs = sb("xs", [P, 2, NT, D])
        hrow = sb("hrow", [P, NT, D])
        nat = sb("nat", [P, 2, 4, NODES], F16)
        mrow8 = sb("mrow8", [P, NODES], U8)
        mcol8 = sb("mcol8", [P, NT], U8)
        mrow = sb("mrow", [P, NODES])
        mcol = sb("mcol", [P, NT])
        wcol = sb("wcol", [P, NT])
        wcol2 = sb("wcol2", [P, NT, 2], F16)
        dsum = sb("dsum", [P, NT])
        dpos = sb("dpos", [P, NT])
        dinv = sb("dinv", [P, NT])
        binv = sb("binv", [P, NT])
        qs = sb("qs", [P, HEADS, NODES], F16)
        ks = sb("ks", [P, HEADS, 2, NODES], F16)
        vs = sb("vs", [P, NT, HEADS, 2, DIM_HEAD], F16)
        mbias = sb("mbias", [P, 2, NODES])
        escale = sb("escale", [P, 2, NT])
        sm = sb("sm", [P, NT, NODES])
        smax = sb("smax", [P, NT])
        nbias = sb("nbias", [P, NT])
        esum = sb("esum", [P, NT])
        einv = sb("einv", [P, NT])
        pt = sb("pt", [P, 2, 2, NT, NODES], F16)
        otmp = sb("otmp", [DIM_HEAD, NODES])
        ot = sb("ot", [P, PAIRS, NODES])
        adjb = sb("adjb", [P, NT, NODES])
        th = sb("th", [P, NT, NODES])
        xb = sb("xb", [P, NT, D])
        hb = sb("hb", [P, NT, D])
        hbt = sb("hbt", [P, FD, NODES])
        yz = sb("yz", [P, NT, D + 1])
        deg = sb("deg", [P, NT])
        rdeg = sb("rdeg", [P, NT])
        sj = sb("sj", [P, NT])
        sj8 = sb("sj8", [P, NT])
        rden = sb("rden", [P, NT])
        stats = sb("stats", [P, 2, NT, 6])
        moments = sb("moments", [P, 2, NT, 2])
        vpe = sb("vpe", [P, 2, NT])
        rstd = sb("rstd", [P, 2, NT])
        nmr = sb("nmr", [P, 2, NT])

        bank = [ctx.enter_context(nc.psum_tensor(f"bank{i}", [P, 512], F32)) for i in range(BANKS)]
        psS = [ctx.enter_context(nc.psum_tensor(f"psS{i}", [P, 512], F32)) for i in range(2)]
        psT = [ctx.enter_context(nc.psum_tensor(f"psT{i}", [P, 512], F32)) for i in range(2)]
        psO = ctx.enter_context(nc.psum_tensor("psO", [P, 512], F32))

        s_const = sem("s_const")
        s_wload = sem("s_wload")
        s_ones = sem("s_ones")
        s_wready = sem("s_wready")
        s_wturn = sem("s_wturn")
        s_wcopy = sem("s_wcopy")
        s_wa = sem("s_wa")
        adj_in = sem("adj_in")
        x_in = sem("x_in")
        mask_in = sem("mask_in")
        adjb_in = sem("adjb_in")
        stack_in = [sem(f"stack_in{p}") for p in range(PAIRS)]
        out_stored = sem("out_stored")
        ready = {n: sem(f"{n}_ready") for n in sorted(PRODUCTS)}
        by_act = {n: sem(f"{n}_act") for n in ("ht", "m", "u", "gt", "z", "m2", "h1t", "qk", "v",
                                              "turn", "pv", "at", "sb", "h2t", "y", "h3t", "zp")}
        by_dve = {n: sem(f"{n}_dve") for n in ("dn", "m", "w1", "z", "m2", "x1", "qk", "v", "score",
                                              "turn", "pv", "wo", "o2", "agg")}
        mask_done = sem("mask_done")
        hmat_done = sem("hmat_done")
        wcol_done = sem("wcol_done")
        binv_done = sem("binv_done")
        dn_step = sem("dn_step")
        relu_done = sem("relu_done")
        h0_done = sem("h0_done")
        h0_high = sem("h0_high")
        h0_low = sem("h0_low")
        xh_done = sem("xh_done")
        g1_done = sem("g1_done")
        h1_done = sem("h1_done")
        xbias_done = sem("xbias_done")
        LNS = ("ln0", "ln1", "ln2", "lnb2", "lnb3")
        ln_stats = {n: sem(f"{n}_stats") for n in LNS}
        ln_moments = {n: sem(f"{n}_moments") for n in LNS}
        ln_scale = {n: sem(f"{n}_scale") for n in LNS}
        gexp_done = sem("gexp_done")
        gadd_done = sem("gadd_done")
        shared_done = sem("shared_done")
        nbias_done = sem("nbias_done")
        exp_done = sem("exp_done")
        einv_done = sem("einv_done")
        attn_done = sem("attn_done")
        deg_step = sem("deg_step")
        h2_done = sem("h2_done")
        sj_done = sem("sj_done")
        diag_done = sem("diag_done")
        leaky_done = sem("leaky_done")
        pexp_done = sem("pexp_done")
        pair_done = sem("pair_done")
        rden_done = sem("rden_done")
        h3_done = sem("h3_done")
        sum_done = sem("sum_done")

        freed = {"ht": (by_act, 4), "dn": (by_dve, 1), "m": (by_dve, 4), "u": (by_act, 2),
                 "w1": (by_dve, 4), "gt": (by_act, 4), "z": (by_dve, 4), "m2": (by_dve, 4),
                 "x1": (by_dve, 4), "h1t": (by_act, 2), "qk": (by_dve, 8), "v": (by_dve, 4),
                 "wo": (by_dve, 4), "at": (by_act, 4), "sb": (by_act, 4), "h2t": (by_act, 2),
                 "y": (by_act, 4), "o2": (by_dve, 4), "h3t": (by_act, 2), "zp": (by_act, 4),
                 "agg": (by_dve, 4)}

        def use_number(name, where):
            if name == "qk":
                return 2 * where[0] + where[1] + 1
            if name == "sb":
                return 4
            return (where[0] if where else 0) + 1

        sp_went = sem("sp_went")
        dve_went = sem("dve_went")

        current = {}

        def note_part(batches):
            names = {(stage, task[0]) for stage, tasks in STREAMS.values() for task in tasks if task[0] in PRODUCTS}
            current["uses"] = [task for task in tasks_of("pe", names, batches) if task[1] in BANK_USES]

        def bank_of(b, name, *where):
            n = [task[1:] for task in current["uses"]].index((name,) + where)
            return bank[n % BANKS][:]

        block = ctx.enter_context(nc.Block())

        @block.sync
        def _(sp):
            sp.dma_start(rbuf[:, 0:HD, 0:D], W1.rearrange("(t p) d -> p t d", p=P)).then_inc(s_wload, 16)
            sp.dma_start(th[:, 0:FD, :], W2.rearrange("(t p) h -> p t h", p=P)).then_inc(s_wload, 16)
            sp.dma_start(th[:, FD:2 * FD, :], W3.rearrange("(t p) f -> p t f", p=P)).then_inc(s_wload, 16)
            sp.dma_start(wl2[:], w.rearrange("(t p) d -> p t d", p=P)).then_inc(s_wload, 16)
            sp.dma_start(warow[:], a.partition_broadcast(P)).then_inc(s_wload, 16)
            sp.dma_start(gcol[:], gamma.rearrange("(t p) -> p t", p=P), allow_slow_non_contiguous=True).then_inc(s_wload, 16)
            sp.dma_start(bcol[:], beta.rearrange("(t p) -> p t", p=P), allow_slow_non_contiguous=True).then_inc(s_wload, 16)
            sp.dma_start(b1row[:], b1.partition_broadcast(P)).then_inc(s_wload, 16)
            sp.dma_start(b2row[:], b2.partition_broadcast(P)).then_inc(s_wload, 16)
            sp.dma_start(boutrow[:], bout.partition_broadcast(P)).then_inc(s_wload, 16)
            qkv = Wqkv.rearrange("(t p) (h c d) -> p c t h d", p=P, h=HEADS, c=3)
            for t in range(FD):
                for c in range(2):
                    sp.dma_start(wqk[:, c, t, :].rearrange("p (h d) -> p h d", h=HEADS),
                                 qkv[:, c, t]).then_inc(s_wload, 16)
                sp.dma_start(wv[:, t, :].rearrange("p (h d) -> p h d", h=HEADS),
                             qkv[:, 2, t]).then_inc(s_wload, 16)
            sp.dma_start(wo[:], Wout.rearrange("(t p) d -> p t d", p=P)).then_inc(s_wload, 16)

            def load_adj(b):
                if b.before(2).exists():
                    sp.wait_ge(attn_done, b.before(2).nth(32, 32))
                    sp.sem_inc(sp_went, 1)
                    sp.wait_ge(wcol_done, b.before(1).nth(2, 2))
                    sp.sem_inc(sp_went, 1)
                    sp.wait_ge(shared_done, b.before(1).nth(4, 4))
                    sp.sem_inc(sp_went, 1)
                elif b.before(1).exists():
                    sp.wait_ge(wcol_done, b.before(1).nth(2, 2))
                    sp.sem_inc(sp_went, 1)
                    sp.wait_ge(shared_done, b.before(1).nth(4, 4))
                    sp.sem_inc(sp_went, 1)
                sp.dma_start(adjf[:, b.slot], adj[b.index].rearrange("(t p) c -> p t c", p=P)).then_inc(adj_in, 16)
                sp.dma_start(wcol[:], adj[b.index, 0, :].rearrange("(t p) -> p t", p=P),
                             allow_slow_non_contiguous=True).then_inc(adj_in, 16)
                sp.dma_start(mcol8[:], nodemask[b.index].rearrange("(t p) -> p t", p=P),
                             allow_slow_non_contiguous=True).then_inc(mask_in, 16)
                sp.dma_start(mrow8[:], nodemask[b.index].partition_broadcast(P)).then_inc(mask_in, 16)

            def load_x(b):
                if b.before(2).exists():
                    sp.wait_ge(by_dve["wo"], b.before(2).nth(4, 4))
                    sp.sem_inc(sp_went, 1)
                sp.dma_start(xs[:, b.slot], x[b.index].rearrange("(t p) d -> p t d", p=P)).then_inc(x_in, 16)

            def stack(b, p):
                sp.wait_ge(by_act["qk"], b.nth(8, 2 * p + 2))
                sp.sem_inc(sp_went, 1)
                sp.wait_ge(by_dve["qk"], b.nth(8, 2 * p + 2))
                sp.sem_inc(sp_went, 1)
                if b.before().exists():
                    sp.wait_ge(ready["score"], b.before().nth(32, 8 * p + 8))
                    sp.sem_inc(sp_went, 1)
                for e in range(2):
                    rows = slice(e * DIM_HEAD, (e + 1) * DIM_HEAD)
                    h = 2 * p + e
                    for part in range(2):
                        to = slice(part * DIM_HEAD, (part + 1) * DIM_HEAD)
                        sp.dma_start(qs[to, h, :], nat[rows, p % 2, part, :]).then_inc(stack_in[p], 16)
                        sp.dma_start(ks[to, h, :, :], nat[rows, p % 2, 2:4, :]).then_inc(stack_in[p], 16)

            def load_adjb(b):
                if b.before().exists():
                    sp.wait_ge(ready["agg"], b.before().nth(4, 4))
                    sp.sem_inc(sp_went, 1)
                sp.dma_start(adjb[:], adj[b.index].rearrange("(t p) c -> p t c", p=P)).then_inc(adjb_in, 16)

            def store(b):
                sp.wait_ge(by_dve["agg"], b.nth(4, 4))
                sp.sem_inc(sp_went, 1)
                sp.wait_ge(sum_done, b.nth(4, 4))
                sp.sem_inc(sp_went, 1)
                sp.dma_start(out[b.index].rearrange("(t p) d -> p t d", p=P), hb[:]).then_inc(out_stored, 16)

            walk("sp", sp.Fori, {("F", "load_adj"): load_adj, ("F", "load_x"): load_x, ("F", "stack"): stack,
                           ("B", "load_adj"): load_adjb, ("B", "store"): store})
            sp.wait_ge(out_stored, 16 * BATCHES)

        @block.gpsimd
        def _(pool):
            pool.memset(ones[:], 1.0).then_inc(s_ones, 1)
            pool.memset(half_power[:], -0.5).then_inc(s_const, 1)
            pool.memset(eps_tile[:], EPS_LN).then_inc(s_const, 1)
            pool.memset(minus_one[:], -1.0).then_inc(s_const, 1)
            pool.memset(hz[:, :, D:D + 2], 1.0).then_inc(s_const, 1)
            pool.memset(yz[:, :, D:D + 1], 1.0).then_inc(s_const, 1)
            pool.wait_ge(s_ones, 1)
            pool.affine_select(out=ident[:], in_=ones[:], compare_op=ALU.is_equal, fill=0.0, base=0,
                               pattern=[[-1, P]], channel_multiplier=1).then_inc(s_const, 1)
            pool.wait_ge(s_const, 6)
            pool.tensor_copy(ident16[:], ident[:]).then_inc(s_const, 1)

            def ln_scales(name, chain):
                def scales(b):
                    pool.wait_ge(ln_moments[name], b.nth(4, 4))
                    pool.tensor_tensor(vpe[:, chain], moments[:, chain, :, 1], eps_tile[:],
                                       ALU.add).then_inc(ln_scale[name], 1)
                    pool.wait_ge(ln_scale[name], b.nth(4, 1))
                    pool.tensor_tensor(rstd[:, chain], vpe[:, chain], half_power[:],
                                       ALU.pow).then_inc(ln_scale[name], 1)
                    pool.wait_ge(ln_scale[name], b.nth(4, 2))
                    pool.tensor_tensor(vpe[:, chain], moments[:, chain, :, 0], rstd[:, chain],
                                       ALU.mult).then_inc(ln_scale[name], 1)
                    pool.wait_ge(ln_scale[name], b.nth(4, 3))
                    pool.tensor_tensor(nmr[:, chain], vpe[:, chain], minus_one[:],
                                       ALU.mult).then_inc(ln_scale[name], 1)
                return scales

            def h0(b):
                pool.wait_ge(h0_high, b.nth(1, 1))
                pool.tensor_tensor(hz[:, :, D + 2:], hrow[:], hz[:, :, 0:D], ALU.subtract).then_inc(h0_low, 1)
                pool.tensor_tensor(xs[:, b.slot], xs[:, b.slot], hrow[:], ALU.add).then_inc(xh_done, 1)
                pool.wait_ge(xh_done, b.nth(2, 1))
                pool.tensor_tensor(xs[:, b.slot], xs[:, b.slot],
                                   b2row[:].unsqueeze(1).to_broadcast([P, NT, D]), ALU.add).then_inc(xh_done, 1)

            def gexp(b, t):
                tile = adjf[:, b.slot, t, :]
                pool.wait_ge(gexp_done, b.nth(4, t + 1))
                pool.wait_ge(hmat_done, b.nth(1, 1))
                pool.tensor_tensor(tile, tile, colf[:, t % 2, :], ALU.add).then_inc(gadd_done, 1)
                pool.wait_ge(gadd_done, b.nth(8, 2 * t + 1))
                pool.wait_ge(mask_done, b.nth(4, 4))
                pool.tensor_tensor(tile, tile, mrow[:], ALU.mult).then_inc(gadd_done, 1)
                pool.wait_ge(gadd_done, b.nth(8, 2 * t + 2))
                pool.tensor_tensor(tile, tile, mcol[:, t:t + 1].to_broadcast([P, NODES]),
                                   ALU.mult).then_inc(shared_done, 1)

            def h1(b):
                pool.wait_ge(h1_done, b.nth(4, 4))
                pool.tensor_tensor(xs[:, b.slot], xs[:, b.slot],
                                   boutrow[:].unsqueeze(1).to_broadcast([P, NT, D]), ALU.add).then_inc(xbias_done, 1)

            def pair_exp(b, t):
                pool.wait_ge(pexp_done, b.nth(4, t + 1))
                pool.wait_ge(by_act["at"], b.nth(4, t + 1))
                pool.tensor_tensor(th[:, t, :], th[:, t, :], adjb[:, t, :], ALU.mult).then_inc(pair_done, 1)

            walk("pool", pool.Fori, {("F", "ln0"): ln_scales("ln0", 0), ("F", "h0_high"): h0, ("F", "gexp"): gexp,
                             ("F", "ln1"): ln_scales("ln1", 0), ("F", "ln2"): ln_scales("ln2", 0),
                             ("F", "h1"): h1, ("B", "lnb2"): ln_scales("lnb2", 1),
                             ("B", "pair_exp"): pair_exp, ("B", "lnb3"): ln_scales("lnb3", 1)})

        @block.scalar
        def _(act):
            weight_tiles = ([w1t[:, f, :] for f in range(FD)]
                            + [w2t[:, h, :] for h in range(HD)]
                            + [w3t[:, f, half * D:(half + 1) * D] for f in range(FD) for half in range(2)])
            for n, tile in enumerate(weight_tiles):
                act.wait_ge(s_wturn, n + 1)
                width = tile.shape[-1]
                act.activation(tile, bank[n % 2][:, 0:width], ACT.Copy).then_inc(s_wcopy, 1)

            def ht(b, t):
                act.wait_ge(ready["ht"], b.nth(4, t + 1))
                act.activation(htm[:, t, :], bank_of(b, "ht", t).bitcast(F16)[:, 0:NODES], ACT.Copy)\
                    .then_inc(by_act["ht"], 1)

            def h0(b):
                act.wait_ge(ln_scale["ln0"], b.nth(4, 4))
                act.wait_ge(x_in, b.nth(16, 16))
                for t in range(NT):
                    act.activation(hrow[:, t, :], xs[:, b.slot, t, :], ACT.Relu, bias=nmr[:, 0, t:t + 1],
                                   scale=rstd[:, 0, t:t + 1]).then_inc(h0_done, 1)

            def gexp(b, t):
                act.wait_ge(adj_in, b.nth(32, 32))
                if t == 0 and b.before().exists():
                    act.wait_ge(ready["v"], b.before().nth(4, 4))
                if t >= 2:
                    act.wait_ge(gadd_done, b.nth(8, 2 * (t - 2) + 1))
                act.activation(colf[:, t % 2, :], adjf[:, b.slot, t, :], ACT.Exp, scale=-1.0).then_inc(gexp_done, 1)

            def m(b, t):
                act.wait_ge(binv_done, b.nth(8, 2 * t + 2))
                act.activation(mm[:, t, 0, :], bank_of(b, "m", t)[:, 0:D], ACT.Copy,
                               scale=binv[:, t:t + 1]).then_inc(by_act["m"], 1)

            def u(b, f):
                act.wait_ge(ready["u"], b.nth(2, f + 1))
                act.wait_ge(gadd_done, b.nth(8, 7))
                act.activation(colf[:, f, :], bank_of(b, "u", f), ACT.Copy).then_inc(by_act["u"], 1)

            def w1(b, t):
                act.wait_ge(by_dve["w1"], b.nth(4, t + 1))
                act.activation(rbuf[:, t, :], rbuf[:, t, :], ACT.Relu).then_inc(relu_done, 1)

            def ln1_apply(b):
                act.wait_ge(ln_scale["ln1"], b.nth(4, 4))
                for t in range(NT):
                    act.activation(rbuf[:, t, :], rbuf[:, t, :], ACT.Identity, bias=nmr[:, 0, t:t + 1],
                                   scale=rstd[:, 0, t:t + 1]).then_inc(g1_done, 1)

            def gt(b, h):
                act.wait_ge(ready["gt"], b.nth(4, h + 1))
                act.activation(rbuf[:, :, h * P:(h + 1) * P],
                               bank_of(b, "gt", h).rearrange("p (t n) -> p t n", t=NT), ACT.Identity,
                               bias=bcol[:, h:h + 1], scale=gcol[:, h:h + 1]).then_inc(by_act["gt"], 1)

            def z(b, t):
                act.wait_ge(ready["z"], b.nth(4, t + 1))
                act.activation(hz[:, t, 0:D], bank_of(b, "z", t)[:, 0:D], ACT.Copy).then_inc(by_act["z"], 1)

            def m2(b, t):
                act.wait_ge(ready["m2"], b.nth(4, t + 1))
                act.activation(mm[:, t, 0, :], bank_of(b, "m2", t)[:, 0:D], ACT.Copy,
                               scale=binv[:, t:t + 1]).then_inc(by_act["m2"], 1)

            def h1(b):
                act.wait_ge(ln_scale["ln2"], b.nth(4, 4))
                for t in range(NT):
                    act.activation(hrow[:, t, :], xs[:, b.slot, t, :], ACT.Relu, bias=nmr[:, 0, t:t + 1],
                                   scale=rstd[:, 0, t:t + 1]).then_inc(h1_done, 1)

            def h1t(b, f):
                act.wait_ge(ready["h1t"], b.nth(2, f + 1))
                act.activation(colf[:, f, :], bank_of(b, "h1t", f), ACT.Copy).then_inc(by_act["h1t"], 1)

            def qk(b, p, c):
                act.wait_ge(ready["qk"], b.nth(8, 2 * p + c + 1))
                if p >= 2:
                    act.wait_ge(stack_in[p - 2], b.nth(128, 128))
                elif b.before().exists():
                    act.wait_ge(stack_in[p + 2], b.before().nth(128, 128))
                act.activation(nat[:, p % 2, 2 * c, :], bank_of(b, "qk", p, c), ACT.Copy).then_inc(by_act["qk"], 1)

            def v(b, t):
                act.wait_ge(ready["v"], b.nth(4, t + 1))
                act.activation(vs[:, t, :, 0, :], bank_of(b, "v", t).rearrange("p (h d) -> p h d", h=HEADS),
                               ACT.Copy).then_inc(by_act["v"], 1)

            def score(b, g):
                act.wait_ge(nbias_done, b.nth(32, g + 1))
                if g >= NT:
                    act.wait_ge(attn_done, b.nth(32, g - NT + 1))
                elif b.before().exists():
                    act.wait_ge(attn_done, b.before().nth(32, 32 - NT + g + 1))
                act.activation(sm[:, g % NT, :], sm[:, g % NT, :], ACT.Exp, bias=nbias[:, g % NT:g % NT + 1],
                               scale=escale[:, b.slot, g % NT:g % NT + 1],
                               accum_out=esum[:, g % NT:g % NT + 1]).then_inc(exp_done, 1)

            def turn(b, g):
                act.wait_ge(ready["turn"], b.nth(32, g + 1))
                h, t = g // NT, g % NT
                if h >= 2:
                    act.wait_ge(ready["pv"], b.nth(8, h - 1))
                act.activation(pt[:, h % 2, 0, :, t * P:(t + 1) * P],
                               psT[g % 2][:].rearrange("p (j n) -> p j n", j=NT), ACT.Copy).then_inc(by_act["turn"], 1)

            def pv(b, h):
                act.wait_ge(ready["pv"], b.nth(8, h + 1))
                if h >= 1:
                    act.wait_ge(by_dve["pv"], b.nth(8, h))
                elif b.before().exists():
                    act.wait_ge(by_dve["pv"], b.before().nth(8, 8))
                act.activation(otmp[:], psO[DIM_HEAD:P, :], ACT.Copy).then_inc(by_act["pv"], 1)

            def at(b, t):
                act.wait_ge(ready["at"], b.nth(4, t + 1))
                act.wait_ge(deg_step, b.nth(3, 1))
                act.activation(adjb[:, t, :], bank_of(b, "at", t), ACT.Copy).then_inc(by_act["at"], 1)

            def h2(b):
                act.wait_ge(ln_scale["lnb2"], b.nth(4, 4))
                if b.before().exists():
                    act.wait_ge(out_stored, b.before().nth(16, 16))
                for t in range(NT):
                    act.activation(hb[:, t, :], xb[:, t, :], ACT.Relu, bias=nmr[:, 1, t:t + 1],
                                   scale=rstd[:, 1, t:t + 1]).then_inc(h2_done, 1)

            def sb_(b):
                act.wait_ge(ready["sb"], b.nth(1, 1))
                for j in range(NT):
                    act.activation(th[:, :, j * P:(j + 1) * P],
                                   bank_of(b, "sb").rearrange("p (t n) -> p t n", t=NT), ACT.Tanh,
                                   bias=sj8[:, j:j + 1], scale=1.0 / TANH_RANGE).then_inc(by_act["sb"], 1)

            def h2t(b, f):
                act.wait_ge(ready["h2t"], b.nth(2, f + 1))
                act.activation(hbt[:, f, :], bank_of(b, "h2t", f), ACT.Copy).then_inc(by_act["h2t"], 1)

            def y(b, t):
                act.wait_ge(ready["y"], b.nth(4, t + 1))
                if b.before().exists():
                    act.wait_ge(by_dve["agg"], b.before().nth(4, 4))
                act.activation(yz[:, t, 0:D], bank_of(b, "y", t)[:, 0:D], ACT.Copy).then_inc(by_act["y"], 1)

            def pair_exp(b, t):
                act.wait_ge(leaky_done, b.nth(4, t + 1))
                act.activation(th[:, t, :], th[:, t, :], ACT.Exp, scale=TANH_RANGE).then_inc(pexp_done, 1)

            def h3(b):
                act.wait_ge(ln_scale["lnb3"], b.nth(4, 4))
                act.wait_ge(sj_done, b.nth(5, 4))
                for t in range(NT):
                    act.activation(hb[:, t, :], xb[:, t, :], ACT.Relu, bias=nmr[:, 1, t:t + 1],
                                   scale=rstd[:, 1, t:t + 1]).then_inc(h3_done, 1)

            def h3t(b, f):
                act.wait_ge(ready["h3t"], b.nth(2, f + 1))
                act.activation(hbt[:, f, :], bank_of(b, "h3t", f), ACT.Copy).then_inc(by_act["h3t"], 1)

            def zp(b, t):
                act.wait_ge(ready["zp"], b.nth(4, t + 1))
                act.activation(yz[:, t, 0:D], bank_of(b, "zp", t)[:, 0:D], ACT.Copy).then_inc(by_act["zp"], 1)
                act.activation(hb[:, t, :], bank_of(b, "zp", t)[:, D:], ACT.Copy).then_inc(by_act["zp"], 1)

            walk("act", act.Fori, {
                ("F", "ht"): ht, ("F", "h0"): h0, ("F", "gexp"): gexp, ("F", "m"): m, ("F", "u"): u,
                ("F", "w1"): w1, ("F", "ln1_apply"): ln1_apply, ("F", "gt"): gt, ("F", "z"): z, ("F", "m2"): m2,
                ("F", "h1"): h1, ("F", "h1t"): h1t, ("F", "qk"): qk, ("A", "v"): v, ("A", "score"): score,
                ("A", "turn"): turn, ("A", "pv"): pv, ("B", "at"): at, ("B", "h2"): h2, ("B", "sb"): sb_,
                ("B", "h2t"): h2t, ("B", "y"): y, ("B", "pair_exp"): pair_exp, ("B", "h3"): h3,
                ("B", "h3t"): h3t, ("B", "zp"): zp}, note_part)

        @block.vector
        def _(dve):
            dve.wait_ge(s_wload, 16 * 17)
            for f in range(FD):
                dve.tensor_tensor_reduce(hb[:, f, :], wl2[:, f, :], warow[:], 1.0, 0.0, ALU.mult, ALU.add,
                                         wacol[:, f:f + 1]).then_inc(s_wa, 1)
            dve.wait_ge(s_wa, FD)
            dve.wait_ge(s_const, 7)
            for f in range(FD):
                dve.tensor_scalar(hb[:, f, 0:P], ident[:], wacol[:, f:f + 1], None, ALU.mult).then_inc(s_wa, 1)
            dve.wait_ge(s_wturn, FD + HD + 2 * FD + 1)
            dve.tensor_copy(warow[:], bank[2][:, 0:D]).then_inc(s_wready, 1)

            def mask(b):
                dve.wait_ge(mask_in, b.nth(32, 32))
                if b.before(2).exists():
                    dve.wait_ge(exp_done, b.before(2).nth(32, 32))
                dve.tensor_copy(mrow[:], mrow8[:]).then_inc(mask_done, 1)
                dve.tensor_copy(mcol[:], mcol8[:]).then_inc(mask_done, 1)
                dve.wait_ge(mask_done, b.nth(4, 2))
                dve.tensor_scalar(mbias[:, b.slot], mrow[:], 1.0, MASKED, ALU.subtract, ALU.mult).then_inc(mask_done, 1)
                dve.tensor_scalar(escale[:, b.slot], mcol[:], DIM_HEAD ** -0.5, None, ALU.mult).then_inc(mask_done, 1)

            def hmat_(b):
                dve.wait_ge(adj_in, b.nth(32, 32))
                dve.tensor_scalar(hmat[:], adjf[:, b.slot], 0.0, None, ALU.not_equal).then_inc(hmat_done, 1)
                dve.tensor_copy(wcol2[:, :, 0], wcol[:]).then_inc(wcol_done, 1)
                dve.wait_ge(wcol_done, b.nth(2, 1))
                dve.tensor_tensor(wcol2[:, :, 1], wcol[:], wcol2[:, :, 0], ALU.subtract).then_inc(wcol_done, 1)

            def norm(name, chain, source, arrived):
                def stats_of(b, t):
                    arrived(b, t)
                    dve.bn_stats(stats[:, chain, t, :], source(b)[:, t, :]).then_inc(ln_stats[name], 1)

                def moments_of(b):
                    if arrived is x_here:
                        for t in range(NT):
                            stats_of(b, t)
                    for t in range(NT):
                        dve.wait_ge(ln_stats[name], b.nth(4, t + 1))
                        dve.sem_inc(dve_went, 1)
                        dve.bn_aggr(moments[:, chain, t, :], stats[:, chain, t, :]).then_inc(ln_moments[name], 1)
                return {"stats": stats_of, "moments": moments_of}

            def dn(b):
                dve.wait_ge(ready["dn"], b.nth(1, 1))
                dve.reduce_sum(dsum[:], bank_of(b, "dn")[:, 0:2 * NT].rearrange("p (t c) -> p t c", c=2), AX_X)\
                    .then_inc(by_dve["dn"], 1)
                dve.wait_ge(by_dve["dn"], b.nth(1, 1))
                dve.tensor_scalar(dpos[:], dsum[:], 0.0, None, ALU.is_gt).then_inc(dn_step, 1)
                dve.tensor_scalar(dinv[:], dsum[:], TINY, None, ALU.max).then_inc(dn_step, 1)
                dve.wait_ge(dn_step, b.nth(4, 2))
                dve.reciprocal(dinv[:], dinv[:]).then_inc(dn_step, 1)
                dve.wait_ge(dn_step, b.nth(4, 3))
                dve.tensor_tensor(dinv[:], dinv[:], dpos[:], ALU.mult).then_inc(dn_step, 1)

            def h0(b):
                dve.wait_ge(h0_done, b.nth(4, 4))
                dve.tensor_copy(hz[:, :, 0:D], hrow[:]).then_inc(h0_high, 1)

            def m_low(b, t):
                dve.wait_ge(by_act["m"], b.nth(4, t + 1))
                dve.scalar_tensor_tensor(mm[:, t, 1, :], bank_of(b, "m", t)[:, 0:D], binv[:, t:t + 1],
                                         mm[:, t, 0, :], ALU.mult, ALU.subtract).then_inc(by_dve["m"], 1)

            def m(b, t):
                dve.wait_ge(ready["m"], b.nth(4, t + 1))
                dve.tensor_scalar(binv[:, t:t + 1], bank_of(b, "m", t)[:, D:D + 1], 1.0, None, ALU.max)\
                    .then_inc(binv_done, 1)
                dve.wait_ge(binv_done, b.nth(8, 2 * t + 1))
                dve.reciprocal(binv[:, t:t + 1], binv[:, t:t + 1]).then_inc(binv_done, 1)

            def w1(b, t):
                dve.wait_ge(ready["w1"], b.nth(4, t + 1))
                dve.wait_ge(dn_step, b.nth(4, 4))
                dve.scalar_tensor_tensor(rbuf[:, t, :], bank_of(b, "w1", t), dinv[:, t:t + 1], b1row[:],
                                         ALU.mult, ALU.add).then_inc(by_dve["w1"], 1)

            def z(b, t):
                dve.wait_ge(by_act["z"], b.nth(4, t + 1))
                dve.tensor_tensor(hz[:, t, D + 2:], bank_of(b, "z", t)[:, 0:D], hz[:, t, 0:D], ALU.subtract)\
                    .then_inc(by_dve["z"], 1)

            def m2(b, t):
                dve.wait_ge(by_act["m2"], b.nth(4, t + 1))
                dve.scalar_tensor_tensor(mm[:, t, 1, :], bank_of(b, "m2", t)[:, 0:D], binv[:, t:t + 1],
                                         mm[:, t, 0, :], ALU.mult, ALU.subtract).then_inc(by_dve["m2"], 1)

            def x1(b, t):
                dve.wait_ge(ready["x1"], b.nth(4, t + 1))
                dve.wait_ge(xh_done, b.nth(2, 2))
                dve.scalar_tensor_tensor(xs[:, b.slot, t, :], bank_of(b, "x1", t)[:, 0:D], dinv[:, t:t + 1],
                                         xs[:, b.slot, t, :], ALU.mult, ALU.add).then_inc(by_dve["x1"], 1)

            def qk(b, p, c):
                dve.wait_ge(by_act["qk"], b.nth(8, 2 * p + c + 1))
                dve.tensor_tensor(nat[:, p % 2, 2 * c + 1, :], bank_of(b, "qk", p, c), nat[:, p % 2, 2 * c, :],
                                  ALU.subtract).then_inc(by_dve["qk"], 1)

            def v(b, t):
                dve.wait_ge(by_act["v"], b.nth(4, t + 1))
                dve.tensor_tensor(vs[:, t, :, 1, :], bank_of(b, "v", t).rearrange("p (h d) -> p h d", h=HEADS),
                                  vs[:, t, :, 0, :], ALU.subtract).then_inc(by_dve["v"], 1)

            def score(b, g):
                s = slice(g % NT, g % NT + 1)
                dve.wait_ge(ready["score"], b.nth(32, g + 1))
                if g >= NT:
                    dve.wait_ge(ready["turn"], b.nth(32, g - NT + 1))
                elif b.before().exists():
                    dve.wait_ge(ready["turn"], b.before().nth(32, 32 - NT + g + 1))
                dve.sem_inc(dve_went, 1)
                dve.tensor_tensor_reduce(sm[:, g % NT, :], psS[g % 2][:], mbias[:, b.slot], 1.0, -3.4e38,
                                         ALU.add, ALU.max, smax[:, s]).then_inc(by_dve["score"], 1)
                dve.wait_ge(by_dve["score"], b.nth(32, g + 1))
                dve.scalar_tensor_tensor(nbias[:, s], smax[:, s], -1.0, escale[:, b.slot, s], ALU.mult,
                                         ALU.mult).then_inc(nbias_done, 1)

            def norm_(b, g):
                s = slice(g % NT, g % NT + 1)
                dve.wait_ge(exp_done, b.nth(32, g + 1))
                dve.reciprocal(einv[:, s], esum[:, s]).then_inc(einv_done, 1)
                dve.wait_ge(einv_done, b.nth(32, g + 1))
                if g < NT:
                    dve.wait_ge(shared_done, b.nth(4, g + 1))
                dve.scalar_tensor_tensor(sm[:, g % NT, :], sm[:, g % NT, :], einv[:, s],
                                         adjf[:, b.slot, g % NT, :], ALU.mult, ALU.add).then_inc(attn_done, 1)

            def turn(b, g):
                h, t = g // NT, g % NT
                dve.wait_ge(by_act["turn"], b.nth(32, g + 1))
                cols = slice(t * P, (t + 1) * P)
                dve.tensor_tensor(pt[:, h % 2, 1, :, cols], psT[g % 2][:].rearrange("p (j n) -> p j n", j=NT),
                                  pt[:, h % 2, 0, :, cols], ALU.subtract).then_inc(by_dve["turn"], 1)

            def pv(b, h):
                dve.wait_ge(by_act["pv"], b.nth(8, h + 1))
                if h == 0 and b.before().exists():
                    dve.wait_ge(ready["wo"], b.before().nth(4, 4))
                rows = slice((h % 2) * DIM_HEAD, (h % 2 + 1) * DIM_HEAD)
                dve.tensor_tensor(ot[rows, h // 2, :], psO[0:DIM_HEAD, :], otmp[:], ALU.add).then_inc(by_dve["pv"], 1)

            def wo_(b, t):
                dve.wait_ge(ready["wo"], b.nth(4, t + 1))
                dve.wait_ge(xbias_done, b.nth(1, 1))
                dve.scalar_tensor_tensor(xb[:, t, :], bank_of(b, "wo", t)[:, 0:D], MIX, xs[:, b.slot, t, :],
                                         ALU.mult, ALU.add).then_inc(by_dve["wo"], 1)

            def deg_(b):
                dve.wait_ge(adjb_in, b.nth(16, 16))
                dve.reduce_sum(deg[:], adjb[:], AX_X).then_inc(deg_step, 1)
                dve.wait_ge(deg_step, b.nth(3, 1))
                dve.tensor_scalar(rdeg[:], deg[:], EPS_DEG, None, ALU.max).then_inc(deg_step, 1)
                dve.wait_ge(deg_step, b.nth(3, 2))
                dve.reciprocal(rdeg[:], rdeg[:]).then_inc(deg_step, 1)

            def h2(b):
                for t in range(NT):
                    dve.wait_ge(h2_done, b.nth(4, t + 1))
                    if t == 0 and b.before().exists():
                        dve.wait_ge(ready["o2"], b.before().nth(4, 4))
                    dve.tensor_tensor_reduce(th[:, 1 + t // 2, t % 2 * D:(t % 2 + 1) * D], hb[:, t, :], warow[:], 1.0, 0.0, ALU.mult, ALU.add,
                                             sj[:, t:t + 1]).then_inc(sj_done, 1)
                dve.wait_ge(sj_done, b.nth(5, 4))
                dve.tensor_scalar(sj8[:], sj[:], 1.0 / TANH_RANGE, None, ALU.mult).then_inc(sj_done, 1)
                for t in range(NT):
                    dve.tensor_scalar(th[:, 0, t * P:(t + 1) * P], ident[:], sj[:, t:t + 1], None, ALU.mult)\
                        .then_inc(diag_done, 1)

            def leaky(b, t):
                dve.wait_ge(by_act["sb"], b.nth(4, 4))
                dve.scalar_tensor_tensor(th[:, t, :], th[:, t, :], LEAK, th[:, t, :], ALU.mult, ALU.max)\
                    .then_inc(leaky_done, 1)

            def o2(b, t):
                s = slice(t, t + 1)
                dve.wait_ge(ready["o2"], b.nth(4, t + 1))
                dve.reciprocal(rden[:, s], bank_of(b, "o2", t)[:, D:D + 1]).then_inc(rden_done, 1)
                dve.wait_ge(rden_done, b.nth(8, 2 * t + 1))
                dve.tensor_tensor(rden[:, s], rden[:, s], deg[:, s], ALU.mult).then_inc(rden_done, 1)
                dve.wait_ge(rden_done, b.nth(8, 2 * t + 2))
                dve.scalar_tensor_tensor(xb[:, t, :], bank_of(b, "o2", t)[:, 0:D], rden[:, s], xb[:, t, :],
                                         ALU.mult, ALU.add).then_inc(by_dve["o2"], 1)

            def agg(b, t):
                dve.wait_ge(ready["agg"], b.nth(4, t + 1))
                dve.scalar_tensor_tensor(hb[:, t, :], bank_of(b, "agg", t)[:, 0:D], rdeg[:, t:t + 1],
                                         hb[:, t, :], ALU.mult, ALU.add).then_inc(by_dve["agg"], 1)
                dve.wait_ge(by_dve["agg"], b.nth(4, t + 1))
                dve.scalar_tensor_tensor(hb[:, t, :], hb[:, t, :], 0.0, xb[:, t, :], ALU.max, ALU.add)\
                    .then_inc(sum_done, 1)

            def x_here(b, t):
                dve.wait_ge(x_in, b.nth(16, 16))

            def relu_here(b, t):
                dve.wait_ge(relu_done, b.nth(4, t + 1))

            def x1_here(b, t):
                dve.wait_ge(by_dve["x1"], b.nth(4, t + 1))

            def x2_here(b, t):
                dve.wait_ge(by_dve["wo"], b.nth(4, t + 1))

            def x3_here(b, t):
                dve.wait_ge(by_dve["o2"], b.nth(4, t + 1))

            ln0 = norm("ln0", 0, lambda b: xs[:, b.slot], x_here)
            ln1 = norm("ln1", 0, lambda b: rbuf[:], relu_here)
            ln2 = norm("ln2", 0, lambda b: xs[:, b.slot], x1_here)
            lnb2 = norm("lnb2", 1, lambda b: xb[:], x2_here)
            lnb3 = norm("lnb3", 1, lambda b: xb[:], x3_here)

            walk("dve", dve.Fori, {
                ("F", "mask"): mask, ("F", "hmat"): hmat_, ("F", "dn"): dn, ("F", "h0_high"): h0, ("F", "m"): m,
                ("F", "m_low"): m_low, ("F", "ln0"): ln0["moments"], ("F", "ln1"): ln1["moments"],
                ("F", "ln1_stats"): ln1["stats"], ("F", "ln2"): ln2["moments"], ("F", "ln2_stats"): ln2["stats"],
                ("F", "w1"): w1, ("F", "z"): z, ("F", "m2"): m2, ("F", "x1"): x1, ("F", "qk"): qk,
                ("A", "v"): v, ("A", "score"): score, ("A", "norm"): norm_, ("A", "turn"): turn,
                ("A", "pv"): pv, ("B", "wo"): wo_, ("B", "deg"): deg_, ("B", "sj"): h2,
                ("B", "leaky"): leaky, ("B", "lnb2"): lnb2["moments"], ("B", "lnb2_stats"): lnb2["stats"],
                ("B", "lnb3"): lnb3["moments"], ("B", "lnb3_stats"): lnb3["stats"],
                ("B", "o2"): o2, ("B", "agg"): agg}, note_part)

        @block.tensor
        def _(pe):
            pe.wait_ge(s_wload, 16 * 17)
            pe.wait_ge(s_const, 7)
            sources = ([[rbuf[:, h, f * P:(f + 1) * P] for h in range(HD)] for f in range(FD)]
                       + [[th[:, o, h * P:(h + 1) * P] for o in range(FD)] for h in range(HD)]
                       + [[th[:, FD + o, (1 - half) * D + f * P:(1 - half) * D + (f + 1) * P] for o in range(FD)]
                          for f in range(FD) for half in range(2)])
            for n, blocks in enumerate(sources):
                if n >= 2:
                    pe.wait_ge(s_wcopy, n - 1)
                for i, src in enumerate(blocks):
                    last = pe.transpose(bank[n % 2][:, i * P:(i + 1) * P], src, ident[:])
                last.then_inc(s_wturn, 1)
            pe.wait_ge(s_wa, 2 * FD)
            for f in range(FD):
                last = pe.matmul(bank[2][:, f * P:(f + 1) * P], ones[:], hb[:, f, 0:P], start=True, stop=True)
            last.then_inc(s_wturn, 1)
            pe.wait_ge(s_wready, 1)
            pe.wait_ge(s_wcopy, len(sources))

            state = {}

            def start_part(batches):
                note_part(batches)
                state["batches"], state["uses"], state["claimed"] = batches, current["uses"], 0

            def claim(b, stage, name, *where):
                batches = state["batches"]
                n = state["uses"].index((stage, name) + where)
                assert n == state["claimed"]
                state["claimed"] += 1
                if n == 0:
                    if "A" in batches:
                        pe.wait_ge(by_dve["qk"], batches["A"].nth(8, 8))
                    if "B" in batches and "A" in batches:
                        pe.wait_ge(by_dve["v"], batches["B"].nth(4, 4))
                    if "B" in batches and batches["B"].before().exists():
                        pe.wait_ge(by_dve["agg"], batches["B"].before().nth(4, 4))
                    if "B" in batches and "A" not in batches:
                        pe.wait_ge(by_dve["v"], batches["B"].nth(4, 4))
                if n >= BANKS:
                    s, before, *at_ = state["uses"][n - BANKS]
                    sems, per = freed[before]
                    if before == "zp":
                        per, k = 8, 2 * at_[0] + 2
                    else:
                        k = use_number(before, at_)
                    pe.wait_ge(sems[before], state["batches"][s].nth(per, k))
                return bank[n % BANKS][:]

            def ht(b, t):
                pe.wait_ge(hmat_done, b.nth(1, 1))
                out_ = claim(b, "F", "ht", t).bitcast(F16)
                for i in range(NT):
                    last = pe.transpose(out_[:, i * P:(i + 1) * P], hmat[:, i, t * P:(t + 1) * P], ident16[:])
                last.then_inc(ready["ht"], 1)

            def dn(b):
                pe.wait_ge(by_act["ht"], b.nth(4, 4))
                pe.wait_ge(wcol_done, b.nth(2, 2))
                out_ = claim(b, "F", "dn")
                for i in range(NT):
                    for e in range(NT):
                        last = pe.matmul(out_[:, 2 * i:2 * i + 2], htm[:, e, i * P:(i + 1) * P], wcol2[:, e, :],
                                         start=(e == 0), stop=(e == NT - 1))
                last.then_inc(ready["dn"], 1)

            def m(b, t):
                pe.wait_ge(h0_low, b.nth(1, 1))
                out_ = claim(b, "F", "m", t)
                for i in range(NT):
                    lhs = hmat[:, i, t * P:(t + 1) * P]
                    pe.matmul(out_[:, 0:D + 2], lhs, hz[:, i, 0:D + 2], start=(i == 0), stop=False)
                    last = pe.matmul(out_[:, 0:D], lhs, hz[:, i, D + 2:], start=False, stop=(i == NT - 1))
                last.then_inc(ready["m"], 1)

            def u(b, f):
                pe.wait_ge(by_dve["m"], b.nth(4, 4))
                out_ = claim(b, "F", "u", f)
                for e in range(NT):
                    for part in range(2):
                        last = pe.matmul(out_, mm[:, e, part, f * P:(f + 1) * P], htm[:, e, :],
                                         start=(e == 0 and part == 0), stop=(e == NT - 1 and part == 1))
                last.then_inc(ready["u"], 1)

            def w1(b, t):
                pe.wait_ge(by_act["u"], b.nth(2, 2))
                out_ = claim(b, "F", "w1", t)
                for f in range(FD):
                    last = pe.matmul(out_, colf[:, f, t * P:(t + 1) * P], w1t[:, f, :],
                                     start=(f == 0), stop=(f == FD - 1))
                last.then_inc(ready["w1"], 1)

            def gt(b, h):
                pe.wait_ge(g1_done, b.nth(4, 4))
                out_ = claim(b, "F", "gt", h)
                for t in range(NT):
                    last = pe.transpose(out_[:, t * P:(t + 1) * P], rbuf[:, t, h * P:(h + 1) * P], ident[:])
                last.then_inc(ready["gt"], 1)

            def z(b, t):
                pe.wait_ge(by_act["gt"], b.nth(4, 4))
                out_ = claim(b, "F", "z", t)
                for h in range(HD):
                    last = pe.matmul(out_[:, 0:D], rbuf[:, t, h * P:(h + 1) * P], w2t[:, h, :],
                                     start=(h == 0), stop=(h == HD - 1))
                last.then_inc(ready["z"], 1)

            def m2(b, t):
                pe.wait_ge(by_dve["z"], b.nth(4, 4))
                out_ = claim(b, "F", "m2", t)
                for i in range(NT):
                    lhs = hmat[:, i, t * P:(t + 1) * P]
                    pe.matmul(out_[:, 0:D], lhs, hz[:, i, 0:D], start=(i == 0), stop=False)
                    last = pe.matmul(out_[:, 0:D], lhs, hz[:, i, D + 2:], start=False, stop=(i == NT - 1))
                last.then_inc(ready["m2"], 1)

            def x1(b, t):
                pe.wait_ge(by_dve["m2"], b.nth(4, 4))
                out_ = claim(b, "F", "x1", t)
                for e in range(NT):
                    for part in range(2):
                        last = pe.matmul(out_[:, 0:D], htm[:, e, t * P:(t + 1) * P], mm[:, e, part, :],
                                         start=(e == 0 and part == 0), stop=(e == NT - 1 and part == 1))
                last.then_inc(ready["x1"], 1)

            def turned_rows(name, stage, done, source):
                def rows(b, f):
                    pe.wait_ge(done, b.nth(4, 4))
                    out_ = claim(b, stage, name, f)
                    for t in range(NT):
                        last = pe.transpose(out_[:, t * P:(t + 1) * P], source[:, t, f * P:(f + 1) * P], ident[:])
                    last.then_inc(ready[name], 1)
                return rows

            def qk(b, p, c):
                pe.wait_ge(by_act["h1t"], b.nth(2, 2))
                out_ = claim(b, "F", "qk", p, c)
                for f in range(FD):
                    last = pe.matmul(out_, wqk[:, c, f, p * P:(p + 1) * P], colf[:, f, :],
                                     start=(f == 0), stop=(f == FD - 1))
                last.then_inc(ready["qk"], 1)

            def v(b, t):
                pe.wait_ge(by_act["h1t"], b.nth(2, 2))
                out_ = claim(b, "A", "v", t)
                for f in range(FD):
                    last = pe.matmul(out_, colf[:, f, t * P:(t + 1) * P], wv[:, f, :],
                                     start=(f == 0), stop=(f == FD - 1))
                last.then_inc(ready["v"], 1)

            def score(b, g):
                h, t = g // NT, g % NT
                pe.wait_ge(stack_in[h // 2], b.nth(128, 128))
                if g >= 2:
                    pe.wait_ge(by_dve["score"], b.nth(32, g - 1))
                elif b.before().exists():
                    pe.wait_ge(by_dve["score"], b.before().nth(32, 31 + g))
                for part in range(2):
                    last = pe.matmul(psS[g % 2][:], qs[:, h, t * P:(t + 1) * P], ks[:, h, part, :],
                                     start=(part == 0), stop=(part == 1))
                last.then_inc(ready["score"], 1)

            def turn(b, g):
                pe.wait_ge(attn_done, b.nth(32, g + 1))
                if g >= 2:
                    pe.wait_ge(by_dve["turn"], b.nth(32, g - 1))
                elif b.before().exists():
                    pe.wait_ge(by_dve["turn"], b.before().nth(32, 31 + g))
                for j in range(NT):
                    last = pe.transpose(psT[g % 2][:, j * P:(j + 1) * P], sm[:, g % NT, j * P:(j + 1) * P], ident[:])
                last.then_inc(ready["turn"], 1)

            def pv(b, h):
                pe.wait_ge(by_dve["turn"], b.nth(32, NT * (h + 1)))
                if h == 0:
                    pe.wait_ge(by_dve["v"], b.nth(4, 4))
                if h >= 1:
                    pe.wait_ge(by_dve["pv"], b.nth(8, h))
                elif b.before().exists():
                    pe.wait_ge(by_dve["pv"], b.before().nth(8, 8))
                for j in range(NT):
                    for part in range(2):
                        last = pe.matmul(psO[:], vs[:, j, h].rearrange("p c d -> p (c d)"), pt[:, h % 2, part, j, :],
                                         start=(j == 0 and part == 0), stop=(j == NT - 1 and part == 1))
                last.then_inc(ready["pv"], 1)

            def wo_(b, t):
                pe.wait_ge(by_dve["pv"], b.nth(8, 8))
                out_ = claim(b, "B", "wo", t)
                for p in range(PAIRS):
                    last = pe.matmul(out_[:, 0:D], ot[:, p, t * P:(t + 1) * P], wo[:, p, :],
                                     start=(p == 0), stop=(p == PAIRS - 1))
                last.then_inc(ready["wo"], 1)

            def at(b, t):
                pe.wait_ge(adjb_in, b.nth(16, 16))
                out_ = claim(b, "B", "at", t)
                for j in range(NT):
                    last = pe.transpose(out_[:, j * P:(j + 1) * P], adjb[:, t, j * P:(j + 1) * P], ident[:])
                last.then_inc(ready["at"], 1)

            def sb_(b):
                pe.wait_ge(diag_done, b.nth(4, 4))
                out_ = claim(b, "B", "sb")
                pe.matmul(out_, ones[:], th[:, 0, :], start=True, stop=True).then_inc(ready["sb"], 1)

            def y(b, t):
                pe.wait_ge(by_act["h2t"], b.nth(2, 2))
                out_ = claim(b, "B", "y", t)
                for f in range(FD):
                    last = pe.matmul(out_[:, 0:D], hbt[:, f, t * P:(t + 1) * P], wl2[:, f, :],
                                     start=(f == 0), stop=(f == FD - 1))
                last.then_inc(ready["y"], 1)

            def o2(b, t):
                pe.wait_ge(pair_done, b.nth(4, t + 1))
                pe.wait_ge(by_act["y"], b.nth(4, 4))
                out_ = claim(b, "B", "o2", t)
                for j in range(NT):
                    last = pe.matmul(out_[:, 0:D + 1], th[:, t, j * P:(j + 1) * P], yz[:, j, 0:D + 1],
                                     start=(j == 0), stop=(j == NT - 1))
                last.then_inc(ready["o2"], 1)

            def zp(b, t):
                pe.wait_ge(by_act["h3t"], b.nth(2, 2))
                out_ = claim(b, "B", "zp", t)
                for f in range(FD):
                    last = pe.matmul(out_, hbt[:, f, t * P:(t + 1) * P], w3t[:, f, :],
                                     start=(f == 0), stop=(f == FD - 1))
                last.then_inc(ready["zp"], 1)

            def agg(b, t):
                pe.wait_ge(by_act["zp"], b.nth(8, 8))
                out_ = claim(b, "B", "agg", t)
                for j in range(NT):
                    last = pe.matmul(out_[:, 0:D], adjb[:, t, j * P:(j + 1) * P], yz[:, j, 0:D],
                                     start=(j == 0), stop=(j == NT - 1))
                last.then_inc(ready["agg"], 1)

            walk("pe", pe.Fori, {
                ("F", "ht"): ht, ("F", "dn"): dn, ("F", "m"): m, ("F", "u"): u, ("F", "w1"): w1, ("F", "gt"): gt,
                ("F", "z"): z, ("F", "m2"): m2, ("F", "x1"): x1, ("F", "h1t"): turned_rows("h1t", "F", h1_done, hrow),
                ("F", "qk"): qk, ("A", "v"): v, ("A", "score"): score, ("A", "turn"): turn, ("A", "pv"): pv,
                ("B", "wo"): wo_, ("B", "at"): at, ("B", "sb"): sb_,
                ("B", "h2t"): turned_rows("h2t", "B", h2_done, hb), ("B", "y"): y, ("B", "o2"): o2,
                ("B", "h3t"): turned_rows("h3t", "B", h3_done, hb), ("B", "zp"): zp, ("B", "agg"): agg}, start_part)


_INS = ["x", "adj", "nodemask", "L0_gnn_W1", "L0_gnn_b1", "L0_gnn_gamma", "L0_gnn_beta", "L0_gnn_W2",
        "L0_gnn_b2", "L1_gnn_W_qkv", "L1_gnn_W_out", "L1_gnn_b_out", "L2_gnn_w", "L2_gnn_a", "L3_gnn_W"]
_OUTS = [((BATCHES, NODES, D), "float32")]


def kernel(**inputs):
    import numpy as _np
    import concourse.bacc as _bacc
    from concourse import mybir as _mybir
    from concourse.bass_utils import run_bass_kernel_spmd as _run

    nc = _bacc.Bacc("TRN2", target_bir_lowering=False, num_devices=1)
    arrays, args = {}, []
    for name in _INS:
        a = _np.ascontiguousarray(inputs[name])
        if a.dtype == _np.bool_:
            a = a.view(_np.uint8)
        arrays[f"in_{name}_dram"] = a
        args.append(nc.dram_tensor(f"in_{name}_dram", a.shape, _mybir.dt.from_np(a.dtype), kind="ExternalInput").ap())
    for i, (shape, dtype) in enumerate(_OUTS):
        dt = _mybir.dt.from_np(_np.dtype(dtype))
        args.append(nc.dram_tensor(f"out_{i}_dram", shape, dt, kind="ExternalOutput").ap())
    gnn_kernel(nc, *args)
    r = _run(nc, [arrays], core_ids=[0])
    got = tuple(r.results[0][f"out_{i}_dram"] for i in range(len(_OUTS)))
    return got[0]
```

```python
from contextlib import ExitStack

import concourse.bass as bass
from concourse import mybir

F32 = mybir.dt.float32
F16 = mybir.dt.float16
U8 = mybir.dt.uint8
I32 = mybir.dt.int32
ALU = mybir.AluOpType
ACT = mybir.ActivationFunctionType
AX_X = mybir.AxisListType.X
AXES = {1: mybir.AxisListType.X, 2: mybir.AxisListType.XY, 3: mybir.AxisListType.XYZ}

P = 128
BATCHES = 16
NODES = 512
NT = NODES // P
D = 256
FD = D // P
DH = 512
HD = DH // P
HEADS = 8
DIM_HEAD = 64
PAIRS = HEADS // 2
EPS_LN = 1e-5
EPS_DEG = 1e-6
MIX = 0.33
TANH_RANGE = 8.0
LEAK = 0.1
MASKED = 1e30
TINY = 1.2e-38
W_RANGE = 4096.0
COL_SCALE = 256.0
U_SCALE = 4.0
SMALLEST = 2.0 ** -60
EXPONENT_BITS = 0x7F800000
PASSES = ((0, 0), (0, 1), (1, 0))
BANKS = 3




def tiles(name, count, behind=None):
    tasks = []
    for t in range(count):
        tasks.append((name, t))
        if behind and t:
            tasks.append((behind, t - 1))
    return tasks + ([(behind, count - 1)] if behind else [])


QK = [task for p in range(PAIRS) for task in (("qk", p, 0), ("qk", p, 1), ("stack", p))]

STREAMS = {
    "L": ("F", [("load_adj",), ("load_x",)]),
    "G": ("F", [("mask",)] + tiles("gexp", NT)),
    "F": ("F", [("hmat",), ("ln0",)] + tiles("ht", NT) + [("h0",), ("dn",)]
          + tiles("m", NT, "m_low") + tiles("u", FD) + tiles("w1", NT, "ln1_stats") + [("ln1",), ("ln1_apply",)]
          + tiles("gt", HD) + tiles("z", NT) + tiles("m2", NT) + tiles("x1", NT, "ln2_stats")
          + [("ln2",), ("h1",)] + tiles("h1t", FD)
          + QK[0:3]),
    "Q": ("A", QK[3:]),
    "V": ("A", tiles("v", NT)),
    "S": ("A", tiles("score", HEADS * NT)),
    "I": ("A", tiles("inverse", HEADS * NT)),
    "M": ("A", tiles("bias", HEADS * NT)),
    "N": ("A", tiles("norm", HEADS * NT)),
    "T": ("A", tiles("turn", HEADS * NT)),
    "O": ("A", tiles("pv", HEADS)),
    "J": ("B", [("load_adj",)] + tiles("at", NT)),
    "B": ("B", tiles("wo", NT, "lnb2_stats") + [("deg",), ("lnb2",), ("h2",), ("sj",), ("sb",)]
          + tiles("leaky", NT) + tiles("h2t", FD) + tiles("y", NT) + tiles("pair_exp", NT)
          + tiles("o2", NT, "lnb3_stats") + [("lnb3",), ("h3",)] + tiles("h3t", FD) + tiles("zp", NT)
          + tiles("agg", NT, "result") + [("store",)]),
}

ORDER = {
    "FA": {
        "sp": ("LLQQQF"),
        "pool": ("FFGGGGFFF"),
        "act": ("SSVVSVTSQTVSQTFFFFQSTFTQQQSSSTSGTFOGTSSGFTSGTFTFSTSOFFTFSSFTTFSFOSTFTSTFFFFTOTSSSFSF"
                "TFFTSTFFFSFTSSTTOFTSFSFSTOSTTFFOTTO"),
        "dve": ("SMSSMISNIMMNVSFMVSVMITNQITVQFNITSNQSIFTGNMMQTSQMISFMINQITNSFMNOTSFIMTISFNMNISIFTFMTN"
                "FFSITMNTSNFFSOTMIFNFFMFSSFMIIFFTFFMNNTOTINISMSNTINMSTSMTMSOTIMINNFIIFNNSFMTFSTIMNFTF"
                "SFMIFNSFTFFFIMFFFFIFNTSSTNMOSTMSMFIMINFNITNIONFTFTOTTO"),
        "pe": ("SSSSVSTVSVTQVQTFFSFFQTSTFQQSQSFTOSFTSTFSTFSSTOSTTFFTSFFTFSTSFOSTSTOTSFFFTFSSTFFFSTFT"
               "STFFFSFSTTFFFFOSSTTSSTFFOTFTFOTTO"),
    },
    "FAB": {
        "sp": ("LJLQQQFB"),
        "pool": ("FBFGGGGBBBBFBFF"),
        "act": ("VVSSTVVTFFFSFQQJJJSQQFTQQTSJBFGGFSSFSFOTGTBBTTSGSFBFTTSSBBSFBBBOBTFBFSFTBSFTSFFFFSTT"
                "FSFOTSFSTFBTOTBSTFSFFTBFSOSTBTSSSTBBSFTSFTBSOTFTSTFSFTOTTO"),
        "dve": ("VSMSMVIBNIFTBBNGBVBVTBBSBMBQSQIMFNSIQNBQSMFSMSTQQTIFNFBFMMFFISFNFIFINTTNSOMSMBTISTIN"
                "BNFMMSFBSMITITIFNFNMFFBTFNFSFFMTFBIBOSIMBNBBBNSTIMNSBSBMITTINMBFNSSTMFINOFTMIFSNTTBS"
                "MOIFMNISFTFNBFISNMMFOTINSFTSMFFMFFFFIFSTMNTIIISNNMTNSFMSITNTMFIBSIMNONTBFTFTBINOBTTB"
                "BBBO"),
        "pe": ("VVSSBBTBVVTBSFFFQFSQJJSJQQSSTFQTSQJSFFFTSOFBTBSFTTSBFSSOTTBBFBFBFTTSFBBSTBBSOFFTFFST"
               "SFFSTTSFFTSOTBFTSSFBSFTSFOFBTSFTFFSTBBBSTSOFTSTFBTSBFTFTOTBTBO"),
    },
    "AB": {
        "sp": ("JQQQB"),
        "pool": ("BBBBBB"),
        "act": ("SSSSTTQTQSVVSQQVTVTSSBTJJSTOQTJSSBTBQSTTBJSBBSTSBSBBTBTSBBOTSTSOTSBSTTBBSTSTSOBTSTSO"
                "TBSTBBTSTOSTSSSTTOTTO"),
        "dve": ("SMSMINSBMISNMIBSNSMBTIBNBMTQBBBBSIQMVNSIVQMTBNQVTVTISSIMNNBTITMSNMOIQSTSMINMBNTSQITN"
                "TIMBSNMISNIMTSBNBITNMSBSTIOTBMBBBNMBBBIBSITMSNITNMSNIMOSTBBTNIMSTMISNINTMSOMNSITINTM"
                "NTOSITMNSSITNMTMSSIMMTININIONNTTBOTTBBBBBBBO"),
        "pe": ("SSBSSBTSTSBQBSSTTQVVQQVVTJSTSOJSTQTJSBSTBQSBTTJSSBBBTSTBSOTSBTBSBBTTOSSTSTBSBOTSBTSB"
               "TBTSOSTSBTTOSTBSTSBBTTOTTBO"),
    },
}

BANK_USES = {"ht", "dn", "m", "u", "w1", "gt", "z", "m2", "x1", "h1t", "qk", "v",
             "wo", "at", "sb", "h2t", "y", "o2", "h3t", "zp", "agg"}
FED_BY = {"dn": "ht", "u": "m", "w1": "u", "z": "gt", "m2": "z", "x1": "m2", "qk": "h1t",
          "y": "h2t", "o2": "y", "zp": "h3t", "agg": "zp"}
PRODUCTS = BANK_USES | {"score", "turn", "pv"}


class Batch:

    def __init__(self, turn, offset):
        self.turn, self.offset = turn, offset

    def exists(self):
        return not isinstance(self.turn, int) or 2 * self.turn + self.offset >= 0

    def before(self, n=1):
        return Batch(self.turn, self.offset - n)

    @property
    def index(self):
        return self.turn * 2 + self.offset

    @property
    def slot(self):
        return self.offset % 2

    def nth(self, per, k):
        return self.turn * (2 * per) + (self.offset * per + k)


def parts(fori):
    yield {"F": Batch(0, 0)}
    yield {"F": Batch(0, 1), "A": Batch(0, 0)}
    with fori(0, (BATCHES - 2) // 2) as turn:
        for k in (1, 2):
            yield {"F": Batch(turn, k + 1), "A": Batch(turn, k), "B": Batch(turn, k - 1)}
    yield {"A": Batch(0, BATCHES - 1), "B": Batch(0, BATCHES - 2)}
    yield {"B": Batch(0, BATCHES - 1)}


def tasks_of(engine, names, batches):
    left = {letter: [(stage,) + task for task in tasks if (stage, task[0]) in names]
            for letter, (stage, tasks) in STREAMS.items()}
    stages = "".join(batches)
    tasks = [left[letter].pop(0) for letter in ORDER[{"F": "FA", "B": "AB"}.get(stages, stages)][engine]]
    return [task for task in tasks if task[0] in batches]


def walk(engine, fori, handlers, start_part=None):
    for batches in parts(fori):
        if start_part:
            start_part(batches)
        for stage, name, *where in tasks_of(engine, handlers, batches):
            handlers[stage, name](batches[stage], *where)


def gnn_kernel(nc, x, adj, nodemask, W1, b1, gamma, beta, W2, b2, Wqkv, Wout, bout, w, a, W3, out):
    with ExitStack() as ctx:
        def sb(name, shape, dt=F32):
            return ctx.enter_context(nc.sbuf_tensor(name, shape, dt))

        def sem(name):
            return ctx.enter_context(nc.semaphore(name))

        ident = sb("ident", [P, P])
        ident16 = sb("ident16", [P, P], F16)
        ones = sb("ones", [P, P])
        half_power = sb("half_power", [P, NT])
        eps_tile = sb("eps_tile", [P, NT])
        minus_one = sb("minus_one", [P, NT])
        w1s = sb("w1s", [P, 2, FD, DH], F16)
        wqks = sb("wqks", [P, 2, 2, FD, DH], F16)
        wvs = sb("wvs", [P, 2, FD, DH], F16)
        w3s = sb("w3s", [P, 2, FD, 2 * D], F16)
        wmax = sb("wmax", [P, 3, 2])
        wpow = sb("wpow", [P, 3])
        wscale = sb("wscale", [P, 3])
        wback = sb("wback", [P, 3])
        w2t = sb("w2t", [P, HD, D])
        wo = sb("wo", [P, PAIRS, D])
        wl2 = sb("wl2", [P, FD, D])
        b1row = sb("b1row", [P, DH])
        b2row = sb("b2row", [P, D])
        boutrow = sb("boutrow", [P, D])
        warow = sb("warow", [P, D])
        gcol = sb("gcol", [P, HD])
        bcol = sb("bcol", [P, HD])
        wacol = sb("wacol", [P, FD])

        adjf = sb("adjf", [P, 2, NT, NODES])
        hmat = sb("hmat", [P, NT, NODES], F16)
        htm = sb("htm", [P, NT, NODES], F16)
        SPLIT = 2 * D + 2
        hz = sb("hz", [P, NT, SPLIT], F16)
        mm = sb("mm", [P, NT, 2, D], F16)
        cols = sb("cols", [P, 2, FD, NODES], F16)
        rbuf = sb("rbuf", [P, NT, DH])
        xs = sb("xs", [P, 2, NT, D])
        hrow = sb("hrow", [P, NT, D])
        nat = sb("nat", [P, 2, 4, NODES], F16)
        mrow8 = sb("mrow8", [P, NODES], U8)
        mcol8 = sb("mcol8", [P, NT], U8)
        mrow = sb("mrow", [P, NODES])
        mcol = sb("mcol", [P, NT])
        wcol = sb("wcol", [P, NT])
        wcol2 = sb("wcol2", [P, NT, 2], F16)
        dsum = sb("dsum", [P, NT])
        dpos = sb("dpos", [P, NT])
        dinv = sb("dinv", [P, NT])
        dinv1 = sb("dinv1", [P, NT])
        binv = sb("binv", [P, NT])
        qs = sb("qs", [P, HEADS, NODES], F16)
        ks = sb("ks", [P, HEADS, 2, NODES], F16)
        vs = sb("vs", [P, NT, HEADS, 2, DIM_HEAD], F16)
        mbias = sb("mbias", [P, 2, NODES])
        escale = sb("escale", [P, 2, NT])
        sm = sb("sm", [P, NT, NODES])
        smax = sb("smax", [P, NT])
        nbias = sb("nbias", [P, NT])
        esum = sb("esum", [P, NT])
        einv = sb("einv", [P, NT])
        pt = sb("pt", [P, 2, 2, NT, NODES], F16)
        otmp = sb("otmp", [DIM_HEAD, NODES])
        ot = sb("ot", [P, PAIRS, NODES])
        adjb = sb("adjb", [P, NT, NODES])
        th = sb("th", [P, NT, NODES])
        xb = sb("xb", [P, NT, D])
        hb = sb("hb", [P, NT, D])
        hbt = sb("hbt", [P, FD, NODES])
        yz = sb("yz", [P, NT, D + 1])
        deg = sb("deg", [P, NT])
        rdeg = sb("rdeg", [P, NT])
        sj = sb("sj", [P, NT])
        sj8 = sb("sj8", [P, NT])
        rden = sb("rden", [P, NT])
        stats = sb("stats", [P, 2, NT, 6])
        moments = sb("moments", [P, 2, NT, 2])
        vpe = sb("vpe", [P, 2, NT])
        rstd = sb("rstd", [P, 2, NT])
        nmr = sb("nmr", [P, 2, NT])

        bank = [ctx.enter_context(nc.psum_tensor(f"bank{i}", [P, 512], F32)) for i in range(BANKS)]
        psS = [ctx.enter_context(nc.psum_tensor(f"psS{i}", [P, 512], F32)) for i in range(2)]
        psT = [ctx.enter_context(nc.psum_tensor(f"psT{i}", [P, 512], F32)) for i in range(2)]
        psO = ctx.enter_context(nc.psum_tensor("psO", [P, 512], F32))

        s_const = sem("s_const")
        s_wload = sem("s_wload")
        s_ones = sem("s_ones")
        s_wready = sem("s_wready")
        s_wturn = sem("s_wturn")
        s_wcopy = sem("s_wcopy")
        s_wa = sem("s_wa")
        s_wmax = sem("s_wmax")
        s_wscale = sem("s_wscale")
        s_whigh = sem("s_whigh")
        s_wlow = sem("s_wlow")
        adj_in = sem("adj_in")
        x_in = sem("x_in")
        mask_in = sem("mask_in")
        adjb_in = sem("adjb_in")
        stack_in = [sem(f"stack_in{p}") for p in range(PAIRS)]
        out_stored = sem("out_stored")
        ready = {n: sem(f"{n}_ready") for n in sorted(PRODUCTS)}
        by_act = {n: sem(f"{n}_act") for n in ("ht", "m", "u", "gt", "z", "m2", "h1t", "qk", "v",
                                              "turn", "pv", "at", "sb", "h2t", "y", "h3t", "zp")}
        by_dve = {n: sem(f"{n}_dve") for n in ("dn", "m", "u", "h1t", "h3t", "w1", "z", "m2", "x1", "qk", "v", "score",
                                              "turn", "pv", "wo", "o2", "agg")}
        mask_done = sem("mask_done")
        hmat_done = sem("hmat_done")
        wcol_done = sem("wcol_done")
        binv_done = sem("binv_done")
        dn_step = sem("dn_step")
        relu_done = sem("relu_done")
        h0_done = sem("h0_done")
        h0_low = sem("h0_low")
        xh_done = sem("xh_done")
        g1_done = sem("g1_done")
        h1_done = sem("h1_done")
        xbias_done = sem("xbias_done")
        LNS = ("ln0", "ln1", "ln2", "lnb2", "lnb3")
        ln_stats = {n: sem(f"{n}_stats") for n in LNS}
        ln_moments = {n: sem(f"{n}_moments") for n in LNS}
        ln_scale = {n: sem(f"{n}_scale") for n in LNS}
        gexp_done = sem("gexp_done")
        gadd_done = sem("gadd_done")
        shared_done = sem("shared_done")
        nbias_done = sem("nbias_done")
        exp_done = sem("exp_done")
        einv_done = sem("einv_done")
        attn_done = sem("attn_done")
        deg_step = sem("deg_step")
        h2_done = sem("h2_done")
        sj_done = sem("sj_done")
        diag_done = sem("diag_done")
        leaky_done = sem("leaky_done")
        pexp_done = sem("pexp_done")
        pair_done = sem("pair_done")
        rden_done = sem("rden_done")
        h3_done = sem("h3_done")
        sum_done = sem("sum_done")

        freed = {"ht": (by_act, 4), "dn": (by_dve, 1), "m": (by_dve, 4), "u": (by_dve, 2),
                 "w1": (by_dve, 4), "gt": (by_act, 4), "z": (by_dve, 4), "m2": (by_dve, 4),
                 "x1": (by_dve, 4), "h1t": (by_dve, 2), "qk": (by_dve, 8), "v": (by_dve, 4),
                 "wo": (by_dve, 4), "at": (by_act, 4), "sb": (by_act, 4), "h2t": (by_act, 2),
                 "y": (by_act, 4), "o2": (by_dve, 4), "h3t": (by_dve, 2), "zp": (by_act, 4),
                 "agg": (by_dve, 4)}

        def use_number(name, where):
            if name == "qk":
                return 2 * where[0] + where[1] + 1
            if name == "sb":
                return 4
            return (where[0] if where else 0) + 1

        sp_went = sem("sp_went")
        dve_went = sem("dve_went")

        current = {}

        def note_part(batches):
            names = {(stage, task[0]) for stage, tasks in STREAMS.values() for task in tasks if task[0] in PRODUCTS}
            current["uses"] = [task for task in tasks_of("pe", names, batches) if task[1] in BANK_USES]

        def bank_of(b, name, *where):
            n = [task[1:] for task in current["uses"]].index((name,) + where)
            return bank[n % BANKS][:]

        w1full, w3full = sm[:, 0:FD, :], sm[:, FD:2 * FD, :]
        qkfull, vfull = adjb[:].rearrange("p (c t) n -> p c t n", c=2), xb[:].rearrange("p (t h) d -> p t (h d)", t=FD)
        colf = cols[:].rearrange("p c f n -> p (c f n)").bitcast(F32).rearrange("p (f n) -> p f n", f=FD)
        cols3 = hbt[:].rearrange("p f n -> p (f n)").bitcast(F16).rearrange("p (c f n) -> p c f n", c=2, f=FD)

        block = ctx.enter_context(nc.Block())

        @block.sync
        def _(sp):
            sp.dma_start(rbuf[:, 0:HD, 0:D], W1.rearrange("(t p) d -> p t d", p=P)).then_inc(s_wload, 16)
            sp.dma_start(th[:, 0:FD, :], W2.rearrange("(t p) h -> p t h", p=P)).then_inc(s_wload, 16)
            sp.dma_start(th[:, FD:2 * FD, :], W3.rearrange("(t p) f -> p t f", p=P)).then_inc(s_wload, 16)
            sp.dma_start(wl2[:], w.rearrange("(t p) d -> p t d", p=P)).then_inc(s_wload, 16)
            sp.dma_start(warow[:], a.partition_broadcast(P)).then_inc(s_wload, 16)
            sp.dma_start(gcol[:], gamma.rearrange("(t p) -> p t", p=P),
                         allow_slow_non_contiguous=True).then_inc(s_wload, 16)
            sp.dma_start(bcol[:], beta.rearrange("(t p) -> p t", p=P),
                         allow_slow_non_contiguous=True).then_inc(s_wload, 16)
            sp.dma_start(b1row[:], b1.partition_broadcast(P)).then_inc(s_wload, 16)
            sp.dma_start(b2row[:], b2.partition_broadcast(P)).then_inc(s_wload, 16)
            sp.dma_start(boutrow[:], bout.partition_broadcast(P)).then_inc(s_wload, 16)
            qkv = Wqkv.rearrange("(t p) (h c d) -> p c t h d", p=P, h=HEADS, c=3)
            for t in range(FD):
                for c in range(2):
                    sp.dma_start(qkfull[:, c, t, :].rearrange("p (h d) -> p h d", h=HEADS),
                                 qkv[:, c, t]).then_inc(s_wload, 16)
                sp.dma_start(vfull[:, t, :].rearrange("p (h d) -> p h d", h=HEADS),
                             qkv[:, 2, t]).then_inc(s_wload, 16)
            sp.dma_start(wo[:], Wout.rearrange("(t p) d -> p t d", p=P)).then_inc(s_wload, 16)

            def load_adj(b):
                if b.before(2).exists():
                    sp.wait_ge(attn_done, b.before(2).nth(32, 32))
                    sp.sem_inc(sp_went, 1)
                    sp.wait_ge(wcol_done, b.before(1).nth(2, 2))
                    sp.sem_inc(sp_went, 1)
                    sp.wait_ge(shared_done, b.before(1).nth(4, 4))
                    sp.sem_inc(sp_went, 1)
                elif b.before(1).exists():
                    sp.wait_ge(wcol_done, b.before(1).nth(2, 2))
                    sp.sem_inc(sp_went, 1)
                    sp.wait_ge(shared_done, b.before(1).nth(4, 4))
                    sp.sem_inc(sp_went, 1)
                sp.dma_start(adjf[:, b.slot], adj[b.index].rearrange("(t p) c -> p t c", p=P)).then_inc(adj_in, 16)
                sp.dma_start(wcol[:], adj[b.index, 0, :].rearrange("(t p) -> p t", p=P),
                             allow_slow_non_contiguous=True).then_inc(adj_in, 16)
                sp.dma_start(mcol8[:], nodemask[b.index].rearrange("(t p) -> p t", p=P),
                             allow_slow_non_contiguous=True).then_inc(mask_in, 16)
                sp.dma_start(mrow8[:], nodemask[b.index].partition_broadcast(P)).then_inc(mask_in, 16)

            def load_x(b):
                if b.before(2).exists():
                    sp.wait_ge(by_dve["wo"], b.before(2).nth(4, 4))
                    sp.sem_inc(sp_went, 1)
                sp.dma_start(xs[:, b.slot], x[b.index].rearrange("(t p) d -> p t d", p=P)).then_inc(x_in, 16)

            def stack(b, p):
                sp.wait_ge(by_act["qk"], b.nth(8, 2 * p + 2))
                sp.sem_inc(sp_went, 1)
                sp.wait_ge(by_dve["qk"], b.nth(8, 2 * p + 2))
                sp.sem_inc(sp_went, 1)
                if b.before().exists():
                    sp.wait_ge(ready["score"], b.before().nth(32, 8 * p + 8))
                    sp.sem_inc(sp_went, 1)
                for e in range(2):
                    rows = slice(e * DIM_HEAD, (e + 1) * DIM_HEAD)
                    h = 2 * p + e
                    for part in range(2):
                        to = slice(part * DIM_HEAD, (part + 1) * DIM_HEAD)
                        sp.dma_start(qs[to, h, :], nat[rows, p % 2, part, :]).then_inc(stack_in[p], 16)
                        sp.dma_start(ks[to, h, :, :], nat[rows, p % 2, 2:4, :]).then_inc(stack_in[p], 16)

            def load_adjb(b):
                if b.before().exists():
                    sp.wait_ge(ready["agg"], b.before().nth(4, 4))
                    sp.sem_inc(sp_went, 1)
                sp.dma_start(adjb[:], adj[b.index].rearrange("(t p) c -> p t c", p=P)).then_inc(adjb_in, 16)

            def store(b):
                sp.wait_ge(by_dve["agg"], b.nth(4, 4))
                sp.sem_inc(sp_went, 1)
                sp.wait_ge(sum_done, b.nth(4, 4))
                sp.sem_inc(sp_went, 1)
                sp.dma_start(out[b.index].rearrange("(t p) d -> p t d", p=P), hb[:]).then_inc(out_stored, 16)

            walk("sp", sp.Fori, {("F", "load_adj"): load_adj, ("F", "load_x"): load_x, ("F", "stack"): stack,
                           ("A", "stack"): stack,
                           ("B", "load_adj"): load_adjb, ("B", "store"): store})
            sp.wait_ge(out_stored, 16 * BATCHES)

        @block.gpsimd
        def _(pool):
            pool.memset(ones[:], 1.0).then_inc(s_ones, 1)
            pool.memset(half_power[:], -0.5).then_inc(s_const, 1)
            pool.memset(eps_tile[:], EPS_LN).then_inc(s_const, 1)
            pool.memset(minus_one[:], -1.0).then_inc(s_const, 1)
            pool.memset(hz[:, :, D:D + 2], 1.0).then_inc(s_const, 1)
            pool.memset(yz[:, :, D:D + 1], 1.0).then_inc(s_const, 1)
            pool.wait_ge(s_ones, 1)
            pool.affine_select(out=ident[:], in_=ones[:], compare_op=ALU.is_equal, fill=0.0, base=0,
                               pattern=[[-1, P]], channel_multiplier=1).then_inc(s_const, 1)
            pool.wait_ge(s_const, 6)
            pool.tensor_copy(ident16[:], ident[:]).then_inc(s_const, 1)

            def ln_scales(name, chain):
                def scales(b):
                    pool.wait_ge(ln_moments[name], b.nth(4, 4))
                    pool.tensor_tensor(vpe[:, chain], moments[:, chain, :, 1], eps_tile[:],
                                       ALU.add).then_inc(ln_scale[name], 1)
                    pool.wait_ge(ln_scale[name], b.nth(4, 1))
                    pool.tensor_tensor(rstd[:, chain], vpe[:, chain], half_power[:],
                                       ALU.pow).then_inc(ln_scale[name], 1)
                    pool.wait_ge(ln_scale[name], b.nth(4, 2))
                    pool.tensor_tensor(vpe[:, chain], moments[:, chain, :, 0], rstd[:, chain],
                                       ALU.mult).then_inc(ln_scale[name], 1)
                    pool.wait_ge(ln_scale[name], b.nth(4, 3))
                    pool.tensor_tensor(nmr[:, chain], vpe[:, chain], minus_one[:],
                                       ALU.mult).then_inc(ln_scale[name], 1)
                return scales

            def h0(b):
                pool.wait_ge(h0_done, b.nth(8, 8))
                pool.tensor_tensor(hz[:, :, D + 2:], hrow[:], hz[:, :, 0:D], ALU.subtract).then_inc(h0_low, 1)
                pool.tensor_tensor(xs[:, b.slot], xs[:, b.slot], hrow[:], ALU.add).then_inc(xh_done, 1)
                pool.wait_ge(xh_done, b.nth(2, 1))
                pool.tensor_tensor(xs[:, b.slot], xs[:, b.slot],
                                   b2row[:].unsqueeze(1).to_broadcast([P, NT, D]), ALU.add).then_inc(xh_done, 1)

            def gexp(b, t):
                tile = adjf[:, b.slot, t, :]
                pool.wait_ge(gexp_done, b.nth(4, t + 1))
                pool.wait_ge(hmat_done, b.nth(1, 1))
                pool.tensor_tensor(tile, tile, colf[:, t % 2, :], ALU.add).then_inc(gadd_done, 1)
                pool.wait_ge(gadd_done, b.nth(8, 2 * t + 1))
                pool.wait_ge(mask_done, b.nth(4, 4))
                pool.tensor_tensor(tile, tile, mrow[:], ALU.mult).then_inc(gadd_done, 1)
                pool.wait_ge(gadd_done, b.nth(8, 2 * t + 2))
                pool.tensor_tensor(tile, tile, mcol[:, t:t + 1].to_broadcast([P, NODES]),
                                   ALU.mult).then_inc(shared_done, 1)

            def h1(b):
                pool.wait_ge(h1_done, b.nth(4, 4))
                pool.tensor_tensor(xs[:, b.slot], xs[:, b.slot],
                                   boutrow[:].unsqueeze(1).to_broadcast([P, NT, D]), ALU.add).then_inc(xbias_done, 1)

            def pair_exp(b, t):
                pool.wait_ge(pexp_done, b.nth(4, t + 1))
                pool.wait_ge(by_act["at"], b.nth(4, t + 1))
                pool.tensor_tensor(th[:, t, :], th[:, t, :], adjb[:, t, :], ALU.mult).then_inc(pair_done, 1)

            walk("pool", pool.Fori, {("F", "ln0"): ln_scales("ln0", 0), ("F", "h0"): h0, ("F", "gexp"): gexp,
                             ("F", "ln1"): ln_scales("ln1", 0), ("F", "ln2"): ln_scales("ln2", 0),
                             ("F", "h1"): h1, ("B", "lnb2"): ln_scales("lnb2", 1),
                             ("B", "pair_exp"): pair_exp, ("B", "lnb3"): ln_scales("lnb3", 1)})

        @block.scalar
        def _(act):
            weight_tiles = ([w1full[:, f, :] for f in range(FD)]
                            + [w2t[:, h, :] for h in range(HD)]
                            + [w3full[:, f, half * D:(half + 1) * D] for f in range(FD) for half in range(2)])
            for n, tile in enumerate(weight_tiles):
                act.wait_ge(s_wturn, n + 1)
                width = tile.shape[-1]
                act.activation(tile, bank[n % 2][:, 0:width], ACT.Copy).then_inc(s_wcopy, 1)
            for high, full, group in ((w1s[:, 0], w1full, 0), (wqks[:, 0], qkfull, 1), (wvs[:, 0], vfull, 1),
                                      (w3s[:, 0], w3full, 2)):
                act.wait_ge(s_wscale, 8)
                act.activation(high, full, ACT.Copy, scale=wscale[:, group:group + 1]).then_inc(s_whigh, 1)

            def ht(b, t):
                act.wait_ge(ready["ht"], b.nth(4, t + 1))
                act.activation(htm[:, t, :], bank_of(b, "ht", t).bitcast(F16)[:, 0:NODES], ACT.Copy)\
                    .then_inc(by_act["ht"], 1)

            def h0(b):
                act.wait_ge(ln_scale["ln0"], b.nth(4, 4))
                act.wait_ge(x_in, b.nth(16, 16))
                for t in range(NT):
                    for target in (hrow[:, t, :], hz[:, t, 0:D]):
                        act.activation(target, xs[:, b.slot, t, :], ACT.Relu, bias=nmr[:, 0, t:t + 1],
                                       scale=rstd[:, 0, t:t + 1]).then_inc(h0_done, 1)

            def gexp(b, t):
                act.wait_ge(adj_in, b.nth(32, 32))
                if t == 0 and b.before().exists():
                    act.wait_ge(ready["v"], b.before().nth(4, 4))
                    act.wait_ge(by_dve["qk"], b.before().nth(8, 8))
                if t >= 2:
                    act.wait_ge(gadd_done, b.nth(8, 2 * (t - 2) + 1))
                act.activation(colf[:, t % 2, :], adjf[:, b.slot, t, :], ACT.Exp, scale=-1.0).then_inc(gexp_done, 1)

            def m(b, t):
                act.wait_ge(binv_done, b.nth(8, 2 * t + 2))
                act.activation(mm[:, t, 0, :], bank_of(b, "m", t)[:, 0:D], ACT.Copy,
                               scale=binv[:, t:t + 1]).then_inc(by_act["m"], 1)

            def u(b, f):
                act.wait_ge(ready["u"], b.nth(2, f + 1))
                act.wait_ge(gadd_done, b.nth(8, 7))
                act.activation(cols[:, 0, f, :], bank_of(b, "u", f), ACT.Copy, scale=U_SCALE).then_inc(by_act["u"], 1)

            def w1(b, t):
                act.wait_ge(by_dve["w1"], b.nth(4, t + 1))
                act.activation(rbuf[:, t, :], rbuf[:, t, :], ACT.Relu).then_inc(relu_done, 1)

            def ln1_apply(b):
                act.wait_ge(ln_scale["ln1"], b.nth(4, 4))
                for t in range(NT):
                    act.activation(rbuf[:, t, :], rbuf[:, t, :], ACT.Identity, bias=nmr[:, 0, t:t + 1],
                                   scale=rstd[:, 0, t:t + 1]).then_inc(g1_done, 1)

            def gt(b, h):
                act.wait_ge(ready["gt"], b.nth(4, h + 1))
                act.activation(rbuf[:, :, h * P:(h + 1) * P],
                               bank_of(b, "gt", h).rearrange("p (t n) -> p t n", t=NT), ACT.Identity,
                               bias=bcol[:, h:h + 1], scale=gcol[:, h:h + 1]).then_inc(by_act["gt"], 1)

            def z(b, t):
                act.wait_ge(ready["z"], b.nth(4, t + 1))
                act.activation(hz[:, t, 0:D], bank_of(b, "z", t)[:, 0:D], ACT.Copy).then_inc(by_act["z"], 1)

            def m2(b, t):
                act.wait_ge(ready["m2"], b.nth(4, t + 1))
                act.activation(mm[:, t, 0, :], bank_of(b, "m2", t)[:, 0:D], ACT.Copy,
                               scale=binv[:, t:t + 1]).then_inc(by_act["m2"], 1)

            def h1(b):
                act.wait_ge(ln_scale["ln2"], b.nth(4, 4))
                for t in range(NT):
                    act.activation(hrow[:, t, :], xs[:, b.slot, t, :], ACT.Relu, bias=nmr[:, 0, t:t + 1],
                                   scale=rstd[:, 0, t:t + 1]).then_inc(h1_done, 1)

            def h1t(b, f):
                act.wait_ge(ready["h1t"], b.nth(2, f + 1))
                act.activation(cols[:, 0, f, :], bank_of(b, "h1t", f), ACT.Copy, scale=COL_SCALE)\
                    .then_inc(by_act["h1t"], 1)

            def qk(b, p, c):
                act.wait_ge(ready["qk"], b.nth(8, 2 * p + c + 1))
                if p >= 2:
                    act.wait_ge(stack_in[p - 2], b.nth(128, 128))
                elif b.before().exists():
                    act.wait_ge(stack_in[p + 2], b.before().nth(128, 128))
                act.activation(nat[:, p % 2, 2 * c, :], bank_of(b, "qk", p, c), ACT.Copy,
                               scale=wback[:, 1:2]).then_inc(by_act["qk"], 1)

            def v(b, t):
                act.wait_ge(ready["v"], b.nth(4, t + 1))
                act.activation(vs[:, t, :, 0, :], bank_of(b, "v", t).rearrange("p (h d) -> p h d", h=HEADS),
                               ACT.Copy, scale=wback[:, 1:2]).then_inc(by_act["v"], 1)

            def score(b, g):
                act.wait_ge(nbias_done, b.nth(32, g + 1))
                if g >= NT:
                    act.wait_ge(attn_done, b.nth(32, g - NT + 1))
                elif b.before().exists():
                    act.wait_ge(attn_done, b.before().nth(32, 32 - NT + g + 1))
                act.activation(sm[:, g % NT, :], sm[:, g % NT, :], ACT.Exp, bias=nbias[:, g % NT:g % NT + 1],
                               scale=escale[:, b.slot, g % NT:g % NT + 1],
                               accum_out=esum[:, g % NT:g % NT + 1]).then_inc(exp_done, 1)

            def turn(b, g):
                act.wait_ge(ready["turn"], b.nth(32, g + 1))
                h, t = g // NT, g % NT
                if h >= 2:
                    act.wait_ge(ready["pv"], b.nth(8, h - 1))
                act.activation(pt[:, h % 2, 0, :, t * P:(t + 1) * P],
                               psT[g % 2][:].rearrange("p (j n) -> p j n", j=NT), ACT.Copy).then_inc(by_act["turn"], 1)

            def pv(b, h):
                act.wait_ge(ready["pv"], b.nth(8, h + 1))
                if h >= 1:
                    act.wait_ge(by_dve["pv"], b.nth(8, h))
                elif b.before().exists():
                    act.wait_ge(by_dve["pv"], b.before().nth(8, 8))
                act.activation(otmp[:], psO[DIM_HEAD:P, :], ACT.Copy).then_inc(by_act["pv"], 1)

            def at(b, t):
                act.wait_ge(ready["at"], b.nth(4, t + 1))
                act.wait_ge(deg_step, b.nth(3, 1))
                act.activation(adjb[:, t, :], bank_of(b, "at", t), ACT.Copy).then_inc(by_act["at"], 1)

            def h2(b):
                act.wait_ge(ln_scale["lnb2"], b.nth(4, 4))
                if b.before().exists():
                    act.wait_ge(out_stored, b.before().nth(16, 16))
                for t in range(NT):
                    act.activation(hb[:, t, :], xb[:, t, :], ACT.Relu, bias=nmr[:, 1, t:t + 1],
                                   scale=rstd[:, 1, t:t + 1]).then_inc(h2_done, 1)

            def sb_(b):
                act.wait_ge(ready["sb"], b.nth(1, 1))
                for j in range(NT):
                    act.activation(th[:, :, j * P:(j + 1) * P],
                                   bank_of(b, "sb").rearrange("p (t n) -> p t n", t=NT), ACT.Tanh,
                                   bias=sj8[:, j:j + 1], scale=1.0 / TANH_RANGE).then_inc(by_act["sb"], 1)

            def h2t(b, f):
                act.wait_ge(ready["h2t"], b.nth(2, f + 1))
                act.activation(hbt[:, f, :], bank_of(b, "h2t", f), ACT.Copy).then_inc(by_act["h2t"], 1)

            def y(b, t):
                act.wait_ge(ready["y"], b.nth(4, t + 1))
                if b.before().exists():
                    act.wait_ge(by_dve["agg"], b.before().nth(4, 4))
                act.activation(yz[:, t, 0:D], bank_of(b, "y", t)[:, 0:D], ACT.Copy).then_inc(by_act["y"], 1)

            def pair_exp(b, t):
                act.wait_ge(leaky_done, b.nth(4, t + 1))
                act.activation(th[:, t, :], th[:, t, :], ACT.Exp, scale=TANH_RANGE).then_inc(pexp_done, 1)

            def h3(b):
                act.wait_ge(ln_scale["lnb3"], b.nth(4, 4))
                act.wait_ge(sj_done, b.nth(5, 4))
                for t in range(NT):
                    act.activation(hb[:, t, :], xb[:, t, :], ACT.Relu, bias=nmr[:, 1, t:t + 1],
                                   scale=rstd[:, 1, t:t + 1]).then_inc(h3_done, 1)

            def h3t(b, f):
                act.wait_ge(ready["h3t"], b.nth(2, f + 1))
                act.activation(cols3[:, 0, f, :], bank_of(b, "h3t", f), ACT.Copy, scale=COL_SCALE)\
                    .then_inc(by_act["h3t"], 1)

            def zp(b, t):
                act.wait_ge(ready["zp"], b.nth(4, t + 1))
                act.activation(yz[:, t, 0:D], bank_of(b, "zp", t)[:, 0:D], ACT.Copy, scale=wback[:, 2:3])\
                    .then_inc(by_act["zp"], 1)
                act.activation(hb[:, t, :], bank_of(b, "zp", t)[:, D:], ACT.Copy, scale=wback[:, 2:3])\
                    .then_inc(by_act["zp"], 1)

            walk("act", act.Fori, {
                ("F", "ht"): ht, ("F", "h0"): h0, ("F", "gexp"): gexp, ("F", "m"): m, ("F", "u"): u,
                ("F", "w1"): w1, ("F", "ln1_apply"): ln1_apply, ("F", "gt"): gt, ("F", "z"): z, ("F", "m2"): m2,
                ("F", "h1"): h1, ("F", "h1t"): h1t, ("F", "qk"): qk, ("A", "qk"): qk, ("A", "v"): v,
                ("A", "score"): score,
                ("A", "turn"): turn, ("A", "pv"): pv, ("B", "at"): at, ("B", "h2"): h2, ("B", "sb"): sb_,
                ("B", "h2t"): h2t, ("B", "y"): y, ("B", "pair_exp"): pair_exp, ("B", "h3"): h3,
                ("B", "h3t"): h3t, ("B", "zp"): zp}, note_part)

        @block.vector
        def _(dve):
            dve.wait_ge(s_wload, 16 * 17)
            for f in range(FD):
                dve.tensor_tensor_reduce(hb[:, f, :], wl2[:, f, :], warow[:], 1.0, 0.0, ALU.mult, ALU.add,
                                         wacol[:, f:f + 1]).then_inc(s_wa, 1)
            dve.wait_ge(s_wa, FD)
            dve.wait_ge(s_const, 7)
            for f in range(FD):
                dve.tensor_scalar(hb[:, f, 0:P], ident[:], wacol[:, f:f + 1], None, ALU.mult).then_inc(s_wa, 1)
            dve.wait_ge(s_wturn, FD + HD + 2 * FD + 1)
            dve.tensor_copy(warow[:], bank[2][:, 0:D]).then_inc(s_wready, 1)
            dve.wait_ge(s_wcopy, FD + HD + 2 * FD)
            for target, full in ((wmax[:, 0, 0:1], w1full), (wmax[:, 1, 0:1], qkfull), (wmax[:, 1, 1:2], vfull),
                                 (wmax[:, 2, 0:1], w3full)):
                dve.tensor_reduce(target, full, AXES[len(full.shape) - 1], ALU.max,
                                  apply_absolute_value=True).then_inc(s_wmax, 1)
            dve.wait_ge(s_wmax, 4)
            dve.tensor_tensor(wmax[:, 1, 0:1], wmax[:, 1, 0:1], wmax[:, 1, 1:2], ALU.max).then_inc(s_wmax, 1)
            dve.wait_ge(s_wmax, 5)
            for group in range(3):
                dve.tensor_scalar(hb[:, group, 0:P], ident[:], wmax[:, group, 0:1], None, ALU.mult).then_inc(s_wmax, 1)
            dve.wait_ge(s_wturn, FD + HD + 2 * FD + 2)
            dve.tensor_reduce(wpow[:], bank[2][:, 0:3 * P].rearrange("p (g n) -> p g n", g=3), AX_X, ALU.max)\
                .then_inc(s_wscale, 1)
            dve.wait_ge(s_wscale, 1)
            dve.tensor_scalar(wpow[:], wpow[:], SMALLEST, None, ALU.max).then_inc(s_wscale, 1)
            dve.wait_ge(s_wscale, 2)
            dve.tensor_scalar(wpow[:].bitcast(I32), wpow[:].bitcast(I32), EXPONENT_BITS, None, ALU.bitwise_and)\
                .then_inc(s_wscale, 1)
            dve.wait_ge(s_wscale, 3)
            dve.reciprocal(wscale[:], wpow[:]).then_inc(s_wscale, 1)
            dve.wait_ge(s_wscale, 4)
            dve.tensor_scalar(wscale[:], wscale[:], W_RANGE, None, ALU.mult).then_inc(s_wscale, 1)
            for group, column_scale in enumerate((U_SCALE, COL_SCALE, COL_SCALE)):
                dve.tensor_scalar(wback[:, group:group + 1], wpow[:, group:group + 1],
                                  1 / (W_RANGE * column_scale), None, ALU.mult)\
                    .then_inc(s_wscale, 1)
            dve.wait_ge(s_wscale, 8)
            for n, (parts_, full, group) in enumerate(((w1s, w1full, 0), (wqks, qkfull, 1), (wvs, vfull, 1),
                                                       (w3s, w3full, 2))):
                dve.wait_ge(s_whigh, n + 1)
                dve.scalar_tensor_tensor(parts_[:, 1], full, wscale[:, group:group + 1], parts_[:, 0], ALU.mult,
                                         ALU.subtract).then_inc(s_wlow, 1)

            def mask(b):
                dve.wait_ge(mask_in, b.nth(32, 32))
                if b.before(2).exists():
                    dve.wait_ge(exp_done, b.before(2).nth(32, 32))
                dve.tensor_copy(mrow[:], mrow8[:]).then_inc(mask_done, 1)
                dve.tensor_copy(mcol[:], mcol8[:]).then_inc(mask_done, 1)
                dve.wait_ge(mask_done, b.nth(4, 2))
                dve.tensor_scalar(mbias[:, b.slot], mrow[:], 1.0, MASKED, ALU.subtract, ALU.mult).then_inc(mask_done, 1)
                dve.tensor_scalar(escale[:, b.slot], mcol[:], DIM_HEAD ** -0.5, None, ALU.mult).then_inc(mask_done, 1)

            def hmat_(b):
                dve.wait_ge(adj_in, b.nth(32, 32))
                dve.tensor_scalar(hmat[:], adjf[:, b.slot], 0.0, None, ALU.not_equal).then_inc(hmat_done, 1)
                dve.tensor_copy(wcol2[:, :, 0], wcol[:]).then_inc(wcol_done, 1)
                dve.wait_ge(wcol_done, b.nth(2, 1))
                dve.tensor_tensor(wcol2[:, :, 1], wcol[:], wcol2[:, :, 0], ALU.subtract).then_inc(wcol_done, 1)

            def norm(name, chain, source, arrived):
                def stats_of(b, t):
                    arrived(b, t)
                    dve.bn_stats(stats[:, chain, t, :], source(b)[:, t, :]).then_inc(ln_stats[name], 1)

                def moments_of(b):
                    if arrived is x_here:
                        for t in range(NT):
                            stats_of(b, t)
                    for t in range(NT):
                        dve.wait_ge(ln_stats[name], b.nth(4, t + 1))
                        dve.sem_inc(dve_went, 1)
                        dve.bn_aggr(moments[:, chain, t, :], stats[:, chain, t, :]).then_inc(ln_moments[name], 1)
                return {"stats": stats_of, "moments": moments_of}

            def dn(b):
                dve.wait_ge(ready["dn"], b.nth(1, 1))
                dve.reduce_sum(dsum[:], bank_of(b, "dn")[:, 0:2 * NT].rearrange("p (t c) -> p t c", c=2), AX_X)\
                    .then_inc(by_dve["dn"], 1)
                dve.wait_ge(by_dve["dn"], b.nth(1, 1))
                dve.tensor_scalar(dpos[:], dsum[:], 0.0, None, ALU.is_gt).then_inc(dn_step, 1)
                dve.tensor_scalar(dinv[:], dsum[:], TINY, None, ALU.max).then_inc(dn_step, 1)
                dve.wait_ge(dn_step, b.nth(5, 2))
                dve.reciprocal(dinv[:], dinv[:]).then_inc(dn_step, 1)
                dve.wait_ge(dn_step, b.nth(5, 3))
                dve.tensor_tensor(dinv[:], dinv[:], dpos[:], ALU.mult).then_inc(dn_step, 1)
                dve.wait_ge(dn_step, b.nth(5, 4))
                dve.tensor_scalar(dinv1[:], dinv[:], wback[:, 0:1], None, ALU.mult).then_inc(dn_step, 1)

            def m_low(b, t):
                dve.wait_ge(by_act["m"], b.nth(4, t + 1))
                dve.scalar_tensor_tensor(mm[:, t, 1, :], bank_of(b, "m", t)[:, 0:D], binv[:, t:t + 1],
                                         mm[:, t, 0, :], ALU.mult, ALU.subtract).then_inc(by_dve["m"], 1)

            def m(b, t):
                dve.wait_ge(ready["m"], b.nth(4, t + 1))
                dve.tensor_scalar(binv[:, t:t + 1], bank_of(b, "m", t)[:, D:D + 1], 1.0, None, ALU.max)\
                    .then_inc(binv_done, 1)
                dve.wait_ge(binv_done, b.nth(8, 2 * t + 1))
                dve.reciprocal(binv[:, t:t + 1], binv[:, t:t + 1]).then_inc(binv_done, 1)

            def w1(b, t):
                dve.wait_ge(ready["w1"], b.nth(4, t + 1))
                dve.wait_ge(dn_step, b.nth(5, 5))
                dve.scalar_tensor_tensor(rbuf[:, t, :], bank_of(b, "w1", t), dinv1[:, t:t + 1], b1row[:],
                                         ALU.mult, ALU.add).then_inc(by_dve["w1"], 1)

            def z(b, t):
                dve.wait_ge(by_act["z"], b.nth(4, t + 1))
                dve.tensor_tensor(hz[:, t, D + 2:], bank_of(b, "z", t)[:, 0:D], hz[:, t, 0:D], ALU.subtract)\
                    .then_inc(by_dve["z"], 1)

            def m2(b, t):
                dve.wait_ge(by_act["m2"], b.nth(4, t + 1))
                dve.scalar_tensor_tensor(mm[:, t, 1, :], bank_of(b, "m2", t)[:, 0:D], binv[:, t:t + 1],
                                         mm[:, t, 0, :], ALU.mult, ALU.subtract).then_inc(by_dve["m2"], 1)

            def x1(b, t):
                dve.wait_ge(ready["x1"], b.nth(4, t + 1))
                dve.wait_ge(xh_done, b.nth(2, 2))
                dve.scalar_tensor_tensor(xs[:, b.slot, t, :], bank_of(b, "x1", t)[:, 0:D], dinv[:, t:t + 1],
                                         xs[:, b.slot, t, :], ALU.mult, ALU.add).then_inc(by_dve["x1"], 1)

            def qk(b, p, c):
                dve.wait_ge(by_act["qk"], b.nth(8, 2 * p + c + 1))
                dve.scalar_tensor_tensor(nat[:, p % 2, 2 * c + 1, :], bank_of(b, "qk", p, c), wback[:, 1:2],
                                         nat[:, p % 2, 2 * c, :], ALU.mult, ALU.subtract).then_inc(by_dve["qk"], 1)

            def v(b, t):
                dve.wait_ge(by_act["v"], b.nth(4, t + 1))
                dve.scalar_tensor_tensor(vs[:, t, :, 1, :], bank_of(b, "v", t).rearrange("p (h d) -> p h d", h=HEADS),
                                         wback[:, 1:2], vs[:, t, :, 0, :], ALU.mult, ALU.subtract)\
                    .then_inc(by_dve["v"], 1)

            def low_columns(name, target, scale):
                def columns(b, f):
                    dve.wait_ge(by_act[name], b.nth(2, f + 1))
                    dve.scalar_tensor_tensor(target[:, 1, f, :], bank_of(b, name, f), scale, target[:, 0, f, :],
                                             ALU.mult, ALU.subtract).then_inc(by_dve[name], 1)
                return columns

            def score(b, g):
                s = slice(g % NT, g % NT + 1)
                dve.wait_ge(ready["score"], b.nth(32, g + 1))
                if g >= NT:
                    dve.wait_ge(ready["turn"], b.nth(32, g - NT + 1))
                elif b.before().exists():
                    dve.wait_ge(ready["turn"], b.before().nth(32, 32 - NT + g + 1))
                dve.sem_inc(dve_went, 1)
                dve.tensor_tensor_reduce(sm[:, g % NT, :], psS[g % 2][:], mbias[:, b.slot], 1.0, -3.4e38,
                                         ALU.add, ALU.max, smax[:, s]).then_inc(by_dve["score"], 1)

            def bias(b, g):
                s = slice(g % NT, g % NT + 1)
                dve.wait_ge(by_dve["score"], b.nth(32, g + 1))
                dve.scalar_tensor_tensor(nbias[:, s], smax[:, s], -1.0, escale[:, b.slot, s], ALU.mult,
                                         ALU.mult).then_inc(nbias_done, 1)

            def inverse(b, g):
                s = slice(g % NT, g % NT + 1)
                dve.wait_ge(exp_done, b.nth(32, g + 1))
                dve.reciprocal(einv[:, s], esum[:, s]).then_inc(einv_done, 1)

            def norm_(b, g):
                s = slice(g % NT, g % NT + 1)
                dve.wait_ge(einv_done, b.nth(32, g + 1))
                if g < NT:
                    dve.wait_ge(shared_done, b.nth(4, g + 1))
                dve.scalar_tensor_tensor(sm[:, g % NT, :], sm[:, g % NT, :], einv[:, s],
                                         adjf[:, b.slot, g % NT, :], ALU.mult, ALU.add).then_inc(attn_done, 1)

            def turn(b, g):
                h, t = g // NT, g % NT
                dve.wait_ge(by_act["turn"], b.nth(32, g + 1))
                cols = slice(t * P, (t + 1) * P)
                dve.tensor_tensor(pt[:, h % 2, 1, :, cols], psT[g % 2][:].rearrange("p (j n) -> p j n", j=NT),
                                  pt[:, h % 2, 0, :, cols], ALU.subtract).then_inc(by_dve["turn"], 1)

            def pv(b, h):
                dve.wait_ge(by_act["pv"], b.nth(8, h + 1))
                if h == 0 and b.before().exists():
                    dve.wait_ge(ready["wo"], b.before().nth(4, 4))
                rows = slice((h % 2) * DIM_HEAD, (h % 2 + 1) * DIM_HEAD)
                dve.tensor_tensor(ot[rows, h // 2, :], psO[0:DIM_HEAD, :], otmp[:], ALU.add).then_inc(by_dve["pv"], 1)

            def wo_(b, t):
                dve.wait_ge(ready["wo"], b.nth(4, t + 1))
                dve.wait_ge(xbias_done, b.nth(1, 1))
                dve.scalar_tensor_tensor(xb[:, t, :], bank_of(b, "wo", t)[:, 0:D], MIX, xs[:, b.slot, t, :],
                                         ALU.mult, ALU.add).then_inc(by_dve["wo"], 1)

            def deg_(b):
                dve.wait_ge(adjb_in, b.nth(16, 16))
                dve.reduce_sum(deg[:], adjb[:], AX_X).then_inc(deg_step, 1)
                dve.wait_ge(deg_step, b.nth(3, 1))
                dve.tensor_scalar(rdeg[:], deg[:], EPS_DEG, None, ALU.max).then_inc(deg_step, 1)
                dve.wait_ge(deg_step, b.nth(3, 2))
                dve.reciprocal(rdeg[:], rdeg[:]).then_inc(deg_step, 1)

            def h2(b):
                for t in range(NT):
                    dve.wait_ge(h2_done, b.nth(4, t + 1))
                    if t == 0 and b.before().exists():
                        dve.wait_ge(ready["o2"], b.before().nth(4, 4))
                    dve.tensor_tensor_reduce(th[:, 1 + t // 2, t % 2 * D:(t % 2 + 1) * D], hb[:, t, :], warow[:],
                                             1.0, 0.0, ALU.mult, ALU.add, sj[:, t:t + 1]).then_inc(sj_done, 1)
                dve.wait_ge(sj_done, b.nth(5, 4))
                dve.tensor_scalar(sj8[:], sj[:], 1.0 / TANH_RANGE, None, ALU.mult).then_inc(sj_done, 1)
                for t in range(NT):
                    dve.tensor_scalar(th[:, 0, t * P:(t + 1) * P], ident[:], sj[:, t:t + 1], None, ALU.mult)\
                        .then_inc(diag_done, 1)

            def leaky(b, t):
                dve.wait_ge(by_act["sb"], b.nth(4, 4))
                dve.scalar_tensor_tensor(th[:, t, :], th[:, t, :], LEAK, th[:, t, :], ALU.mult, ALU.max)\
                    .then_inc(leaky_done, 1)

            def o2(b, t):
                s = slice(t, t + 1)
                dve.wait_ge(ready["o2"], b.nth(4, t + 1))
                dve.reciprocal(rden[:, s], bank_of(b, "o2", t)[:, D:D + 1]).then_inc(rden_done, 1)
                dve.wait_ge(rden_done, b.nth(8, 2 * t + 1))
                dve.tensor_tensor(rden[:, s], rden[:, s], deg[:, s], ALU.mult).then_inc(rden_done, 1)
                dve.wait_ge(rden_done, b.nth(8, 2 * t + 2))
                dve.scalar_tensor_tensor(xb[:, t, :], bank_of(b, "o2", t)[:, 0:D], rden[:, s], xb[:, t, :],
                                         ALU.mult, ALU.add).then_inc(by_dve["o2"], 1)

            def agg(b, t):
                dve.wait_ge(ready["agg"], b.nth(4, t + 1))
                dve.scalar_tensor_tensor(hb[:, t, :], bank_of(b, "agg", t)[:, 0:D], rdeg[:, t:t + 1],
                                         hb[:, t, :], ALU.mult, ALU.add).then_inc(by_dve["agg"], 1)

            def result(b, t):
                dve.wait_ge(by_dve["agg"], b.nth(4, t + 1))
                dve.scalar_tensor_tensor(hb[:, t, :], hb[:, t, :], 0.0, xb[:, t, :], ALU.max, ALU.add)\
                    .then_inc(sum_done, 1)

            def x_here(b, t):
                dve.wait_ge(x_in, b.nth(16, 16))

            def relu_here(b, t):
                dve.wait_ge(relu_done, b.nth(4, t + 1))

            def x1_here(b, t):
                dve.wait_ge(by_dve["x1"], b.nth(4, t + 1))

            def x2_here(b, t):
                dve.wait_ge(by_dve["wo"], b.nth(4, t + 1))

            def x3_here(b, t):
                dve.wait_ge(by_dve["o2"], b.nth(4, t + 1))

            ln0 = norm("ln0", 0, lambda b: xs[:, b.slot], x_here)
            ln1 = norm("ln1", 0, lambda b: rbuf[:], relu_here)
            ln2 = norm("ln2", 0, lambda b: xs[:, b.slot], x1_here)
            lnb2 = norm("lnb2", 1, lambda b: xb[:], x2_here)
            lnb3 = norm("lnb3", 1, lambda b: xb[:], x3_here)

            walk("dve", dve.Fori, {
                ("F", "mask"): mask, ("F", "hmat"): hmat_, ("F", "dn"): dn, ("F", "m"): m,
                ("F", "m_low"): m_low, ("F", "ln0"): ln0["moments"], ("F", "ln1"): ln1["moments"],
                ("F", "ln1_stats"): ln1["stats"], ("F", "ln2"): ln2["moments"], ("F", "ln2_stats"): ln2["stats"],
                ("F", "u"): low_columns("u", cols, U_SCALE), ("F", "h1t"): low_columns("h1t", cols, COL_SCALE),
                ("B", "h3t"): low_columns("h3t", cols3, COL_SCALE),
                ("F", "w1"): w1, ("F", "z"): z, ("F", "m2"): m2, ("F", "x1"): x1, ("F", "qk"): qk, ("A", "qk"): qk,
                ("A", "v"): v, ("A", "score"): score, ("A", "bias"): bias,
                ("A", "inverse"): inverse, ("A", "norm"): norm_, ("A", "turn"): turn,
                ("A", "pv"): pv, ("B", "wo"): wo_, ("B", "deg"): deg_, ("B", "sj"): h2,
                ("B", "leaky"): leaky, ("B", "lnb2"): lnb2["moments"], ("B", "lnb2_stats"): lnb2["stats"],
                ("B", "lnb3"): lnb3["moments"], ("B", "lnb3_stats"): lnb3["stats"],
                ("B", "o2"): o2, ("B", "agg"): agg, ("B", "result"): result}, note_part)

        @block.tensor
        def _(pe):
            pe.wait_ge(s_wload, 16 * 17)
            pe.wait_ge(s_const, 7)
            sources = ([[rbuf[:, h, f * P:(f + 1) * P] for h in range(HD)] for f in range(FD)]
                       + [[th[:, o, h * P:(h + 1) * P] for o in range(FD)] for h in range(HD)]
                       + [[th[:, FD + o, (1 - half) * D + f * P:(1 - half) * D + (f + 1) * P] for o in range(FD)]
                          for f in range(FD) for half in range(2)])
            for n, blocks in enumerate(sources):
                if n >= 2:
                    pe.wait_ge(s_wcopy, n - 1)
                for i, src in enumerate(blocks):
                    last = pe.transpose(bank[n % 2][:, i * P:(i + 1) * P], src, ident[:])
                last.then_inc(s_wturn, 1)
            pe.wait_ge(s_wa, 2 * FD)
            for f in range(FD):
                last = pe.matmul(bank[2][:, f * P:(f + 1) * P], ones[:], hb[:, f, 0:P], start=True, stop=True)
            last.then_inc(s_wturn, 1)
            pe.wait_ge(s_wready, 1)
            pe.wait_ge(s_wmax, 8)
            for group in range(3):
                last = pe.matmul(bank[2][:, group * P:(group + 1) * P], ones[:], hb[:, group, 0:P], start=True, stop=True)
            last.then_inc(s_wturn, 1)
            pe.wait_ge(s_wlow, 4)

            state = {}

            def start_part(batches):
                note_part(batches)
                state["batches"], state["uses"], state["claimed"] = batches, current["uses"], 0

            def claim(b, stage, name, *where):
                batches = state["batches"]
                n = state["uses"].index((stage, name) + where)
                assert n == state["claimed"]
                state["claimed"] += 1
                if n == 0:
                    if "A" in batches:
                        pe.wait_ge(by_dve["qk"], batches["A"].nth(8, 2))
                    if "B" in batches and "A" in batches:
                        pe.wait_ge(by_dve["v"], batches["B"].nth(4, 4))
                    if "B" in batches and batches["B"].before().exists():
                        pe.wait_ge(by_dve["agg"], batches["B"].before().nth(4, 4))
                    if "B" in batches and "A" not in batches:
                        pe.wait_ge(by_dve["v"], batches["B"].nth(4, 4))
                        pe.wait_ge(by_dve["qk"], batches["B"].nth(8, 8))
                if n >= BANKS:
                    s, before, *at_ = state["uses"][n - BANKS]
                    if (s, before) == (stage, FED_BY.get(name)):
                        return bank[n % BANKS][:]
                    sems, per = freed[before]
                    if before == "zp":
                        per, k = 8, 2 * at_[0] + 2
                    else:
                        k = use_number(before, at_)
                    pe.wait_ge(sems[before], state["batches"][s].nth(per, k))
                return bank[n % BANKS][:]

            def split_product(out_, stationary, moving):
                steps = [(i, j, f) for i, j in PASSES for f in range(FD)]
                for n, (i, j, f) in enumerate(steps):
                    last = pe.matmul(out_, stationary(i, f), moving(j, f), start=(n == 0), stop=(n == len(steps) - 1))
                return last

            def ht(b, t):
                pe.wait_ge(hmat_done, b.nth(1, 1))
                out_ = claim(b, "F", "ht", t).bitcast(F16)
                for i in range(NT):
                    last = pe.transpose(out_[:, i * P:(i + 1) * P], hmat[:, i, t * P:(t + 1) * P], ident16[:])
                last.then_inc(ready["ht"], 1)

            def dn(b):
                pe.wait_ge(by_act["ht"], b.nth(4, 4))
                pe.wait_ge(wcol_done, b.nth(2, 2))
                out_ = claim(b, "F", "dn")
                for i in range(NT):
                    for e in range(NT):
                        last = pe.matmul(out_[:, 2 * i:2 * i + 2], htm[:, e, i * P:(i + 1) * P], wcol2[:, e, :],
                                         start=(e == 0), stop=(e == NT - 1))
                last.then_inc(ready["dn"], 1)

            def m(b, t):
                pe.wait_ge(h0_low, b.nth(1, 1))
                out_ = claim(b, "F", "m", t)
                for i in range(NT):
                    lhs = hmat[:, i, t * P:(t + 1) * P]
                    pe.matmul(out_[:, 0:D + 2], lhs, hz[:, i, 0:D + 2], start=(i == 0), stop=False)
                    last = pe.matmul(out_[:, 0:D], lhs, hz[:, i, D + 2:], start=False, stop=(i == NT - 1))
                last.then_inc(ready["m"], 1)

            def u(b, f):
                pe.wait_ge(by_dve["m"], b.nth(4, 4))
                out_ = claim(b, "F", "u", f)
                for e in range(NT):
                    for part in range(2):
                        last = pe.matmul(out_, mm[:, e, part, f * P:(f + 1) * P], htm[:, e, :],
                                         start=(e == 0 and part == 0), stop=(e == NT - 1 and part == 1))
                last.then_inc(ready["u"], 1)

            def w1(b, t):
                pe.wait_ge(by_dve["u"], b.nth(2, 2))
                out_ = claim(b, "F", "w1", t)
                split_product(out_, lambda part, f: cols[:, part, f, t * P:(t + 1) * P],
                              lambda part, f: w1s[:, part, f, :])\
                    .then_inc(ready["w1"], 1)

            def gt(b, h):
                pe.wait_ge(g1_done, b.nth(4, 4))
                out_ = claim(b, "F", "gt", h)
                for t in range(NT):
                    last = pe.transpose(out_[:, t * P:(t + 1) * P], rbuf[:, t, h * P:(h + 1) * P], ident[:])
                last.then_inc(ready["gt"], 1)

            def z(b, t):
                pe.wait_ge(by_act["gt"], b.nth(4, 4))
                out_ = claim(b, "F", "z", t)
                for h in range(HD):
                    last = pe.matmul(out_[:, 0:D], rbuf[:, t, h * P:(h + 1) * P], w2t[:, h, :],
                                     start=(h == 0), stop=(h == HD - 1))
                last.then_inc(ready["z"], 1)

            def m2(b, t):
                pe.wait_ge(by_dve["z"], b.nth(4, 4))
                out_ = claim(b, "F", "m2", t)
                for i in range(NT):
                    lhs = hmat[:, i, t * P:(t + 1) * P]
                    pe.matmul(out_[:, 0:D], lhs, hz[:, i, 0:D], start=(i == 0), stop=False)
                    last = pe.matmul(out_[:, 0:D], lhs, hz[:, i, D + 2:], start=False, stop=(i == NT - 1))
                last.then_inc(ready["m2"], 1)

            def x1(b, t):
                pe.wait_ge(by_dve["m2"], b.nth(4, 4))
                out_ = claim(b, "F", "x1", t)
                for e in range(NT):
                    for part in range(2):
                        last = pe.matmul(out_[:, 0:D], htm[:, e, t * P:(t + 1) * P], mm[:, e, part, :],
                                         start=(e == 0 and part == 0), stop=(e == NT - 1 and part == 1))
                last.then_inc(ready["x1"], 1)

            def turned_rows(name, stage, done, source):
                def rows(b, f):
                    pe.wait_ge(done, b.nth(4, 4))
                    out_ = claim(b, stage, name, f)
                    for t in range(NT):
                        last = pe.transpose(out_[:, t * P:(t + 1) * P], source[:, t, f * P:(f + 1) * P], ident[:])
                    last.then_inc(ready[name], 1)
                return rows

            def qk(b, p, c):
                pe.wait_ge(by_dve["h1t"], b.nth(2, 2))
                out_ = claim(b, "F" if p == 0 else "A", "qk", p, c)
                split_product(out_, lambda part, f: wqks[:, part, c, f, p * P:(p + 1) * P],
                              lambda part, f: cols[:, part, f, :])\
                    .then_inc(ready["qk"], 1)

            def v(b, t):
                pe.wait_ge(by_dve["h1t"], b.nth(2, 2))
                out_ = claim(b, "A", "v", t)
                split_product(out_, lambda part, f: cols[:, part, f, t * P:(t + 1) * P],
                              lambda part, f: wvs[:, part, f, :])\
                    .then_inc(ready["v"], 1)

            def score(b, g):
                h, t = g // NT, g % NT
                pe.wait_ge(stack_in[h // 2], b.nth(128, 128))
                if g >= 2:
                    pe.wait_ge(by_dve["score"], b.nth(32, g - 1))
                elif b.before().exists():
                    pe.wait_ge(by_dve["score"], b.before().nth(32, 31 + g))
                for part in range(2):
                    last = pe.matmul(psS[g % 2][:], qs[:, h, t * P:(t + 1) * P], ks[:, h, part, :],
                                     start=(part == 0), stop=(part == 1))
                last.then_inc(ready["score"], 1)

            def turn(b, g):
                pe.wait_ge(attn_done, b.nth(32, g + 1))
                if g >= 2:
                    pe.wait_ge(by_dve["turn"], b.nth(32, g - 1))
                elif b.before().exists():
                    pe.wait_ge(by_dve["turn"], b.before().nth(32, 31 + g))
                for j in range(NT):
                    last = pe.transpose(psT[g % 2][:, j * P:(j + 1) * P], sm[:, g % NT, j * P:(j + 1) * P], ident[:])
                last.then_inc(ready["turn"], 1)

            def pv(b, h):
                pe.wait_ge(by_dve["turn"], b.nth(32, NT * (h + 1)))
                if h == 0:
                    pe.wait_ge(by_dve["v"], b.nth(4, 4))
                if h >= 1:
                    pe.wait_ge(by_dve["pv"], b.nth(8, h))
                elif b.before().exists():
                    pe.wait_ge(by_dve["pv"], b.before().nth(8, 8))
                for j in range(NT):
                    for part in range(2):
                        last = pe.matmul(psO[:], vs[:, j, h].rearrange("p c d -> p (c d)"), pt[:, h % 2, part, j, :],
                                         start=(j == 0 and part == 0), stop=(j == NT - 1 and part == 1))
                last.then_inc(ready["pv"], 1)

            def wo_(b, t):
                pe.wait_ge(by_dve["pv"], b.nth(8, 8))
                out_ = claim(b, "B", "wo", t)
                for p in range(PAIRS):
                    last = pe.matmul(out_[:, 0:D], ot[:, p, t * P:(t + 1) * P], wo[:, p, :],
                                     start=(p == 0), stop=(p == PAIRS - 1))
                last.then_inc(ready["wo"], 1)

            def at(b, t):
                pe.wait_ge(adjb_in, b.nth(16, 16))
                out_ = claim(b, "B", "at", t)
                for j in range(NT):
                    last = pe.transpose(out_[:, j * P:(j + 1) * P], adjb[:, t, j * P:(j + 1) * P], ident[:])
                last.then_inc(ready["at"], 1)

            def sb_(b):
                pe.wait_ge(diag_done, b.nth(4, 4))
                out_ = claim(b, "B", "sb")
                pe.matmul(out_, ones[:], th[:, 0, :], start=True, stop=True).then_inc(ready["sb"], 1)

            def y(b, t):
                pe.wait_ge(by_act["h2t"], b.nth(2, 2))
                out_ = claim(b, "B", "y", t)
                for f in range(FD):
                    last = pe.matmul(out_[:, 0:D], hbt[:, f, t * P:(t + 1) * P], wl2[:, f, :],
                                     start=(f == 0), stop=(f == FD - 1))
                last.then_inc(ready["y"], 1)

            def o2(b, t):
                pe.wait_ge(pair_done, b.nth(4, t + 1))
                pe.wait_ge(by_act["y"], b.nth(4, 4))
                out_ = claim(b, "B", "o2", t)
                for j in range(NT):
                    last = pe.matmul(out_[:, 0:D + 1], th[:, t, j * P:(j + 1) * P], yz[:, j, 0:D + 1],
                                     start=(j == 0), stop=(j == NT - 1))
                last.then_inc(ready["o2"], 1)

            def zp(b, t):
                pe.wait_ge(by_dve["h3t"], b.nth(2, 2))
                out_ = claim(b, "B", "zp", t)
                split_product(out_, lambda part, f: cols3[:, part, f, t * P:(t + 1) * P],
                              lambda part, f: w3s[:, part, f, :])\
                    .then_inc(ready["zp"], 1)

            def agg(b, t):
                pe.wait_ge(by_act["zp"], b.nth(8, 8))
                out_ = claim(b, "B", "agg", t)
                for j in range(NT):
                    last = pe.matmul(out_[:, 0:D], adjb[:, t, j * P:(j + 1) * P], yz[:, j, 0:D],
                                     start=(j == 0), stop=(j == NT - 1))
                last.then_inc(ready["agg"], 1)

            walk("pe", pe.Fori, {
                ("F", "ht"): ht, ("F", "dn"): dn, ("F", "m"): m, ("F", "u"): u, ("F", "w1"): w1, ("F", "gt"): gt,
                ("F", "z"): z, ("F", "m2"): m2, ("F", "x1"): x1, ("F", "h1t"): turned_rows("h1t", "F", h1_done, hrow),
                ("F", "qk"): qk, ("A", "qk"): qk, ("A", "v"): v, ("A", "score"): score, ("A", "turn"): turn,
                ("A", "pv"): pv,
                ("B", "wo"): wo_, ("B", "at"): at, ("B", "sb"): sb_,
                ("B", "h2t"): turned_rows("h2t", "B", h2_done, hb), ("B", "y"): y, ("B", "o2"): o2,
                ("B", "h3t"): turned_rows("h3t", "B", h3_done, hb), ("B", "zp"): zp, ("B", "agg"): agg}, start_part)


_INS = ["x", "adj", "nodemask", "L0_gnn_W1", "L0_gnn_b1", "L0_gnn_gamma", "L0_gnn_beta", "L0_gnn_W2",
        "L0_gnn_b2", "L1_gnn_W_qkv", "L1_gnn_W_out", "L1_gnn_b_out", "L2_gnn_w", "L2_gnn_a", "L3_gnn_W"]
_OUTS = [((BATCHES, NODES, D), "float32")]


def kernel(**inputs):
    import numpy as _np
    import concourse.bacc as _bacc
    from concourse import mybir as _mybir
    from concourse.bass_utils import run_bass_kernel_spmd as _run

    nc = _bacc.Bacc("TRN2", target_bir_lowering=False, num_devices=1)
    arrays, args = {}, []
    for name in _INS:
        a = _np.ascontiguousarray(inputs[name])
        if a.dtype == _np.bool_:
            a = a.view(_np.uint8)
        arrays[f"in_{name}_dram"] = a
        args.append(nc.dram_tensor(f"in_{name}_dram", a.shape, _mybir.dt.from_np(a.dtype), kind="ExternalInput").ap())
    for i, (shape, dtype) in enumerate(_OUTS):
        dt = _mybir.dt.from_np(_np.dtype(dtype))
        args.append(nc.dram_tensor(f"out_{i}_dram", shape, dt, kind="ExternalOutput").ap())
    gnn_kernel(nc, *args)
    r = _run(nc, [arrays], core_ids=[0])
    got = tuple(r.results[0][f"out_{i}_dram"] for i in range(len(_OUTS)))
    return got[0]
```
